# Optimizing a Trainium2 kernel written in Bass

```python
import numpy as np
import jax
import jax.numpy as jnp

def _softmax(x, axis=-1):
    return jax.nn.softmax(x, axis=axis)

def _gelu(x):
    return jax.nn.gelu(x, approximate=True)

def _silu(x):
    return jax.nn.silu(x)

def _sigmoid(x):
    return jax.nn.sigmoid(x)

def _layernorm(x, axis=-1, eps=1e-05):
    m = jnp.mean(x, axis=axis, keepdims=True)
    v = jnp.var(x, axis=axis, keepdims=True)
    return (x - m) / jnp.sqrt(v + eps)

def _scatter_add(tgt, idx, src, axis=0):
    return tgt.at[idx].add(src)

def _segment_sum(src, seg, n):
    return jax.ops.segment_sum(src, seg, n)
kernel_name = 'mk_early_fusion_embed_d1_tok_img256_r4_152861'

def setup_inputs(seed: int=0):
    np.random.seed(seed)
    _w = jnp.asarray

    def _rec_inputs():
        import jax
        import jax.numpy as jnp
        _rk = jax.random.key(seed)
        x = -0.000125008 + 0.999885 * jax.random.normal(jax.random.fold_in(_rk, 1), (64, 64, 64, 64), jnp.float32)
        x_txt = jax.random.randint(jax.random.fold_in(_rk, 51), (64, 128), 0, 64, jnp.int32)
        fside_BS_continuous_positions = jax.random.uniform(jax.random.fold_in(_rk, 71), (64, 128), jnp.float32, 0.0, 0.999927)
        return (x, x_txt, fside_BS_continuous_positions)
    x, x_txt, fside_BS_continuous_positions = _rec_inputs()

    def _L0_tok_setup():
        import jax, jax.numpy as jnp
        import numpy as np
        B, C, H, W = (32, 64, 64, 64)
        STRIDE, HEADS = (4, 8)

        def _ln(x, w, b):
            mu = x.mean(-1, keepdims=True)
            var = ((x - mu) ** 2).mean(-1, keepdims=True)
            return (x - mu) * jax.lax.rsqrt(var + 1e-05) * w + b
        key = jax.random.key(seed)
        ks = jax.random.split(key, 4)
        return {'features': jax.random.normal(ks[0], (B, C, H, W), dtype=jnp.float32), 'ln_q_w': jnp.ones((C,), jnp.float32), 'ln_q_b': jnp.zeros((C,), jnp.float32), 'Wq': jax.random.normal(ks[1], (C, C), dtype=jnp.float32) * 0.02, 'ln_kv_w': jnp.ones((C,), jnp.float32), 'ln_kv_b': jnp.zeros((C,), jnp.float32), 'Wkv': jax.random.normal(ks[2], (2 * C, C), dtype=jnp.float32) * 0.02, 'proj_w': jax.random.normal(ks[3], (C, C), dtype=jnp.float32) * 0.02, 'proj_b': jnp.zeros((C,), jnp.float32), 'conv_stride': STRIDE, 'num_heads': HEADS}
    _L0_tok_all = _L0_tok_setup()
    _L0_tok_in = {k: v for k, v in _L0_tok_all.items() if k in ('ln_q_w', 'ln_q_b', 'Wq', 'ln_kv_w', 'ln_kv_b', 'Wkv', 'proj_w', 'proj_b')}
    del _L0_tok_all

    def _L0_txt_setup():
        import jax, jax.numpy as jnp
        import numpy as np
        N_SCALES = 4

        def _conv1d(x, w, b, pad):
            y = jax.lax.conv_general_dilated(x, w, window_strides=(1,), padding=[(pad, pad)], dimension_numbers=('NCH', 'OIH', 'NCH'))
            return y + b[None, :, None]
        key = jax.random.key(seed)
        ks = jax.random.split(key, 12)
        B, S, P, D = (8, 512, 512, 64)
        byte_sequence = jax.random.randint(ks[0], (B, S), 0, 64, dtype=jnp.int64)
        continuous_positions = jax.random.uniform(ks[1], (B, P), dtype=jnp.float32)
        emb = jax.random.normal(ks[2], (64, D), dtype=jnp.float32)
        locality_shapes = jax.random.normal(ks[3], (64, 4), dtype=jnp.float32)
        w1 = jax.random.normal(ks[4], (128, 64, 7), dtype=jnp.float32) * 0.02
        b1 = jnp.zeros((128,), dtype=jnp.float32)
        w2 = jax.random.normal(ks[5], (64, 128, 5), dtype=jnp.float32) * 0.02
        b2 = jnp.zeros((64,), dtype=jnp.float32)
        w3 = jax.random.normal(ks[6], (1, 64, 3), dtype=jnp.float32) * 0.02
        b3 = jnp.zeros((1,), dtype=jnp.float32)
        multiscale_widths = jnp.array([0.01, 0.02, 0.05, 0.1], dtype=jnp.float32)
        scale_weights = jnp.ones((4,), dtype=jnp.float32)
        return {'byte_sequence': byte_sequence, 'continuous_positions': continuous_positions, 'emb': emb, 'locality_shapes': locality_shapes, 'w1': w1, 'b1': b1, 'w2': w2, 'b2': b2, 'w3': w3, 'b3': b3, 'multiscale_widths': multiscale_widths, 'scale_weights': scale_weights}
    _L0_txt_all = _L0_txt_setup()
    _L0_txt_in = {k: v for k, v in _L0_txt_all.items() if k in ('emb', 'locality_shapes', 'w1', 'b1', 'w2', 'b2', 'w3', 'b3', 'multiscale_widths', 'scale_weights')}
    del _L0_txt_all

    def _L0_attn_setup():
        import jax, jax.numpy as jnp
        import numpy as np
        MIDC = 64
        HEADS = 16
        HEADC = MIDC // HEADS
        EPS = 1e-05

        def _layernorm(x, w, b):
            mean = jnp.mean(x, axis=-1, keepdims=True)
            std = jnp.std(x, axis=-1, keepdims=True, ddof=1)
            return w * (x - mean) / (std + EPS) + b
        key = jax.random.key(seed)
        ks = jax.random.split(key, 3)
        B, HW = (8, 4096)
        x = jax.random.normal(ks[0], (B, HW, MIDC), dtype=jnp.float32)
        W_qkv = jax.random.normal(ks[1], (3 * MIDC, MIDC), dtype=jnp.float32) * 0.02
        b_qkv = jnp.zeros((3 * MIDC,), dtype=jnp.float32)
        kln_w = jnp.ones((HEADS, 1, HEADC), dtype=jnp.float32)
        kln_b = jnp.zeros((HEADS, 1, HEADC), dtype=jnp.float32)
        vln_w = jnp.ones((HEADS, 1, HEADC), dtype=jnp.float32)
        vln_b = jnp.zeros((HEADS, 1, HEADC), dtype=jnp.float32)
        W_proj = jax.random.normal(ks[2], (MIDC, MIDC), dtype=jnp.float32) * 0.02
        b_proj = jnp.zeros((MIDC,), dtype=jnp.float32)
        return {'x': x, 'W_qkv': W_qkv, 'b_qkv': b_qkv, 'kln_w': kln_w, 'kln_b': kln_b, 'vln_w': vln_w, 'vln_b': vln_b, 'W_proj': W_proj, 'b_proj': b_proj}
    _L0_attn_all = _L0_attn_setup()
    _L0_attn_in = {k: v for k, v in _L0_attn_all.items() if k in ('W_qkv', 'b_qkv', 'kln_w', 'kln_b', 'vln_w', 'vln_b', 'W_proj', 'b_proj')}
    del _L0_attn_all

    def _L0_ffn_setup():
        import jax, jax.numpy as jnp
        import numpy as np
        D_MODEL = 64
        N_EXPERTS = 16
        HIDDEN = 128
        SCALE = 0.02
        key = jax.random.key(seed)
        ks = jax.random.split(key, 5)
        x = jax.random.normal(ks[0], (4, 2048, D_MODEL), dtype=jnp.float32)
        gate_w = jax.random.normal(ks[1], (D_MODEL, N_EXPERTS), dtype=jnp.float32) * SCALE
        gate_b = jnp.zeros((N_EXPERTS,), dtype=jnp.float32)
        w1 = jax.random.normal(ks[2], (N_EXPERTS, D_MODEL, HIDDEN), dtype=jnp.float32) * SCALE
        w2 = jax.random.normal(ks[3], (N_EXPERTS, D_MODEL, HIDDEN), dtype=jnp.float32) * SCALE
        w3 = jax.random.normal(ks[4], (N_EXPERTS, HIDDEN, D_MODEL), dtype=jnp.float32) * SCALE
        return {'x': x, 'gate_w': gate_w, 'gate_b': gate_b, 'w1': w1, 'w2': w2, 'w3': w3}
    _L0_ffn_all = _L0_ffn_setup()
    _L0_ffn_in = {k: v for k, v in _L0_ffn_all.items() if k in ('gate_w', 'gate_b', 'w1', 'w2', 'w3')}
    del _L0_ffn_all
    return {'x': x, 'x_txt': x_txt, 'fside_BS_continuous_positions': fside_BS_continuous_positions, 'L0_tok_ln_q_w': _L0_tok_in['ln_q_w'], 'L0_tok_ln_q_b': _L0_tok_in['ln_q_b'], 'L0_tok_Wq': _L0_tok_in['Wq'], 'L0_tok_ln_kv_w': _L0_tok_in['ln_kv_w'], 'L0_tok_ln_kv_b': _L0_tok_in['ln_kv_b'], 'L0_tok_Wkv': _L0_tok_in['Wkv'], 'L0_tok_proj_w': _L0_tok_in['proj_w'], 'L0_tok_proj_b': _L0_tok_in['proj_b'], 'L0_txt_emb': _L0_txt_in['emb'], 'L0_txt_locality_shapes': _L0_txt_in['locality_shapes'], 'L0_txt_w1': _L0_txt_in['w1'], 'L0_txt_b1': _L0_txt_in['b1'], 'L0_txt_w2': _L0_txt_in['w2'], 'L0_txt_b2': _L0_txt_in['b2'], 'L0_txt_w3': _L0_txt_in['w3'], 'L0_txt_b3': _L0_txt_in['b3'], 'L0_txt_multiscale_widths': _L0_txt_in['multiscale_widths'], 'L0_txt_scale_weights': _L0_txt_in['scale_weights'], 'L0_attn_W_qkv': _L0_attn_in['W_qkv'], 'L0_attn_b_qkv': _L0_attn_in['b_qkv'], 'L0_attn_kln_w': _L0_attn_in['kln_w'], 'L0_attn_kln_b': _L0_attn_in['kln_b'], 'L0_attn_vln_w': _L0_attn_in['vln_w'], 'L0_attn_vln_b': _L0_attn_in['vln_b'], 'L0_attn_W_proj': _L0_attn_in['W_proj'], 'L0_attn_b_proj': _L0_attn_in['b_proj'], 'L0_ffn_gate_w': _L0_ffn_in['gate_w'], 'L0_ffn_gate_b': _L0_ffn_in['gate_b'], 'L0_ffn_w1': _L0_ffn_in['w1'], 'L0_ffn_w2': _L0_ffn_in['w2'], 'L0_ffn_w3': _L0_ffn_in['w3']}

def reference(x, x_txt, fside_BS_continuous_positions, L0_tok_ln_q_w, L0_tok_ln_q_b, L0_tok_Wq, L0_tok_ln_kv_w, L0_tok_ln_kv_b, L0_tok_Wkv, L0_tok_proj_w, L0_tok_proj_b, L0_txt_emb, L0_txt_locality_shapes, L0_txt_w1, L0_txt_b1, L0_txt_w2, L0_txt_b2, L0_txt_w3, L0_txt_b3, L0_txt_multiscale_widths, L0_txt_scale_weights, L0_attn_W_qkv, L0_attn_b_qkv, L0_attn_kln_w, L0_attn_kln_b, L0_attn_vln_w, L0_attn_vln_b, L0_attn_W_proj, L0_attn_b_proj, L0_ffn_gate_w, L0_ffn_gate_b, L0_ffn_w1, L0_ffn_w2, L0_ffn_w3):
    import jax
    import jax.numpy as jnp

    def _L0_tok_ref(features, ln_q_w, ln_q_b, Wq, ln_kv_w, ln_kv_b, Wkv, proj_w, proj_b, conv_stride, num_heads):
        import jax, jax.numpy as jnp
        import numpy as np
        B, C, H, W = (32, 64, 64, 64)
        STRIDE, HEADS = (4, 8)

        def _ln(x, w, b):
            mu = x.mean(-1, keepdims=True)
            var = ((x - mu) ** 2).mean(-1, keepdims=True)
            return (x - mu) * jax.lax.rsqrt(var + 1e-05) * w + b
        s = conv_stride
        b, c, hh, ww = features.shape
        h, w = (hh // s, ww // s)
        hw, n, d = (h * w, s * s, c // num_heads)
        scale = c ** (-0.5)
        x = features.reshape(b, c, h, s, w, s)
        reduce_feats = x.mean((3, 5)).reshape(b, c, hw).transpose(0, 2, 1)
        unf = x.transpose(0, 1, 2, 4, 3, 5).reshape(b, c, hw, n).transpose(0, 2, 3, 1)
        q = _ln(reduce_feats, ln_q_w, ln_q_b) @ Wq.T
        q = q.reshape(b, hw, num_heads, d).transpose(0, 2, 1, 3)
        kv = _ln(unf, ln_kv_w, ln_kv_b) @ Wkv.T
        kv = kv.reshape(b, hw, n, 2, num_heads, d).transpose(3, 0, 4, 1, 2, 5)
        k, v = (kv[0], kv[1])
        attn = jax.nn.softmax(jnp.einsum('bhpd,bhpnd->bhpn', q * scale, k), axis=-1)
        aggre = jnp.einsum('bhpn,bhpnd->bhpd', attn, v)
        aggre = aggre.transpose(0, 2, 1, 3).reshape(b, hw, c)
        return reduce_feats + aggre @ proj_w.T + proj_b

    def _L0_txt_ref(byte_sequence, continuous_positions, emb, locality_shapes, w1, b1, w2, b2, w3, b3, multiscale_widths, scale_weights):
        import jax, jax.numpy as jnp
        import numpy as np
        N_SCALES = 4

        def _conv1d(x, w, b, pad):
            y = jax.lax.conv_general_dilated(x, w, window_strides=(1,), padding=[(pad, pad)], dimension_numbers=('NCH', 'OIH', 'NCH'))
            return y + b[None, :, None]
        B, S = byte_sequence.shape
        P = continuous_positions.shape[1]
        amps = emb[byte_sequence]
        onehot = jax.nn.one_hot(byte_sequence, 64, dtype=jnp.float32)
        onehot = jnp.transpose(onehot, (0, 2, 1))
        h = jax.nn.gelu(_conv1d(onehot, w1, b1, 3), approximate=False)
        h = jax.nn.gelu(_conv1d(h, w2, b2, 2), approximate=False)
        ctx = jax.nn.sigmoid(_conv1d(h, w3, b3, 1))[:, 0, :]
        amps = amps * ctx[:, :, None]
        lp = locality_shapes[byte_sequence]
        byte_pos = jnp.linspace(0.0, 1.0, S, dtype=jnp.float32)
        center = byte_pos[None, :] + lp[..., 0] * 0.05
        xd = continuous_positions[:, None, :] - center[..., None]
        amp_scale = jax.nn.sigmoid(lp[..., 2])
        phase = lp[..., 3] * jnp.pi
        abs_w = jnp.abs(lp[..., 1])
        TWO_PI = 2.0 * jnp.pi
        basis_total = jnp.zeros((B, S, P), dtype=jnp.float32)
        for s in range(N_SCALES):
            width = abs_w * multiscale_widths[s] + 1e-05
            z = xd / width[..., None]
            basis = jnp.exp(-0.5 * z * z) * jnp.cos(phase[..., None] + TWO_PI * z)
            basis_total = basis_total + basis * (amp_scale[..., None] * scale_weights[s] ** 2)
        semantic_field = jnp.einsum('bsp,bsd->bpd', basis_total, amps)
        return semantic_field

    def _L0_attn_ref(x, W_qkv, b_qkv, kln_w, kln_b, vln_w, vln_b, W_proj, b_proj):
        import jax, jax.numpy as jnp
        import numpy as np
        MIDC = 64
        HEADS = 16
        HEADC = MIDC // HEADS
        EPS = 1e-05

        def _layernorm(x, w, b):
            mean = jnp.mean(x, axis=-1, keepdims=True)
            std = jnp.std(x, axis=-1, keepdims=True, ddof=1)
            return w * (x - mean) / (std + EPS) + b
        B, HW, C = x.shape
        bias = x
        qkv = jnp.einsum('bnc,oc->bno', x, W_qkv) + b_qkv
        qkv = qkv.reshape(B, HW, HEADS, 3 * HEADC).transpose(0, 2, 1, 3)
        q, k, v = jnp.split(qkv, 3, axis=-1)
        k = _layernorm(k, kln_w, kln_b)
        v = _layernorm(v, vln_w, vln_b)
        kv = jnp.einsum('bhnd,bhne->bhde', k, v) / HW
        out = jnp.einsum('bhnd,bhde->bhne', q, kv)
        out = out.transpose(0, 2, 1, 3).reshape(B, HW, C)
        ret = out + bias
        proj = jnp.einsum('bnc,oc->bno', ret, W_proj) + b_proj
        return jax.nn.gelu(proj, approximate=False) + bias

    def _L0_ffn_ref(x, gate_w, gate_b, w1, w2, w3):
        import jax, jax.numpy as jnp
        import numpy as np
        D_MODEL = 64
        N_EXPERTS = 16
        HIDDEN = 128
        SCALE = 0.02
        n_experts = w1.shape[0]
        logits = jnp.einsum('bsd,de->bse', x, gate_w) + gate_b
        probs = jax.nn.softmax(logits, axis=-1)
        top_probs, top_idx = jax.lax.top_k(probs, 2)
        top_probs = top_probs / jnp.sum(top_probs, axis=-1, keepdims=True)
        dispatch = jnp.sum(jax.nn.one_hot(top_idx, n_experts, dtype=x.dtype) * top_probs[..., None], axis=-2)
        h1 = jnp.einsum('bsd,edh->bseh', x, w1)
        h2 = jnp.einsum('bsd,edh->bseh', x, w2)
        hidden = jax.nn.silu(h1) * h2
        expert_out = jnp.einsum('bseh,eho->bseo', hidden, w3)
        return jnp.einsum('bseo,bse->bso', expert_out, dispatch)
    h = _L0_tok_ref(x, L0_tok_ln_q_w, L0_tok_ln_q_b, L0_tok_Wq, L0_tok_ln_kv_w, L0_tok_ln_kv_b, L0_tok_Wkv, L0_tok_proj_w, L0_tok_proj_b, 4, 8)
    h = jnp.concatenate([h, _L0_txt_ref(x_txt, fside_BS_continuous_positions, L0_txt_emb, L0_txt_locality_shapes, L0_txt_w1, L0_txt_b1, L0_txt_w2, L0_txt_b2, L0_txt_w3, L0_txt_b3, L0_txt_multiscale_widths, L0_txt_scale_weights)], axis=1)
    h = h + _L0_attn_ref(_layernorm(h, axis=-1), L0_attn_W_qkv, L0_attn_b_qkv, L0_attn_kln_w, L0_attn_kln_b, L0_attn_vln_w, L0_attn_vln_b, L0_attn_W_proj, L0_attn_b_proj)
    h = h + _L0_ffn_ref(_layernorm(h, axis=-1), L0_ffn_gate_w, L0_ffn_gate_b, L0_ffn_w1, L0_ffn_w2, L0_ffn_w3)
    return h

_drawn_inputs = setup_inputs


def setup_inputs(seed=0):
    import zlib

    import numpy as np

    out = dict(_drawn_inputs(seed))
    spreads = {'L0_tok_ln_q_w': (1.0, 0.6),
     'L0_tok_ln_q_b': (0.0, 0.8),
     'L0_tok_ln_kv_w': (1.0, 0.6),
     'L0_tok_ln_kv_b': (0.0, 0.8),
     'L0_tok_proj_b': (0.0, 0.1),
     'L0_txt_b1': (0.0, 0.8),
     'L0_txt_b2': (0.0, 0.8),
     'L0_txt_scale_weights': (1.0, 0.2),
     'L0_attn_b_qkv': (0.0, 0.8),
     'L0_attn_kln_w': (1.0, 0.6),
     'L0_attn_kln_b': (0.0, 0.8),
     'L0_attn_vln_w': (1.0, 0.6),
     'L0_attn_vln_b': (0.0, 0.8),
     'L0_attn_b_proj': (0.0, 0.1),
     'L0_ffn_gate_b': (0.0, 0.8)}
    factors = {'L0_tok_Wq': 8.0,
     'L0_tok_Wkv': 3.357,
     'L0_tok_proj_w': 3.298,
     'L0_txt_w1': 8.0,
     'L0_txt_w2': 8.0,
     'L0_txt_w3': 8.0,
     'L0_attn_W_qkv': 8.0,
     'L0_ffn_gate_w': 8.0,
     'L0_ffn_w1': 8.0,
     'L0_ffn_w2': 8.0,
     'L0_ffn_w3': 8.0}
    for name, (base, spread) in spreads.items():
        noise = np.random.default_rng([zlib.crc32(name.encode()), seed]).standard_normal(out[name].shape)
        drawn = base * np.exp(spread * noise) if base else spread * noise
        out[name] = jnp.asarray(drawn.astype(out[name].dtype))
    for name, factor in factors.items():
        out[name] = (out[name] * factor).astype(out[name].dtype)
    return out
```

```python
from contextlib import ExitStack

import numpy as np
import concourse.bass as bass
from concourse import mybir

FP32 = mybir.dt.float32
FP16 = mybir.dt.float16
I32 = mybir.dt.int32
U32 = mybir.dt.uint32
ACT = mybir.ActivationFunctionType
ALU = mybir.AluOpType
X = mybir.AxisListType.X

B = 64
C = 64
P = 128
PAIRS = B // 2
PIX = 64 * 64
WIN = 16
IMG_T = PIX // WIN
TXT_T = 128
TOK = IMG_T + TXT_T
HEADS = 8
EPS = 1e-5

GROUP = 2048
GROUPS = B * PIX // 2 // GROUP
CHUNK = 512
CH = GROUP // CHUNK
WG = GROUP // WIN
WC = CHUNK // WIN

E_N = 16
HID = 128
TILES_TOK = B * TOK // P
LIST_T = TILES_TOK + 1
LIST = LIST_T * P
LISTS = E_N * LIST_T + 1
RUN_T = 2 * TILES_TOK + E_N
ROW = 66
X_SCALE = 32.0
W_SCALE = 64.0
MAGIC = 12582912.0


def pair_view(t):
    return t.rearrange("b c n -> (b c) n")


class Names:
    pass


def wait(engine, sem, value):
    if isinstance(value, int) and value <= 0:
        return
    engine.wait_ge(sem, value)



F32_PARTS = [("ident", 128), ("center", 128), ("average", 128), ("mean32", 32), ("head32", 32),
             ("center4", 64), ("mask4", 128), ("byte_pos", 1), ("eps", 1), ("tiny", 1), ("rank_e", 16),
             ("list_base", 16), ("pad_place", 1), ("tile_no", 4), ("row_no", 12), ("vocab", 1)]
F16_PARTS = [("ident16", 128), ("ones16", 128), ("before16", 128), ("spread16", 4 * 128)]


def columns(parts):
    at, out = 0, {}
    for name, n in parts:
        out[name] = (at, at + n)
        at += n
    return out, at


F32_AT, F32_N = columns(F32_PARTS)
F16_AT, F16_N = columns(F16_PARTS)


def shape_constants():
    two = np.eye(2)
    f = np.zeros((P, F32_N), np.float32)
    h = np.zeros((P, F16_N), np.float16)

    def put(name, value):
        a, b = F32_AT[name]
        f[:value.shape[0], a:b] = value

    p = np.arange(P)
    put("ident", np.eye(P))
    put("center", np.kron(two, np.eye(C) - 1.0 / C))
    put("average", np.kron(two, np.full((C, C), 1.0 / C)))
    mean32 = np.zeros((P, 32))
    head32 = np.zeros((P, 32))
    for s in range(2):
        for head in range(HEADS):
            mean32[s * C:(s + 1) * C, s * HEADS + head] = 1.0 / C
            head32[s * C + head * 8:s * C + head * 8 + 8, s * HEADS + head] = 1.0
    put("mean32", mean32)
    put("head32", head32)
    put("center4", np.kron(np.eye(16), np.eye(4) - 0.25))
    put("mask4", np.kron(np.eye(32), np.full((4, 4), 1.0 / TOK)))
    put("byte_pos", np.linspace(0.0, 1.0, TXT_T, dtype=np.float32)[:, None])
    put("eps", np.full((P, 1), EPS))
    put("tiny", np.full((P, 1), 1e-30))
    put("list_base", np.tile(np.arange(E_N) * LIST, (P, 1)))
    put("pad_place", np.full((P, 1), 2 * B * TOK + 1.0))
    put("tile_no", p[:, None] + P * np.arange(4)[None, :])
    put("rank_e", np.tile(E_N - np.arange(E_N), (P, 1)))
    k, t, smp = np.meshgrid(np.arange(2), np.arange(TOK // P), np.arange(2), indexing="ij")
    put("row_no", p[:, None] + (k * B * TOK + smp * TOK + t * P).reshape(1, -1))
    put("vocab", (p % 64)[:, None])
    for name, value in (("ident16", np.eye(P)), ("ones16", np.ones((P, P))),
                        ("before16", (p[:, None] < p[None, :]))):
        a, b = F16_AT[name]
        h[:, a:b] = value
    a, _ = F16_AT["spread16"]
    for c in range(CH):
        for s in range(2):
            for head in range(HEADS):
                row = 32 * c + s * HEADS + head
                col = a + P * c + s * C + head * 8
                h[row, col:col + 8] = 1.0
    return f, h


W_PARTS = [("wk", 128), ("wv", 128), ("wq", 128), ("proj", 128),
           ("kv_scale", 1), ("kv_shift", 1), ("q_scale", 1), ("q_shift", 1), ("proj_b", 1),
           ("mk", 128), ("mv", 128), ("mk_b", 1), ("mv_b", 1), ("mq", 128), ("mq_b", 1),
           ("mproj", 128), ("mproj_b", 1), ("kv_ln_w", 256), ("kv_ln_b", 256),
           ("gate", 32), ("gate_b", 32), ("w3", E_N * C),
           ("c1", 4 * 128), ("c1_b", 1), ("c2", 5 * 64), ("c2_b", 1), ("c3", 3 * 2), ("c3_b", 1),
           ("embed", 68), ("widths", 4), ("scales", 4)]
W_AT, W_N = columns(W_PARTS)


def pack_weights(g):
    w = np.zeros((P, W_N), np.float32)

    def put(name, value, rows=slice(None)):
        a, b = W_AT[name]
        w[rows, a:b] = value

    def both(name, matrix):
        a, b = W_AT[name]
        n = (b - a) // 2
        w[:C, a:a + n] = matrix
        w[C:, a + n:b] = matrix

    def column(name, vector):
        put(name, np.tile(vector, P // vector.shape[0])[:, None])

    both("wk", g["L0_tok_Wkv"][:C].T)
    both("wv", g["L0_tok_Wkv"][C:].T)
    both("wq", g["L0_tok_Wq"].T)
    both("proj", g["L0_tok_proj_w"].T)
    column("kv_scale", g["L0_tok_ln_kv_w"])
    column("kv_shift", g["L0_tok_ln_kv_b"])
    column("q_scale", g["L0_tok_ln_q_w"])
    column("q_shift", g["L0_tok_ln_q_b"])
    column("proj_b", g["L0_tok_proj_b"])
    qkv = g["L0_attn_W_qkv"].reshape(16, 3, 4, C)
    qkv_b = g["L0_attn_b_qkv"].reshape(16, 3, 4)
    for name, part in (("mk", 1), ("mv", 2)):
        put(name, np.tile(qkv[:, part].reshape(C, C), (1, 2)), slice(0, C))
        put(name + "_b", qkv_b[:, part].reshape(C, 1), slice(0, C))
    both("mq", qkv[:, 0].reshape(C, C).T)
    column("mq_b", qkv_b[:, 0].reshape(C))
    both("mproj", g["L0_attn_W_proj"].T)
    column("mproj_b", g["L0_attn_b_proj"])
    for name, k, v in (("kv_ln_w", "L0_attn_kln_w", "L0_attn_vln_w"), ("kv_ln_b", "L0_attn_kln_b", "L0_attn_vln_b")):
        put(name, np.concatenate([np.tile(g[k].reshape(C), 2), np.tile(g[v].reshape(C), 2)])[None, :])
    both("gate", g["L0_ffn_gate_w"])
    put("gate_b", np.tile(g["L0_ffn_gate_b"], 2)[None, :])
    put("w3", g["L0_ffn_w3"].transpose(1, 0, 2).reshape(HID, E_N * C))
    taps = np.zeros((2, C, 4, 128), np.float32)
    w1 = g["L0_txt_w1"]
    for tap in range(7):
        taps[tap % 2, :, tap // 2] = w1[:, :, tap].T
    put("c1", taps.reshape(P, 4 * 128))
    column("c1_b", g["L0_txt_b1"])
    put("c2", g["L0_txt_w2"].transpose(1, 2, 0).reshape(P, 5 * C))
    column("c2_b", g["L0_txt_b2"])
    c3 = np.zeros((2, C, 3, 2), np.float32)
    for s in range(2):
        c3[s, :, :, s] = g["L0_txt_w3"][0]
    put("c3", c3.reshape(P, 6))
    put("c3_b", g["L0_txt_b3"][0])
    put("embed", np.concatenate([g["L0_txt_emb"], g["L0_txt_locality_shapes"]], axis=1), slice(0, C))
    put("widths", g["L0_txt_multiscale_widths"][None, :])
    put("scales", g["L0_txt_scale_weights"][None, :])
    return w


def constants(nc, n):
    with ExitStack() as ctx:
        raw = ctx.enter_context(nc.sbuf_tensor("raw12", [P, 2, E_N * HID], FP32))
        big = ctx.enter_context(nc.sbuf_tensor("big12", [P, 2, E_N * HID], FP32))
        scaled = ctx.enter_context(nc.sbuf_tensor("scaled", [P, 3, 128], FP32))
        bias_rows = ctx.enter_context(nc.sbuf_tensor("bias_rows", [C, 2, 128], FP32))
        v_bias = ctx.enter_context(nc.sbuf_tensor("v_bias", [P, 1], FP32))
        pw = ctx.enter_context(nc.psum_tensor("pw", [P, 512], FP32))
        pm = ctx.enter_context(nc.psum_tensor("pm", [P, 512], FP32))
        pb = ctx.enter_context(nc.psum_tensor("pb", [P, 8], FP32))
        sem = lambda name: ctx.enter_context(nc.semaphore(name))
        weights_in, w12_in = n.sem("weights_in"), n.sem("w12_in")
        scaled_rows, w_products, vb_product, vb_copied = (n.sem(x) for x in ("scaled_rows", "w_products", "vb_product", "vb_copied"))
        pb_product, w12_scaled, w12_high = (n.sem(x) for x in ("pb_product", "w12_scaled", "w12_high"))
        w, f = n.w, n.f

        def W(name, rows=P):
            a, b = W_AT[name]
            return w[0:rows, a:b]

        def K(name, rows=P):
            a, b = F32_AT[name]
            return f[0:rows, a:b]

        with nc.Block() as block:
            @block.sync
            def _(sp):
                sp.dma_start(w[:, :], n.in_weights).then_inc(weights_in, 16)
                sp.dma_start(f[:, :], n.in_f32).then_inc(weights_in, 16)
                sp.dma_start(n.h[:, :], n.in_f16).then_inc(weights_in, 16)
                for half in range(2):
                    for which, src in enumerate((n.in_w1, n.in_w2)):
                        sp.dma_start(raw[half * C:(half + 1) * C, which, :].rearrange("c (e j) -> c e j", e=E_N),
                                     src.rearrange("e c j -> c e j")).then_inc(w12_in, 16)

            @block.vector
            def _(dve):
                dve.wait_ge(weights_in, 48)
                nc.vector.tensor_scalar(scaled[:, 0, :], W("wk"), W("kv_scale"), None, ALU.mult).then_inc(scaled_rows, 1)
                nc.vector.tensor_scalar(scaled[:, 1, :], W("wv"), W("kv_scale"), None, ALU.mult).then_inc(scaled_rows, 1)
                nc.vector.tensor_scalar(n.wq[:, :], W("wq"), W("q_scale"), 0.125, ALU.mult, ALU.mult)
                nc.vector.tensor_scalar(scaled[:, 2, :], W("wq"), 0.125, None, ALU.mult).then_inc(scaled_rows, 1)
                for i, name in enumerate(("mk_b", "mv_b")):
                    nc.vector.tensor_scalar(bias_rows[:, i, :], f[0:C, F32_AT["average"][0]:F32_AT["average"][1]], 0.0,
                                            W(name, C), ALU.mult, ALU.add).then_inc(scaled_rows, 1)
                dve.wait_ge(w_products, 1)
                nc.vector.tensor_copy(n.wk[:, :], pw[:, 0:128])
                nc.vector.tensor_copy(n.wv[:, :], pw[:, 128:256])
                nc.vector.memset(n.mkv[:, :, :, :], 0.0).then_inc(vb_copied, 1)
                dve.wait_ge(vb_copied, 1)
                for s in range(2):
                    nc.vector.tensor_copy(n.mkv[s * C:(s + 1) * C, :, s, :],
                                          pm[s * C:(s + 1) * C, 0:128].rearrange("p (a c) -> p a c", a=2))
                    nc.vector.tensor_copy(n.mkv_b[:, :, s, :], pm[:, 128:256].rearrange("p (a c) -> p a c", a=2))
                nc.vector.tensor_copy(n.bq[:, :], pw[:, 256:257])
                nc.vector.tensor_copy(v_bias[:, :], pw[:, 257:258]).then_inc(vb_copied, 1)
                dve.wait_ge(pb_product, 1)
                nc.vector.tensor_tensor(n.pb[:, :], pb[:, 0:1], W("proj_b"), ALU.add)
                dve.wait_ge(w12_in, 64)
                nc.vector.tensor_scalar(big[:, :, :], raw[:, :, :], W_SCALE, None, ALU.mult).then_inc(w12_scaled, 1)
                dve.wait_ge(w12_scaled, 1)
                for which in range(2):
                    src = big[:, which, :].rearrange("p (e j) -> p e j", e=E_N)
                    nc.vector.tensor_copy(n.w12[:, :, which, 0, :], src).then_inc(w12_high, 1)
                    dve.wait_ge(w12_high, which + 1)
                    nc.vector.tensor_tensor(n.w12[:, :, which, 1, :], src, n.w12[:, :, which, 0, :], ALU.subtract)

            @block.tensor
            def _(pe):
                pe.wait_ge(weights_in, 48)
                pe.wait_ge(scaled_rows, 5)
                nc.tensor.matmul(pw[:, 0:128], K("center"), scaled[:, 0, :], start=True, stop=True)
                nc.tensor.matmul(pw[:, 128:256], K("center"), scaled[:, 1, :], start=True, stop=True)
                nc.tensor.matmul(pw[:, 256:257], scaled[:, 2, :], W("q_shift"), start=True, stop=True)
                nc.tensor.matmul(pw[:, 257:258], W("wv"), W("kv_shift"), start=True, stop=True)
                for i, name in enumerate(("mk", "mv")):
                    nc.tensor.matmul(pm[:, 64 * i:64 * i + 64], W(name, C), K("center4", C), start=True, stop=True)
                for i in range(2):
                    last = nc.tensor.matmul(pm[:, 128 + 64 * i:192 + 64 * i], bias_rows[:, i, :], K("center4", C),
                                            start=True, stop=True)
                last.then_inc(w_products, 1)
                pe.wait_ge(vb_copied, 2)
                nc.tensor.matmul(pb[:, 0:1], W("proj"), v_bias[:, :], start=True, stop=True).then_inc(pb_product, 1)


def text(nc, n):
    with ExitStack() as ctx:
        def sb(name, shape, dt=FP32):
            return ctx.enter_context(nc.sbuf_tensor(name, shape, dt))

        def bank(name):
            return ctx.enter_context(nc.psum_tensor(name, [P, 512], FP32))

        FOUR = 4
        SC = 4
        STEPS = B // FOUR
        PAD1, PAD2, PAD3 = TXT_T + 6, TXT_T + 4, TXT_T + 2
        UNSCALE = 1.0 / W_SCALE
        ids = sb("ids", [P, FOUR, TXT_T], I32)
        pos = sb("pos", [P, 2, FOUR, TXT_T])
        onehot = sb("onehot", [P, FOUR, PAD1], FP16)
        c1 = sb("c1_parts", [P, 2, 4, P], FP16)
        c1_big = sb("c1_big", [P, 4, P])
        emb = sb("emb_parts", [P, 3, 68], FP16)
        emb_big = sb("emb_big", [P, 2, 68])
        hidden1 = sb("hidden1", [P, FOUR, PAD2])
        hidden2 = sb("hidden2", [P, 2, PAD3])
        gates = sb("gates", [P, 2, FOUR])
        gates1 = sb("gates1", [P, 2, FOUR])
        factor = sb("factor", [P, FOUR])
        loc = sb("loc", [P, FOUR, 4])
        abs_w = sb("abs_w", [P, FOUR])
        center = sb("wave_center", [P, 2, FOUR])
        width = sb("width", [P, FOUR, SC])
        width1 = sb("width1", [P, FOUR, SC])
        inv_w = sb("inv_w", [P, 2, FOUR, SC])
        shift = sb("shift", [P, 2, FOUR])
        amps = sb("amps", [P, 2, FOUR, C])
        sw2 = sb("sw2", [P, SC])
        b3_half = sb("b3_half", [P, 1])
        dist = sb("dist", [P, FOUR, TXT_T])
        z = sb("z", [P, SC, FOUR, TXT_T])
        zc = sb("zc", [P, SC, FOUR, TXT_T])
        z_sq = sb("z_sq", [P, SC, FOUR, TXT_T])
        turns = sb("turns", [P, SC, FOUR, TXT_T])
        whole = sb("whole", [P, SC, FOUR, TXT_T])
        frac = sb("frac", [P, SC, FOUR, TXT_T])
        bell = sb("bell", [P, SC, FOUR, TXT_T])
        wave = sb("wave", [P, SC, FOUR, TXT_T])
        packet = sb("packet", [P, SC, FOUR, TXT_T])
        p_c1, p_c2, p_ctx, p_emb, p_field = (bank(x) for x in ("p_c1", "p_c2", "p_ctx", "p_emb", "p_field"))
        names = ("parts_hi parts_mid parts_done ids_in onehot_done c1_ready gelu1_done c2_ready gelu2_done ctx_ready emb_ready "
                 "gates_done loc_done gates_eased factor_done amps_done width_made width_eased params_done dist_done z_done "
                 "clamped squared bell_done turned rounded frac_done wave_done packet_done field_ready field_copied zeroed")
        s = {name: ctx.enter_context(nc.semaphore("t_" + name)) for name in names.split()}
        pos_in = [ctx.enter_context(nc.semaphore(f"t_pos_in{k}")) for k in range(2)]
        W = lambda name: n.w[:, W_AT[name][0]:W_AT[name][1]]
        K = lambda name: n.f[:, F32_AT[name][0]:F32_AT[name][1]]

        def run(engine, body):
            for i in range(2):
                body(i, i, True, i > 0)
            with engine.Fori(1, STEPS // 2) as j:
                for u in range(2):
                    body(2 * j + u, u, True, True)
            body(STEPS, 0, False, True)

        with nc.Block() as block:
            @block.sync
            def _(sp):
                def body(i, u, new, old):
                    if not new:
                        return
                    wait(sp, s["onehot_done"], 2 * i)
                    sp.dma_start(ids[:, :, :].rearrange("p b t -> p (b t)"),
                                 n.in_ids[0, bass.ds(i * 512, 512)].partition_broadcast(P)).then_inc(s["ids_in"], 16)
                    wait(sp, s["dist_done"], i - 1)
                    sp.dma_start(pos[:, u, :, :].rearrange("p b t -> p (b t)"),
                                 n.in_pos[0, bass.ds(i * 512, 512)].partition_broadcast(P)).then_inc(pos_in[u], 16)

                run(sp, body)

            @block.tensor
            def _(pe):
                mm = nc.tensor.matmul

                def body(i, u, new, old):
                    if new:
                        pe.wait_ge(s["onehot_done"], 2 * i + 2)
                        wait(pe, s["gelu1_done"], i)
                        if isinstance(i, int) and i == 0:
                            pe.wait_ge(s["parts_done"], 3)
                            pe.wait_ge(s["zeroed"], 3)
                        for j in range(4):
                            for part in range(2):
                                last = mm(p_c1[:, :], c1[:, part, j, :], onehot[:, :, 2 * j:2 * j + TXT_T],
                                          start=(j + part == 0), stop=(j == 3 and part == 1))
                        last.then_inc(s["c1_ready"], 1)
                        wait(pe, s["amps_done"], i)
                        wait(pe, s["loc_done"], i)
                        for b in range(FOUR):
                            for part in range(3):
                                last = mm(p_emb[:, 68 * b:68 * b + 68], onehot[:, b, 3:3 + TXT_T], emb[:, part, :],
                                          start=(part == 0), stop=(part == 2))
                        last.then_inc(s["emb_ready"], 1)
                    if new:
                        pe.wait_ge(s["gelu1_done"], i + 1)
                        wait(pe, s["gelu2_done"], i)
                        for k in range(2):
                            for tap in range(5):
                                last = mm(p_c2[C * k:C * k + C, 0:2 * TXT_T], n.w[:, W_AT["c2"][0] + C * tap:W_AT["c2"][0] + C * tap + C],
                                          hidden1[:, k:4:2, tap:tap + TXT_T], start=(tap == 0), stop=(tap == 4), tile_position=(0, C * k))
                        last.then_inc(s["c2_ready"], 1)
                        pe.wait_ge(s["gelu2_done"], i + 1)
                        wait(pe, s["gates_done"], i)
                        for q in range(2):
                            for tap in range(3):
                                last = mm(p_ctx[:, 2 * q:2 * q + 2], hidden2[:, q, tap:tap + TXT_T],
                                          n.w[:, W_AT["c3"][0] + 2 * tap:W_AT["c3"][0] + 2 * tap + 2], start=(tap == 0), stop=(tap == 2))
                        last.then_inc(s["ctx_ready"], 1)
                    if old:
                        pe.wait_ge(s["packet_done"], 4 * i)
                        wait(pe, s["field_copied"], i - 1)
                        for b in range(FOUR):
                            for k in range(SC):
                                last = mm(p_field[C * (b % 2):C * (b % 2) + C, P * (b // 2):P * (b // 2) + P], amps[:, 1 - u, b, :],
                                          packet[:, k, b, :], start=(k == 0), stop=(k == SC - 1), tile_position=(0, C * (b % 2)))
                        last.then_inc(s["field_ready"], 1)

                run(pe, body)

            @block.scalar
            def _(act):
                A = nc.scalar.activation

                def body(i, u, new, old):
                    emb4 = p_emb[:, 0:68 * FOUR].rearrange("p (b e) -> p b e", b=FOUR)
                    if new:
                        act.wait_ge(s["c1_ready"], i + 1)
                        wait(act, s["c2_ready"], i)
                        if isinstance(i, int) and i == 0:
                            act.wait_ge(s["zeroed"], 3)
                        A(hidden1[:, :, 2:2 + TXT_T], p_c1[:, :].rearrange("p (b t) -> p b t", b=FOUR), ACT.Gelu,
                          bias=W("c1_b"), scale=UNSCALE).then_inc(s["gelu1_done"], 1)
                    if old:
                        act.wait_ge(s["clamped"], i)
                        wait(act, s["bell_done"], i - 1)
                        A(z_sq[:, :, :, :], zc[:, :, :, :], ACT.Square).then_inc(s["squared"], 1)
                    if new:
                        act.wait_ge(s["c2_ready"], i + 1)
                        wait(act, s["ctx_ready"], i)
                        A(hidden2[:, :, 1:1 + TXT_T], p_c2[:, 0:2 * TXT_T].rearrange("p (q t) -> p q t", q=2), ACT.Gelu,
                          bias=W("c2_b")).then_inc(s["gelu2_done"], 1)
                        act.wait_ge(s["emb_ready"], i + 1)
                        wait(act, s["gates_eased"], i)
                        A(gates[:, 1, :], emb4[:, :, 66], ACT.Tanh, scale=0.5 * UNSCALE)
                        wait(act, s["params_done"], i)
                        A(loc[:, :, :], emb4[:, :, 64:68], ACT.Copy, scale=UNSCALE)
                        A(abs_w[:, :], emb4[:, :, 65], ACT.Abs, scale=UNSCALE).then_inc(s["loc_done"], 1)
                        act.wait_ge(s["ctx_ready"], i + 1)
                        A(gates[:, 0, :], p_ctx[:, 0:FOUR], ACT.Tanh, scale=0.5, bias=b3_half[:, :]).then_inc(s["gates_done"], 1)
                    if old:
                        act.wait_ge(s["squared"], i)
                        wait(act, s["packet_done"], 4 * (i - 1))
                        A(bell[:, :, :, :], z_sq[:, :, :, :], ACT.Exp, scale=-0.5).then_inc(s["bell_done"], 1)
                        act.wait_ge(s["frac_done"], i)
                        A(wave[:, :, :, :], frac[:, :, :, :], ACT.Sin, scale=6.2831845).then_inc(s["wave_done"], 1)
                        act.wait_ge(s["field_ready"], i)
                        A(n.tokens[:, bass.ds(2 * i - 2, 2), IMG_T:TOK], p_field[:, 0:2 * TXT_T].rearrange("p (q t) -> p q t", q=2),
                          ACT.Copy).then_inc(s["field_copied"], 1)

                run(act, body)

            @block.vector
            def _(dve):
                V = nc.vector
                V.tensor_scalar(c1_big[:, :, :].rearrange("p a b -> p (a b)"), W("c1"), W_SCALE, None, ALU.mult)
                V.tensor_scalar(emb_big[:, 0, :], W("embed"), W_SCALE, None, ALU.mult)
                V.tensor_tensor(sw2[:, :], W("scales"), W("scales"), ALU.mult)
                V.tensor_scalar(b3_half[:, :], W("c3_b"), 0.5, None, ALU.mult).then_inc(s["parts_hi"], 1)
                dve.wait_ge(s["parts_hi"], 1)
                V.tensor_copy(c1[:, 0, :, :], c1_big[:, :, :])
                V.tensor_copy(emb[:, 0, :], emb_big[:, 0, :]).then_inc(s["parts_hi"], 1)
                dve.wait_ge(s["parts_hi"], 2)
                V.tensor_tensor(c1[:, 1, :, :], c1_big[:, :, :], c1[:, 0, :, :], ALU.subtract).then_inc(s["parts_done"], 1)
                V.tensor_tensor(emb_big[:, 1, :], emb_big[:, 0, :], emb[:, 0, :], ALU.subtract).then_inc(s["parts_mid"], 1)
                dve.wait_ge(s["parts_mid"], 1)
                V.tensor_copy(emb[:, 1, :], emb_big[:, 1, :]).then_inc(s["parts_done"], 1)
                dve.wait_ge(s["parts_done"], 2)
                V.tensor_tensor(emb[:, 2, :], emb_big[:, 1, :], emb[:, 1, :], ALU.subtract).then_inc(s["parts_done"], 1)

                def body(i, u, new, old):
                    if new:
                        dve.wait_ge(s["ids_in"], 16 * (i + 1))
                        wait(dve, s["emb_ready"], i)
                        if isinstance(i, int) and i == 0:
                            dve.wait_ge(s["zeroed"], 1)
                        for half in range(2):
                            V.tensor_scalar(onehot[C * half:C * half + C, :, 3 - half:3 - half + TXT_T], ids[C * half:C * half + C, :, :],
                                            K("vocab")[C * half:C * half + C, :], None, ALU.is_equal).then_inc(s["onehot_done"], 1)
                    if old:
                        v = 1 - u
                        dve.wait_ge(pos_in[v], 16 * ((i + 1) // 2) if isinstance(i, int) else 16 * wave_loads(i, u))
                        V.tensor_tensor(dist[:, :, :], pos[:, v, :, :], center[:, v, :].unsqueeze(2).broadcast_to([P, FOUR, TXT_T]),
                                        ALU.subtract).then_inc(s["dist_done"], 1)
                        dve.wait_ge(s["dist_done"], i)
                        wait(dve, s["clamped"], i - 1)
                        for k in range(SC):
                            last = V.tensor_tensor(z[:, k, :, :], dist[:, :, :], inv_w[:, v, :, k:k + 1].broadcast_to([P, FOUR, TXT_T]), ALU.mult)
                        last.then_inc(s["z_done"], 1)
                        dve.wait_ge(s["z_done"], i)
                        wait(dve, s["squared"], i - 1)
                        wait(dve, s["turned"], i - 1)
                        V.tensor_scalar(zc[:, :, :, :], z[:, :, :, :], 30.0, -30.0, ALU.min, ALU.max).then_inc(s["clamped"], 1)
                    if new:
                        dve.wait_ge(s["loc_done"], i + 1)
                        wait(dve, s["dist_done"], i - 1)
                        wait(dve, s["turned"], i - 1)
                        V.tensor_scalar(center[:, u, :], loc[:, :, 0], 0.05, K("byte_pos"), ALU.mult, ALU.add)
                        V.tensor_scalar(shift[:, u, :], loc[:, :, 3], 0.5, 0.25, ALU.mult, ALU.add)
                        V.tensor_tensor(width[:, :, :], abs_w[:, :].unsqueeze(2).broadcast_to([P, FOUR, SC]),
                                        W("widths").unsqueeze(1).broadcast_to([P, FOUR, SC]), ALU.mult).then_inc(s["width_made"], 1)
                        dve.wait_ge(s["width_made"], i + 1)
                        V.tensor_scalar(width1[:, :, :], width[:, :, :], 1e-5, None, ALU.add).then_inc(s["width_eased"], 1)
                        dve.wait_ge(s["width_eased"], i + 1)
                        V.reciprocal(inv_w[:, u, :, :], width1[:, :, :]).then_inc(s["params_done"], 1)
                    if old:
                        dve.wait_ge(s["turned"], i)
                        wait(dve, s["frac_done"], i - 1)
                        V.tensor_scalar(whole[:, :, :, :], turns[:, :, :, :], MAGIC, -MAGIC, ALU.add, ALU.add).then_inc(s["rounded"], 1)
                    if new:
                        dve.wait_ge(s["gates_done"], i + 1)
                        wait(dve, s["factor_done"], i)
                        V.tensor_scalar(gates1[:, :, :], gates[:, :, :], 0.5, 0.5, ALU.mult, ALU.add).then_inc(s["gates_eased"], 1)
                        dve.wait_ge(s["gates_eased"], i + 1)
                        wait(dve, s["amps_done"], i)
                        V.scalar_tensor_tensor(factor[:, :], gates1[:, 0, :], UNSCALE, gates1[:, 1, :], ALU.mult, ALU.mult).then_inc(s["factor_done"], 1)
                        dve.wait_ge(s["factor_done"], i + 1)
                        wait(dve, s["field_ready"], i - 1)
                        V.tensor_tensor(amps[:, u, :, :], p_emb[:, 0:68 * FOUR].rearrange("p (b e) -> p b e", b=FOUR)[:, :, 0:C],
                                        factor[:, :].unsqueeze(2).broadcast_to([P, FOUR, C]), ALU.mult).then_inc(s["amps_done"], 1)
                    if old:
                        dve.wait_ge(s["wave_done"], i)
                        dve.wait_ge(s["bell_done"], i)
                        wait(dve, s["field_ready"], i - 1)
                        for k in range(SC):
                            V.scalar_tensor_tensor(packet[:, k, :, :], bell[:, k, :, :], sw2[:, k:k + 1], wave[:, k, :, :],
                                                   ALU.mult, ALU.mult).then_inc(s["packet_done"], 1)

                def wave_loads(i, u):
                    return i // 2 if u == 0 else (i + 1) // 2

                run(dve, body)

            @block.gpsimd
            def _(pool):
                G = nc.gpsimd
                G.memset(onehot[:, :, :], 0.0).then_inc(s["zeroed"], 1)
                G.memset(hidden1[:, :, :], 0.0).then_inc(s["zeroed"], 1)
                G.memset(hidden2[:, :, :], 0.0).then_inc(s["zeroed"], 1)

                def body(i, u, new, old):
                    if old:
                        v = 1 - u
                        pool.wait_ge(s["clamped"], i)
                        wait(pool, s["rounded"], i - 1)
                        wait(pool, s["frac_done"], i - 1)
                        G.tensor_tensor(turns[:, :, :, :].rearrange("p k b t -> p k b t"), zc[:, :, :, :],
                                        shift[:, v, :].unsqueeze(1).unsqueeze(3).broadcast_to([P, SC, FOUR, TXT_T]), ALU.add).then_inc(s["turned"], 1)
                        pool.wait_ge(s["rounded"], i)
                        wait(pool, s["wave_done"], i - 1)
                        G.tensor_tensor(frac[:, :, :, :], turns[:, :, :, :], whole[:, :, :, :], ALU.subtract).then_inc(s["frac_done"], 1)

                run(pool, body)

        with nc.Block() as block:
            @block.gpsimd
            def _(pool):
                for sem in [*s.values(), *pos_in]:
                    pool.sem_clear(sem)


def windows(nc, n):
    with ExitStack() as ctx:
        def sb(name, shape, dt=FP32):
            return ctx.enter_context(nc.sbuf_tensor(name, shape, dt))

        def bank(name):
            return ctx.enter_context(nc.psum_tensor(name, [P, 512], FP32))

        xs = sb("xs", [P, 4, GROUP])
        squares = sb("squares", [P, GROUP])
        tree1 = sb("tree1", [P, 1024])
        tree2 = sb("tree2", [P, 512])
        tree3 = sb("tree3", [P, 256])
        sums = sb("sums", [P, 4, WG])
        q_cent = sb("q_cent", [P, WG])
        q_square = sb("q_square", [P, WG])
        q_log = sb("q_log", [P, WG])
        q_rstd = sb("q_rstd", [P, WG])
        q_norm = sb("q_norm", [P, WG])
        qs = sb("qs", [P, 2, WG])
        mean_sq = sb("mean_sq", [P, CHUNK])
        var = sb("var", [P, CHUNK])
        var_pos = sb("var_pos", [P, CHUNK])
        var_log = sb("var_log", [P, CHUNK])
        rstd = sb("rstd", [P, 2, CHUNK])
        qk = sb("qk", [P, 2, CHUNK])
        score = sb("score", [P, CHUNK])
        top = sb("top", [P, WC])
        below = sb("below", [P, CHUNK])
        ex = sb("ex", [P, CHUNK])
        total = sb("total", [P, WC])
        inv = sb("inv", [P, WC])
        ex_rstd = sb("ex_rstd", [P, CHUNK])
        weight = sb("weight", [P, CHUNK])
        w_hi = sb("w_hi", [P, 2, CHUNK], FP16)
        w_lo = sb("w_lo", [P, 2, CHUNK], FP16)
        w_wide = sb("w_wide", [P, 2, CHUNK])
        wv = sb("wv_prod", [P, 2, CHUNK])
        agg = sb("agg", [P, WG])
        out_b = sb("out_b", [P, WG])
        p_kv = [bank("p_kv0"), bank("p_kv1")]
        p_w, p_mean, p_sq, p_score, p_q, p_out = (bank(x) for x in ("p_w", "p_mean", "p_sq", "p_score", "p_q", "p_out"))
        names = ("sums_1 sums_2 sums_3 sums_done cent_ready cent_copied q_var_ready q_log_done q_rstd_done q_normed "
                 "q_ready q_copied squared mean_ready sq_ready mean_sq_done var_done var_clamped var_logged rstd_done "
                 "k_ready qk_done scores_ready scored top_done below_done exp_done total_done inv_done ex_rstd_done "
                 "weight_done hi_done lo_done v_ready wide_ready wide_copied wv_done reduced proj_ready out_biased token_done")
        s = {name: n.sem(name) for name in names.split()}
        x_in = [n.sem(f"x_in{k}") for k in range(4)]
        x_dram = n.in_x.rearrange("(q b) c (h n) -> q (b c) h n", b=2, h=2)
        K = lambda name, rows=P: n.f[0:rows, F32_AT[name][0]:F32_AT[name][1]]
        spread = lambda c: n.h[:, F16_AT["spread16"][0] + P * c:F16_AT["spread16"][0] + P * c + P]
        proj = n.w[:, W_AT["proj"][0]:W_AT["proj"][1]]

        def window_order(t):
            return t.rearrange("p (row col x) -> p col row x", row=8, x=4)

        def by_window(t):
            return t.rearrange("p (col k) -> p col k", k=WIN)

        def chunk_windows(t, c):
            return t[:, WC * c:WC * c + WC].rearrange("p (row col) -> p col row", row=2)

        def steps(body):
            for g in range(-1, 4):
                body(g, g % 4, g // 4, g >= 0, g < GROUPS - 1, g >= 1, g >= 2)
            return lambda i: [body(4 * i + u, u, i, True, True, True, True) for u in range(4)]

        def tail(body):
            for g in range(GROUPS - 4, GROUPS + 2):
                body(g, g % 4, g // 4, g < GROUPS, g < GROUPS - 1, g <= GROUPS, True)

        def run(engine, body):
            loop = steps(body)
            with engine.Fori(1, GROUPS // 4 - 1) as i:
                loop(i)
            tail(body)

        with nc.Block() as block:
            @block.sync
            def _(sp):
                def load(g, u, i):
                    wait(sp, s["v_ready"], 4 * (g - 3))
                    sp.dma_start(xs[:, u, :], x_dram[2 * i + u // 2, :, u % 2, :]).then_inc(x_in[u], 16)

                for g in range(4):
                    load(g, g, 0)
                with sp.Fori(1, GROUPS // 4) as i:
                    for u in range(4):
                        load(4 * i + u, u, i)

            @block.tensor
            def _(pe):
                mm = nc.tensor.matmul

                def body(g, u, i, cur, nxt, prev, out):
                    un, uv = (u + 1) % 4, (u + 3) % 4
                    i_n = i + 1 if u == 3 else i
                    for c in range(CH):
                        px = slice(CHUNK * c, CHUNK * c + CHUNK)
                        row = slice(32 * c, 32 * c + 32)
                        if cur:
                            if c < 2:
                                wait(pe, s["wv_done"], 4 * (g - 2) + c + 3)
                            else:
                                pe.wait_ge(s["qk_done"], 4 * g + c - 1)
                            mm(p_kv[c % 2][:, :], n.wk[:, :], window_order(xs[:, u, px]), start=True, stop=True).then_inc(s["k_ready"], 1)
                        if c == 0 and out:
                            pe.wait_ge(s["reduced"], 4 * (g - 1))
                            wait(pe, s["out_biased"], g - 2)
                            mm(p_out[:, 0:WG], proj, agg[:, :], start=True, stop=True).then_inc(s["proj_ready"], 1)
                        if nxt:
                            if c == 0:
                                pe.wait_ge(x_in[un], 16 * (i_n + 1))
                                wait(pe, s["mean_sq_done"], g + 1)
                            last = mm(p_mean[row, :], K("mean32"), window_order(xs[:, un, px]), start=True, stop=True,
                                      tile_position=(0, 32 * c))
                            if c == CH - 1:
                                last.then_inc(s["mean_ready"], 1)
                        if cur and c:
                            score_rows(pe, g, c - 1)
                        if nxt:
                            if c == 0:
                                pe.wait_ge(s["squared"], g + 2)
                                wait(pe, s["var_done"], g + 1)
                            last = mm(p_sq[row, :], K("mean32"), window_order(squares[:, px]), start=True, stop=True,
                                      tile_position=(0, 32 * c))
                            if c == CH - 1:
                                last.then_inc(s["sq_ready"], 1)
                    if cur:
                        score_rows(pe, g, CH - 1)
                    if nxt:
                        pe.wait_ge(s["sums_done"], g + 2)
                        wait(pe, s["q_copied"], g + 1)
                        mm(p_q[:, 0:WG], K("center"), sums[:, un, :], start=True, stop=True).then_inc(s["cent_ready"], 1)
                    for c in range(CH):
                        px = slice(CHUNK * c, CHUNK * c + CHUNK)
                        if prev:
                            if c < 2:
                                if cur:
                                    pe.wait_ge(s["qk_done"], 4 * g + c + 3)
                            else:
                                pe.wait_ge(s["wv_done"], 4 * (g - 1) + c - 1)
                            mm(p_kv[c % 2][:, :], n.wv[:, :], window_order(xs[:, uv, px]), start=True, stop=True).then_inc(s["v_ready"], 1)
                            if c == 0:
                                pe.wait_ge(s["lo_done"], g)
                            wait(pe, s["wide_copied"], 4 * (g - 1) + c)
                            mm(p_w[:, :], spread(c), w_hi[:, uv % 2, :], start=True, stop=False)
                            mm(p_w[:, :], spread(c), w_lo[:, uv % 2, :], start=False, stop=True).then_inc(s["wide_ready"], 1)
                        if nxt and c == 0:
                            pe.wait_ge(s["cent_copied"], g + 2)
                            mm(p_q[:, WG:2 * WG], K("average"), q_square[:, :], start=True, stop=True).then_inc(s["q_var_ready"], 1)
                        if nxt and c == CH - 1:
                            pe.wait_ge(s["q_normed"], g + 2)
                            mm(p_q[:, 2 * WG:3 * WG], n.wq[:, :], q_norm[:, :], start=True, stop=True).then_inc(s["q_ready"], 1)

                def score_rows(pe, g, c):
                    pe.wait_ge(s["qk_done"], 4 * g + c + 1)
                    if c == 0:
                        wait(pe, s["scored"], g)
                    last = mm(p_score[32 * c:32 * c + 32, :], K("head32"), qk[:, c % 2, :], start=True, stop=True,
                              tile_position=(0, 32 * c))
                    last.then_inc(s["scores_ready"], 1)

                run(pe, body)

            @block.scalar
            def _(act):
                A = nc.scalar.activation
                nc.scalar.preload_act_table_set("natural_log_exp_and_others")

                def body(g, u, i, cur, nxt, prev, out):
                    un, uv = (u + 1) % 4, (u + 3) % 4
                    i_n = i + 1 if u == 3 else i
                    if nxt:
                        act.wait_ge(x_in[un], 16 * (i_n + 1))
                        wait(act, s["sq_ready"], g + 1)
                        A(squares[:, :], xs[:, un, :], ACT.Square).then_inc(s["squared"], 1)
                    if out:
                        act.wait_ge(s["proj_ready"], g - 1)
                        wait(act, s["token_done"], g - 2)
                        A(out_b[:, :], p_out[:, 0:WG], ACT.Identity, bias=n.pb[:, :]).then_inc(s["out_biased"], 1)
                    if nxt:
                        act.wait_ge(s["mean_ready"], g + 2)
                        wait(act, s["var_done"], g + 1)
                        A(mean_sq[:, :], p_mean[:, :], ACT.Square).then_inc(s["mean_sq_done"], 1)
                        act.wait_ge(s["cent_ready"], g + 2)
                        wait(act, s["q_normed"], g + 1)
                        A(q_cent[:, :], p_q[:, 0:WG], ACT.Copy, scale=1.0 / WIN)
                        A(q_square[:, :], p_q[:, 0:WG], ACT.Square, scale=1.0 / WIN).then_inc(s["cent_copied"], 1)
                    for c in range(CH):
                        if prev:
                            act.wait_ge(s["wide_ready"], 4 * (g - 1) + c + 1)
                            wait(act, s["wv_done"], 4 * (g - 1) + c - 1)
                            A(w_wide[:, c % 2, :], p_w[:, :], ACT.Copy).then_inc(s["wide_copied"], 1)
                        if c == 0 and cur:
                            act.wait_ge(s["below_done"], g + 1)
                            wait(act, s["ex_rstd_done"], g)
                            wait(act, s["total_done"], g)
                            A(ex[:, :], below[:, :], ACT.Exp).then_inc(s["exp_done"], 1)
                        if c == 0 and nxt:
                            act.wait_ge(s["var_clamped"], g + 2)
                            wait(act, s["rstd_done"], g + 1)
                            A(var_log[:, :], var_pos[:, :], ACT.Ln, bias=K("eps")).then_inc(s["var_logged"], 1)
                            act.wait_ge(s["var_logged"], g + 2)
                            wait(act, s["ex_rstd_done"], g)
                            wait(act, s["scored"], g)
                            A(rstd[:, un % 2, :], var_log[:, :], ACT.Exp, scale=-0.5).then_inc(s["rstd_done"], 1)
                        if c == 1 and nxt:
                            act.wait_ge(s["q_var_ready"], g + 2)
                            wait(act, s["q_rstd_done"], g + 1)
                            A(q_log[:, :], p_q[:, WG:2 * WG], ACT.Ln, bias=K("eps")).then_inc(s["q_log_done"], 1)
                            act.wait_ge(s["q_log_done"], g + 2)
                            A(q_rstd[:, :], q_log[:, :], ACT.Exp, scale=-0.5).then_inc(s["q_rstd_done"], 1)
                    if cur:
                        act.wait_ge(s["weight_done"], g + 1)
                        wait(act, s["wide_ready"], 4 * (g - 1))
                        A(w_hi[:, u % 2, :], weight[:, :], ACT.Copy).then_inc(s["hi_done"], 1)
                    if nxt:
                        act.wait_ge(s["q_ready"], g + 2)
                        wait(act, s["qk_done"], 4 * g)
                        A(qs[:, un % 2, :], p_q[:, 2 * WG:3 * WG], ACT.Identity, bias=n.bq[:, :]).then_inc(s["q_copied"], 1)

                run(act, body)

            @block.vector
            def _(dve):
                V = nc.vector

                def body(g, u, i, cur, nxt, prev, out):
                    uv = (u + 3) % 4
                    if cur:
                        dve.wait_ge(s["q_copied"], g + 1)
                        for c in range(CH):
                            dve.wait_ge(s["k_ready"], 4 * g + c + 1)
                            wait(dve, s["scores_ready"], 4 * g + c - 1)
                            q = chunk_windows(qs[:, u % 2, :], c).unsqueeze(3).broadcast_to([P, 16, 2, WIN])
                            V.tensor_tensor(qk[:, c % 2, :].rearrange("p (col row k) -> p col row k", col=16, row=2),
                                            p_kv[c % 2][:, :].rearrange("p (col row k) -> p col row k", col=16, row=2), q, ALU.mult).then_inc(s["qk_done"], 1)
                    if out:
                        dve.wait_ge(s["out_biased"], g - 1)
                        pair = 2 * i + (u - 2) // 2
                        V.scalar_tensor_tensor(n.tokens[:, pair, WG * (u % 2):WG * (u % 2) + WG], sums[:, (u + 2) % 4, :], 1.0 / WIN,
                                               out_b[:, :], ALU.mult, ALU.add).then_inc(s["token_done"], 1)
                    if cur:
                        dve.wait_ge(s["scores_ready"], 4 * g + 4)
                        dve.wait_ge(s["rstd_done"], g + 1)
                        V.tensor_tensor(score[:, :], p_score[:, :], rstd[:, u % 2, :], ALU.mult).then_inc(s["scored"], 1)
                        dve.wait_ge(s["scored"], g + 1)
                        V.tensor_reduce(top[:, :], by_window(score[:, :]), X, ALU.max).then_inc(s["top_done"], 1)
                        dve.wait_ge(s["top_done"], g + 1)
                        wait(dve, s["exp_done"], g)
                        V.tensor_tensor(by_window(below[:, :]), by_window(score[:, :]), top[:, :].unsqueeze(2).broadcast_to([P, WC, WIN]),
                                        ALU.subtract).then_inc(s["below_done"], 1)
                    if nxt:
                        dve.wait_ge(s["mean_sq_done"], g + 2)
                        dve.wait_ge(s["sq_ready"], g + 2)
                        wait(dve, s["var_clamped"], g + 1)
                        V.tensor_tensor(var[:, :], p_sq[:, :], mean_sq[:, :], ALU.subtract).then_inc(s["var_done"], 1)
                        dve.wait_ge(s["var_done"], g + 2)
                        wait(dve, s["var_logged"], g + 1)
                        V.tensor_scalar(var_pos[:, :], var[:, :], 0.0, None, ALU.max).then_inc(s["var_clamped"], 1)

                    def gather(c):
                        dve.wait_ge(s["wv_done"], 4 * (g - 1) + c + 1)
                        if c == 0:
                            wait(dve, s["proj_ready"], g - 1)
                        V.tensor_reduce(chunk_windows(agg[:, :], c), wv[:, c % 2, :].rearrange("p (col row k) -> p col row k", col=16, row=2), X, ALU.add).then_inc(s["reduced"], 1)

                    for c in range(CH):
                        if prev:
                            dve.wait_ge(s["v_ready"], 4 * (g - 1) + c + 1)
                            dve.wait_ge(s["wide_copied"], 4 * (g - 1) + c + 1)
                            wait(dve, s["reduced"], 4 * (g - 1) + c - 1)
                            V.tensor_tensor(wv[:, c % 2, :], p_kv[c % 2][:, :], w_wide[:, c % 2, :], ALU.mult).then_inc(s["wv_done"], 1)
                            if c:
                                gather(c - 1)
                        if c == 1 and cur:
                            dve.wait_ge(s["exp_done"], g + 1)
                            V.tensor_reduce(total[:, :], by_window(ex[:, :]), X, ALU.add).then_inc(s["total_done"], 1)
                            dve.wait_ge(s["total_done"], g + 1)
                            wait(dve, s["weight_done"], g)
                            V.reciprocal(inv[:, :], total[:, :]).then_inc(s["inv_done"], 1)
                    if prev:
                        gather(CH - 1)

                run(dve, body)

            @block.gpsimd
            def _(pool):
                G = nc.gpsimd

                def body(g, u, i, cur, nxt, prev, out):
                    un = (u + 1) % 4
                    i_n = i + 1 if u == 3 else i
                    if nxt:
                        pool.wait_ge(x_in[un], 16 * (i_n + 1))
                        a = xs[:, un, :].rearrange("p (y h row x) -> p y h row x", h=2, row=2, x=64)
                        t1 = tree1[:, :].rearrange("p (y row x) -> p y row x", row=2, x=64)
                        wait(pool, s["sums_2"], g + 1)
                        G.tensor_tensor(tree1[:, :].rearrange("p (y rowx) -> p y rowx", y=8), xs[:, un, :].rearrange("p (y h rowx) -> p y h rowx", h=2, rowx=128)[:, :, 0, :],
                                        xs[:, un, :].rearrange("p (y h rowx) -> p y h rowx", h=2, rowx=128)[:, :, 1, :], ALU.add).then_inc(s["sums_1"], 1)
                        pool.wait_ge(s["sums_1"], g + 2)
                        wait(pool, s["sums_3"], g + 1)
                        G.tensor_tensor(tree2[:, :].rearrange("p (y x) -> p y x", y=8), t1[:, :, 0, :], t1[:, :, 1, :], ALU.add).then_inc(s["sums_2"], 1)
                        pool.wait_ge(s["sums_2"], g + 2)
                        wait(pool, s["sums_done"], g + 1)
                        t2 = tree2[:, :].rearrange("p (col h x) -> p col h x", h=2, x=2)
                        G.tensor_tensor(tree3[:, :].rearrange("p (col x) -> p col x", x=2), t2[:, :, 0, :], t2[:, :, 1, :], ALU.add).then_inc(s["sums_3"], 1)
                        pool.wait_ge(s["sums_3"], g + 2)
                        wait(pool, s["token_done"], g - 2)
                        t3 = tree3[:, :].rearrange("p (col x) -> p col x", x=2)
                        G.tensor_tensor(sums[:, un, :], t3[:, :, 0], t3[:, :, 1], ALU.add).then_inc(s["sums_done"], 1)
                    if cur:
                        pool.wait_ge(s["exp_done"], g + 1)
                        wait(pool, s["weight_done"], g)
                        G.tensor_tensor(ex_rstd[:, :], ex[:, :], rstd[:, u % 2, :], ALU.mult).then_inc(s["ex_rstd_done"], 1)
                    if nxt:
                        pool.wait_ge(s["q_rstd_done"], g + 2)
                        wait(pool, s["q_ready"], g + 1)
                        G.tensor_tensor(q_norm[:, :], q_cent[:, :], q_rstd[:, :], ALU.mult).then_inc(s["q_normed"], 1)
                    if cur:
                        pool.wait_ge(s["inv_done"], g + 1)
                        pool.wait_ge(s["ex_rstd_done"], g + 1)
                        wait(pool, s["lo_done"], g)
                        G.tensor_tensor(by_window(weight[:, :]), by_window(ex_rstd[:, :]), inv[:, :].unsqueeze(2).broadcast_to([P, WC, WIN]),
                                        ALU.mult).then_inc(s["weight_done"], 1)
                        pool.wait_ge(s["hi_done"], g + 1)
                        wait(pool, s["wide_ready"], 4 * (g - 1))
                        G.tensor_tensor(w_lo[:, u % 2, :], weight[:, :], w_hi[:, u % 2, :], ALU.subtract).then_inc(s["lo_done"], 1)

                run(pool, body)


def mixing(nc, n):
    with ExitStack() as ctx:
        def sb(name, shape, dt=FP32):
            return ctx.enter_context(nc.sbuf_tensor(name, shape, dt))

        bank = [ctx.enter_context(nc.psum_tensor(f"mix{k}", [P, 512], FP32)) for k in range(8)]
        T3 = TOK // P
        R = 2 * T3
        p_cent, p_var, p_cent2, p_var2, p_kv0, p_kv1, p_q, p_kvkv = bank
        xn = sb("xn", [P, 4, TOK])
        sq1, log1, rstd1 = sb("sq1", [P, TOK]), sb("log1", [P, TOK]), sb("rstd1", [P, TOK])
        sq2, log2, rstd2 = sb("sq2", [P, TOK]), sb("log2", [P, TOK]), sb("rstd2", [P, TOK])
        xn2 = sb("xn2", [P, TOK])
        kvb = sb("kvb", [P, T3, 4 * C])
        kv_sq = sb("kv_sq", [P, T3, 4 * C])
        kv_ss, kv_log, kv_std, kv_eased, kv_inv = (sb(x, [P, T3 * C]) for x in ("kv_ss", "kv_log", "kv_std", "kv_eased", "kv_inv"))
        kv_n, kv_w, kv_f = (sb(x, [P, T3, 4 * C]) for x in ("kv_n", "kv_w", "kv_f"))
        kv_m = sb("kv_m", [P, P])
        mixed = sb("mixed", [P, 2, TOK])
        q_sb, ret, gel = sb("q_sb", [P, TOK]), sb("ret", [P, TOK]), sb("gel", [P, TOK])
        rows = sb("rows", [P, 2, 2, R, ROW], U32)
        logits, eq, cand, lower = (sb(x, [P, R, E_N]) for x in ("logits", "eq", "cand", "lower"))
        eq2, cand2 = sb("eq2", [P, R, E_N]), sb("cand2", [P, R, E_N])
        top1, top2, no1, no2 = (sb(x, [P, R]) for x in ("top1", "top2", "no1", "no2"))
        hot = sb("hot", [P, 2, 2, R, E_N])
        hot16 = sb("hot16", [P, 2, R, E_N], FP16)
        gap = sb("gap", [P, 2, R])
        gap_exp, one_more = sb("gap_exp", [P, R]), sb("one_more", [P, R])
        gate = sb("gate_v", [P, 2, R])
        seat, seat_hot = sb("seat", [P, R, E_N]), sb("seat_hot", [P, 2, R, E_N])
        place = sb("place", [P, 2, R])
        place_i = sb("place_i", [P, 2, 2, R], U32)
        place_no = sb("place_no", [P, 2, 2, R])
        names = ("a_cent a_sq a_var a_log a_rstd a_xn a_added b_kv b_bias b_sq b_ss b_log b_std b_eased b_inv b_n b_w b_f "
                 "c_q c_qb c_kv c_kvm c_out c_ret c_proj c_gelu c_added d_cent d_sq d_var d_log d_rstd d_xn d_logits d_xt d_ht "
                 "d_hi d_lo d_hcopy d_biased d_top1 d_eq d_cand d_no1 d_hot1 d_lower d_top2 d_eq2 d_cand2 d_no2 d_hot2 d_hot16 d_gap "
                 "e_rank e_exp e_more e_gate1 e_gate2 e_seat e_seathot e_place e_placei e_meta e_base e_start e_meta_no e_go")
        s = {name: n.sem("m_" + name) for name in names.split()}
        sent = [n.sem(f"m_sent{k}") for k in range(2)]
        W = lambda name, rows=P: n.w[0:rows, W_AT[name][0]:W_AT[name][1]]
        K = lambda name: n.f[:, F32_AT[name][0]:F32_AT[name][1]]
        H16 = lambda name: n.h[:, F16_AT[name][0]:F16_AT[name][1]]
        STEPS = PAIRS + 4

        def run(engine, body):
            def static(j):
                body(j, j % 4, [0 <= j - k < PAIRS for k in range(5)])

            for j in range(8):
                static(j)
            with engine.Fori(2, PAIRS // 4) as i:
                for u in range(4):
                    body(4 * i + u, u, [True] * 5)
            for j in range(PAIRS, STEPS):
                static(j)

        def sent_by(d, u):
            k = d // 2 if isinstance(d, int) else (d - (u % 2)) // 2
            return 16 * 2 * R * k

        with nc.Block() as block:
            @block.tensor
            def _(pe):
                mm = nc.tensor.matmul

                def body(j, u, on):
                    a, b, c, d, e = (j - k for k in range(5))
                    if on[0]:
                        wait(pe, s["a_xn"], a)
                        mm(p_cent[:, 0:TOK], K("center"), n.tokens[:, a, :], start=True, stop=True).then_inc(s["a_cent"], 1)
                    if on[1]:
                        pe.wait_ge(s["a_xn"], b + 1)
                        wait(pe, s["b_bias"], b)
                        for t in range(T3):
                            out = (p_kv0 if t < 2 else p_kv1)[:, 256 * (t % 2):256 * (t % 2) + 256]
                            last = mm(out, xn[:, (u - 1) % 4, P * t:P * t + P], n.mkv[:, :, :, :].rearrange("p a b c -> p (a b c)"),
                                      start=True, stop=True)
                        last.then_inc(s["b_kv"], 1)
                    if on[2]:
                        wait(pe, s["c_ret"], c)
                        mm(p_q[:, 0:TOK], W("mq"), xn[:, (u - 2) % 4, :], start=True, stop=True).then_inc(s["c_q"], 1)
                        pe.wait_ge(s["b_f"], c + 1)
                        wait(pe, s["c_gelu"], c)
                        for t in range(T3):
                            last = mm(p_kvkv[:, 0:P], kv_f[:, t, 0:P], kv_f[:, t, P:2 * P], start=(t == 0), stop=(t == T3 - 1))
                        last.then_inc(s["c_kv"], 1)
                    if on[3]:
                        pe.wait_ge(s["c_added"], d + 1)
                        wait(pe, s["d_lo"], d)
                        mm(p_cent2[:, 0:TOK], K("center"), mixed[:, (u - 3) % 2, :], start=True, stop=True).then_inc(s["d_cent"], 1)
                    if on[4]:
                        v = u % 2
                        pe.wait_ge(s["d_hot16"], e + 1)
                        pe.wait_ge(s["d_biased"], e + 1)
                        hots = hot16[:, v, :, :].rearrange("p r e -> p (r e)")
                        mm(p_var2[:, 0:R * E_N], H16("before16"), hots, start=True, stop=False, skip_group_check=True)
                        for k in range(1, R):
                            mm(p_var2[:, E_N * k:R * E_N], H16("ones16"), hots[:, 0:(R - k) * E_N], start=False, stop=(k == R - 1),
                               skip_group_check=True)
                        for k in range(R):
                            last = mm(p_var2[:, R * E_N:(R + 1) * E_N], H16("ones16"), hots[:, E_N * k:E_N * k + E_N], start=False,
                                      stop=(k == R - 1), skip_group_check=True)
                        last.then_inc(s["e_rank"], 1)
                    if on[0]:
                        pe.wait_ge(s["a_sq"], a + 1)
                        wait(pe, s["d_hcopy"], a - 3)
                        mm(p_var[:, 0:TOK], K("average"), sq1[:, :], start=True, stop=True).then_inc(s["a_var"], 1)
                    if on[2]:
                        pe.wait_ge(s["c_qb"], c + 1)
                        pe.wait_ge(s["c_kvm"], c + 1)
                        mm(p_q[:, 0:TOK], kv_m[:, :], q_sb[:, :], start=True, stop=True).then_inc(s["c_out"], 1)
                    if on[3]:
                        pe.wait_ge(s["d_sq"], d + 1)
                        if on[4]:
                            pe.wait_ge(s["e_base"], e + 1)
                            pe.wait_ge(s["e_seat"], e + 1)
                        mm(p_var2[:, 0:TOK], K("average"), sq2[:, :], start=True, stop=True).then_inc(s["d_var"], 1)
                    if on[2]:
                        pe.wait_ge(s["c_ret"], c + 1)
                        mm(p_kvkv[:, 0:TOK], W("mproj"), ret[:, :], start=True, stop=True).then_inc(s["c_proj"], 1)
                    if on[3]:
                        pe.wait_ge(s["d_xn"], d + 1)
                        for t in range(T3):
                            last = mm(p_var2[:, 32 * t:32 * t + 32], xn2[:, P * t:P * t + P], W("gate"), start=True, stop=True)
                        last.then_inc(s["d_logits"], 1)
                        for t in range(T3):
                            last = nc.tensor.transpose(p_cent2[:, P * t:P * t + P], xn2[:, P * t:P * t + P], K("ident"))
                        last.then_inc(s["d_xt"], 1)
                        wait(pe, s["a_log"], a + 1 if on[0] else PAIRS)
                        for t in range(T3):
                            last = nc.tensor.transpose(p_var[:, P * t:P * t + P], mixed[:, (u - 3) % 2, P * t:P * t + P], K("ident"))
                        last.then_inc(s["d_ht"], 1)

                run(pe, body)

            @block.scalar
            def _(act):
                A = nc.scalar.activation
                nc.scalar.preload_act_table_set("natural_log_exp_and_others")

                def body(j, u, on):
                    a, b, c, d, e = (j - k for k in range(5))
                    v = u % 2
                    nc.scalar.preload_act_table_set("natural_log_exp_and_others")
                    if on[0]:
                        act.wait_ge(s["a_cent"], a + 1)
                        wait(act, s["a_var"], a)
                        A(sq1[:, :], p_cent[:, 0:TOK], ACT.Square).then_inc(s["a_sq"], 1)
                    if on[2]:
                        act.wait_ge(s["c_q"], c + 1)
                        wait(act, s["c_out"], c)
                        A(q_sb[:, :], p_q[:, 0:TOK], ACT.Identity, bias=W("mq_b")).then_inc(s["c_qb"], 1)
                    if on[3]:
                        act.wait_ge(s["d_cent"], d + 1)
                        wait(act, s["d_var"], d)
                        A(sq2[:, :], p_cent2[:, 0:TOK], ACT.Square).then_inc(s["d_sq"], 1)
                    if on[4]:
                        act.wait_ge(s["d_gap"], e + 1)
                        wait(act, s["e_gate2"], e)
                        A(gap_exp[:, :], gap[:, v, :], ACT.Exp).then_inc(s["e_exp"], 1)
                    if on[0]:
                        act.wait_ge(s["a_var"], a + 1)
                        wait(act, s["a_rstd"], a)
                        A(log1[:, :], p_var[:, 0:TOK], ACT.Ln, bias=K("eps")).then_inc(s["a_log"], 1)
                        act.wait_ge(s["a_log"], a + 1)
                        wait(act, s["a_xn"], a)
                        A(rstd1[:, :], log1[:, :], ACT.Exp, scale=-0.5).then_inc(s["a_rstd"], 1)
                    if on[1]:
                        act.wait_ge(s["b_bias"], b + 1)
                        wait(act, s["b_ss"], b)
                        A(kv_sq[:, :, :], kvb[:, :, :], ACT.Square).then_inc(s["b_sq"], 1)
                    if on[3]:
                        act.wait_ge(s["d_var"], d + 1)
                        wait(act, s["d_rstd"], d)
                        A(log2[:, :], p_var2[:, 0:TOK], ACT.Ln, bias=K("eps")).then_inc(s["d_log"], 1)
                        act.wait_ge(s["d_log"], d + 1)
                        wait(act, s["d_xn"], d)
                        A(rstd2[:, :], log2[:, :], ACT.Exp, scale=-0.5).then_inc(s["d_rstd"], 1)
                    if on[1]:
                        act.wait_ge(s["b_ss"], b + 1)
                        wait(act, s["b_std"], b)
                        A(kv_log[:, :], kv_ss[:, :], ACT.Ln, bias=K("tiny"), scale=1.0 / 3.0).then_inc(s["b_log"], 1)
                        act.wait_ge(s["b_log"], b + 1)
                        wait(act, s["b_eased"], b)
                        A(kv_std[:, :], kv_log[:, :], ACT.Exp, scale=0.5).then_inc(s["b_std"], 1)
                    if on[3]:
                        act.wait_ge(s["d_xt"], d + 1)
                        wait(act, sent[v ^ 1], sent_by(d, u - 3))
                        x3 = p_cent2[:, 0:TOK].rearrange("p (ts c) -> p ts c", c=C)
                        for k in range(2):
                            last = A(rows[:, v ^ 1, k, :, 0:C // 2].bitcast(FP16), x3, ACT.Copy, scale=X_SCALE)
                        last.then_inc(s["d_hi"], 1)
                        act.wait_ge(s["d_ht"], d + 1)
                        A(n.tokens_t[:, bass.ds(d * R, R), :].rearrange("p (s t) c -> p t s c", s=2),
                          p_var[:, 0:TOK].rearrange("p (t s c) -> p t s c", t=T3, s=2), ACT.Copy).then_inc(s["d_hcopy"], 1)
                    if on[2]:
                        act.wait_ge(s["c_proj"], c + 1)
                        wait(act, s["c_added"], c)
                        A(gel[:, :], p_kvkv[:, 0:TOK], ACT.Gelu, bias=W("mproj_b")).then_inc(s["c_gelu"], 1)

                run(act, body)

            @block.vector
            def _(dve):
                V = nc.vector
                V.tensor_copy(n.list_end[:, 1, :], K("list_base"))
                V.tensor_copy(place_no[:, 1, :, :], K("row_no").rearrange("p (k r) -> p k r", k=2)).then_inc(s["e_start"], 1)
                dve.wait_ge(s["e_start"], 1)

                def body(j, u, on):
                    a, b, c, d, e = (j - k for k in range(5))
                    v = u % 2
                    w = v ^ 1
                    if on[1]:
                        dve.wait_ge(s["b_kv"], b + 1)
                        wait(dve, s["b_n"], b)
                        wait(dve, s["b_sq"], b)
                        bias = n.mkv_b[:, :, :, :].rearrange("p a b c -> p (a b c)").unsqueeze(1)
                        V.tensor_tensor(kvb[:, 0:2, :], p_kv0[:, :].rearrange("p (t c) -> p t c", t=2), bias.broadcast_to([P, 2, 4 * C]), ALU.add)
                        V.tensor_tensor(kvb[:, 2:3, :], p_kv1[:, 0:256].rearrange("p (t c) -> p t c", t=1), bias, ALU.add).then_inc(s["b_bias"], 1)
                    if on[2]:
                        dve.wait_ge(s["c_kv"], c + 1)
                        wait(dve, s["c_out"], c)
                        V.tensor_tensor(kv_m[:, :], p_kvkv[:, 0:P], K("mask4"), ALU.mult).then_inc(s["c_kvm"], 1)
                    if on[4]:
                        dve.wait_ge(s["e_rank"], e + 1)
                        wait(dve, s["e_seathot"], e)
                        wait(dve, s["e_base"], e)
                        V.tensor_tensor(seat[:, :, :], p_var2[:, 0:R * E_N].rearrange("p (r e) -> p r e", r=R),
                                        n.list_end[:, w, :].unsqueeze(1).broadcast_to([P, R, E_N]), ALU.add).then_inc(s["e_seat"], 1)
                        V.tensor_tensor(n.list_end[:, v, :], p_var2[:, R * E_N:(R + 1) * E_N], n.list_end[:, w, :], ALU.add).then_inc(s["e_base"], 1)
                        dve.wait_ge(s["e_seat"], e + 1)
                        wait(dve, s["e_place"], e)
                        for k in range(2):
                            last = V.tensor_tensor(seat_hot[:, k, :, :], seat[:, :, :], hot[:, v, k, :, :], ALU.mult)
                        last.then_inc(s["e_seathot"], 1)
                        dve.wait_ge(s["e_seathot"], e + 1)
                        wait(dve, s["e_placei"], e)
                        V.tensor_reduce(place[:, :, :], seat_hot[:, :, :, :], X, ALU.add).then_inc(s["e_place"], 1)
                        dve.wait_ge(s["e_place"], e + 1)
                        wait(dve, sent[v], sent_by(e, u))
                        V.tensor_copy(place_i[:, v, :, :], place[:, :, :]).then_inc(s["e_placei"], 1)
                        dve.wait_ge(s["e_exp"], e + 1)
                        wait(dve, s["e_gate1"], e)
                        V.tensor_scalar(one_more[:, :], gap_exp[:, :], 1.0, None, ALU.add).then_inc(s["e_more"], 1)
                        dve.wait_ge(s["e_more"], e + 1)
                        wait(dve, s["e_meta"], e)
                        V.reciprocal(gate[:, 0, :], one_more[:, :]).then_inc(s["e_gate1"], 1)
                        dve.wait_ge(s["e_gate1"], e + 1)
                        V.tensor_tensor(gate[:, 1, :], gate[:, 0, :], gap_exp[:, :], ALU.mult).then_inc(s["e_gate2"], 1)
                        dve.wait_ge(s["e_gate2"], e + 1)
                        wait(dve, s["e_meta_no"], e)
                        V.tensor_copy(rows[:, v, :, :, C:C + 1].rearrange("p k r o -> p k (r o)"), place_no[:, w, :, :])
                        V.tensor_scalar(rows[:, v, :, :, C + 1:C + 2].rearrange("p k r o -> p k (r o)").bitcast(FP32), gate[:, :, :],
                                        1.0 / (X_SCALE * W_SCALE), None, ALU.mult).then_inc(s["e_meta"], 1)
                        V.tensor_scalar(place_no[:, v, :, :], place_no[:, w, :, :], float(2 * TOK), None, ALU.add).then_inc(s["e_meta_no"], 1)
                    if on[0]:
                        dve.wait_ge(s["a_rstd"], a + 1)
                        wait(dve, s["c_ret"], a - 3)
                        wait(dve, s["a_added"], a - 3)
                        V.tensor_tensor(xn[:, u, :], p_cent[:, 0:TOK], rstd1[:, :], ALU.mult).then_inc(s["a_xn"], 1)
                    if on[1]:
                        dve.wait_ge(s["b_sq"], b + 1)
                        wait(dve, s["b_log"], b)
                        V.tensor_reduce(kv_ss[:, :], kv_sq[:, :, :].rearrange("p t (g k) -> p (t g) k", k=4), X, ALU.add).then_inc(s["b_ss"], 1)
                    if on[2]:
                        dve.wait_ge(s["c_out"], c + 1)
                        wait(dve, s["c_proj"], c)
                        V.tensor_tensor(ret[:, :], p_q[:, 0:TOK], xn[:, (u - 2) % 4, :], ALU.add).then_inc(s["c_ret"], 1)
                    if on[3]:
                        dve.wait_ge(s["d_rstd"], d + 1)
                        wait(dve, s["d_xt"], d)
                        V.tensor_tensor(xn2[:, :], p_cent2[:, 0:TOK], rstd2[:, :], ALU.mult).then_inc(s["d_xn"], 1)
                    if on[1]:
                        dve.wait_ge(s["b_std"], b + 1)
                        wait(dve, s["b_inv"], b)
                        V.tensor_scalar(kv_eased[:, :], kv_std[:, :], EPS, None, ALU.add).then_inc(s["b_eased"], 1)
                        dve.wait_ge(s["b_eased"], b + 1)
                        wait(dve, s["b_n"], b)
                        V.reciprocal(kv_inv[:, :], kv_eased[:, :]).then_inc(s["b_inv"], 1)
                    if on[3]:
                        def chain(name):
                            dve.wait_ge(s[name], d + 1)

                        dve.wait_ge(s["d_logits"], d + 1)
                        wait(dve, s["d_lower"], d)
                        V.tensor_tensor(logits[:, :, :].rearrange("p r e -> p (r e)").rearrange("p (t x) -> p t x", t=T3),
                                        p_var2[:, 0:R * E_N].rearrange("p (t x) -> p t x", t=T3),
                                        W("gate_b").unsqueeze(1).broadcast_to([P, T3, 2 * E_N]), ALU.add).then_inc(s["d_biased"], 1)
                        wide = lambda t: t.unsqueeze(2).broadcast_to([P, R, E_N])
                        rank = K("rank_e").unsqueeze(1).broadcast_to([P, R, E_N])
                        chain("d_biased")
                        wait(dve, s["d_gap"], d)
                        V.tensor_reduce(top1[:, :], logits[:, :, :], X, ALU.max).then_inc(s["d_top1"], 1)
                        chain("d_top1")
                        wait(dve, s["d_cand"], d)
                        V.tensor_tensor(eq[:, :, :], logits[:, :, :], wide(top1[:, :]), ALU.is_equal).then_inc(s["d_eq"], 1)
                        chain("d_eq")
                        wait(dve, s["d_no1"], d)
                        V.tensor_tensor(cand[:, :, :], eq[:, :, :], rank, ALU.mult).then_inc(s["d_cand"], 1)
                        chain("d_cand")
                        wait(dve, s["d_hot1"], d)
                        V.tensor_reduce(no1[:, :], cand[:, :, :], X, ALU.max).then_inc(s["d_no1"], 1)
                        chain("d_no1")
                        wait(dve, s["e_seathot"], d - 1)
                        V.tensor_tensor(hot[:, w, 0, :, :], rank, wide(no1[:, :]), ALU.is_equal).then_inc(s["d_hot1"], 1)
                        chain("d_hot1")
                        wait(dve, s["d_eq2"], d)
                        V.scalar_tensor_tensor(lower[:, :, :], hot[:, w, 0, :, :], -1e30, logits[:, :, :], ALU.mult, ALU.add).then_inc(s["d_lower"], 1)
                        chain("d_lower")
                        V.tensor_reduce(top2[:, :], lower[:, :, :], X, ALU.max).then_inc(s["d_top2"], 1)
                        chain("d_top2")
                        wait(dve, s["d_cand2"], d)
                        V.tensor_tensor(eq2[:, :, :], lower[:, :, :], wide(top2[:, :]), ALU.is_equal).then_inc(s["d_eq2"], 1)
                        chain("d_eq2")
                        wait(dve, s["d_no2"], d)
                        V.tensor_tensor(cand2[:, :, :], eq2[:, :, :], rank, ALU.mult).then_inc(s["d_cand2"], 1)
                        chain("d_cand2")
                        wait(dve, s["d_hot2"], d)
                        V.tensor_reduce(no2[:, :], cand2[:, :, :], X, ALU.max).then_inc(s["d_no2"], 1)
                        chain("d_no2")
                        V.tensor_tensor(hot[:, w, 1, :, :], rank, wide(no2[:, :]), ALU.is_equal).then_inc(s["d_hot2"], 1)
                        wait(dve, s["e_exp"], d - 1)
                        V.tensor_tensor(gap[:, w, :], top2[:, :], top1[:, :], ALU.subtract).then_inc(s["d_gap"], 1)
                        chain("d_hot2")
                        wait(dve, s["e_rank"], d - 1)
                        V.tensor_tensor(hot16[:, w, :, :], hot[:, w, 0, :, :], hot[:, w, 1, :, :], ALU.add).then_inc(s["d_hot16"], 1)
                        dve.wait_ge(s["d_hi"], d + 1)
                        for k in range(2):
                            last = V.scalar_tensor_tensor(rows[:, w, k, :, C // 2:C].bitcast(FP16), p_cent2[:, 0:TOK].rearrange("p (ts c) -> p ts c", c=C),
                                                          X_SCALE, rows[:, w, k, :, 0:C // 2].bitcast(FP16), ALU.mult, ALU.subtract)
                        last.then_inc(s["d_lo"], 1)

                run(dve, body)

            @block.gpsimd
            def _(pool):
                G = nc.gpsimd

                def body(j, u, on):
                    a, b, c, d, e = (j - k for k in range(5))
                    v = u % 2
                    if on[4]:
                        pool.wait_ge(s["e_meta"], e + 1)
                        pool.wait_ge(s["e_placei"], e + 1)
                        pool.wait_ge(s["d_lo"], e + 1)
                        pool.sem_inc(s["e_go"], 1)
                        for k in range(2):
                            for r in range(R):
                                G.indirect_dma_start(out=n.lists, out_offset=bass.IndirectOffsetOnAxis(ap=place_i[:, v, k, r:r + 1], axis=0),
                                                     in_=rows[:, v, k, r, :], in_offset=None).then_inc(sent[v], 16)
                    if on[0]:
                        pool.wait_ge(s["e_start"], 1)
                        pool.wait_ge(s["a_xn"], a + 1)
                        G.tensor_tensor(n.tokens[:, a, :], n.tokens[:, a, :], xn[:, u, :], ALU.add).then_inc(s["a_added"], 1)
                    if on[1]:
                        pool.wait_ge(s["b_inv"], b + 1)
                        wait(pool, s["b_w"], b)
                        four = lambda t: t.rearrange("p t (g k) -> p (t g) k", k=4)
                        G.tensor_tensor(four(kv_n[:, :, :]), four(kvb[:, :, :]), kv_inv[:, :].unsqueeze(2).broadcast_to([P, T3 * C, 4]),
                                        ALU.mult).then_inc(s["b_n"], 1)
                        pool.wait_ge(s["b_n"], b + 1)
                        wait(pool, s["b_f"], b)
                        G.tensor_tensor(kv_w[:, :, :], kv_n[:, :, :], W("kv_ln_w").unsqueeze(1).broadcast_to([P, T3, 4 * C]), ALU.mult).then_inc(s["b_w"], 1)
                        pool.wait_ge(s["b_w"], b + 1)
                        wait(pool, s["c_kv"], b)
                        G.tensor_tensor(kv_f[:, :, :], kv_w[:, :, :], W("kv_ln_b").unsqueeze(1).broadcast_to([P, T3, 4 * C]), ALU.add).then_inc(s["b_f"], 1)
                    if on[2]:
                        pool.wait_ge(s["e_start"], 1)
                        pool.wait_ge(s["c_gelu"], c + 1)
                        pool.wait_ge(s["a_added"], c + 1)
                        wait(pool, s["d_ht"], c - 1)
                        G.tensor_tensor(mixed[:, u % 2, :], n.tokens[:, c, :], gel[:, :], ALU.add).then_inc(s["c_added"], 1)

                run(pool, body)
                for k in range(2):
                    pool.wait_ge(sent[k], 16 * 2 * R * (PAIRS // 2))


def experts(nc, n):
    with ExitStack() as ctx:
        def sb(name, shape, dt=FP32):
            return ctx.enter_context(nc.sbuf_tensor(name, shape, dt))

        J = 4
        GROUPS_E = -(-RUN_T // (2 * J)) * 2
        pad = sb("pad", [P, ROW], U32)
        count, tiles0, tiles = sb("count", [P, E_N]), sb("tiles0", [P, E_N]), sb("tiles", [P, E_N])
        cum = [sb(f"cum{k}", [P, E_N]) for k in range(5)]
        past, past_tiles = sb("past", [P, J, E_N]), sb("past_tiles", [P, J, E_N])
        first, which, clipped, tile_at, tile_in = (sb(x, [P, J]) for x in ("first", "which", "clipped", "tile_at", "tile_in"))
        plan = sb("plan_cols", [P, 2, J], I32)
        ends = sb("ends", [1, E_N], I32)
        plan_row = sb("plan_row", [1, 2, J * P], I32)
        rows = sb("x_rows", [P, 2, J, ROW], U32)
        xt = sb("xt", [P, 2, J * P], FP16)
        act1 = sb("act1", [P, 2, J * P])
        hid = sb("hid", [P, 2, J * P])
        y = sb("y", [P, 2, J, C])
        p_xt = [ctx.enter_context(nc.psum_tensor(f"p_xt{k}", [P, J * P], FP16)) for k in range(2)]
        p_h1 = [ctx.enter_context(nc.psum_tensor(f"p_h1_{k}", [P, J * P], FP32)) for k in range(2)]
        p_h2 = [ctx.enter_context(nc.psum_tensor(f"p_h2_{k}", [P, J * P], FP32)) for k in range(2)]
        p_y = [ctx.enter_context(nc.psum_tensor(f"p_y{k}", [P, J * C], FP32)) for k in range(2)]
        names = ("pad_zero pad_done planned plan_out plan_in pads_sent x_turned x_copied h1_ready h2_ready silu_done hid_done y_ready y_done y_go")
        s = {name: n.sem("x_" + name) for name in names.split()}
        rows_in = [n.sem(f"x_rows_in{k}") for k in range(2)]
        y_sent = [n.sem(f"x_y_sent{k}") for k in range(2)]
        K = lambda name: n.f[:, F32_AT[name][0]:F32_AT[name][1]]

        with nc.Block() as block:
            @block.gpsimd
            def _(pool):
                nc.gpsimd.memset(pad[:, :], 0).then_inc(s["pad_zero"], 1)

            @block.vector
            def _(dve):
                V = nc.vector
                step = [0]

                def then(op):
                    step[0] += 1
                    op.then_inc(s["planned"], 1)
                    dve.wait_ge(s["planned"], step[0])

                dve.wait_ge(s["pad_zero"], 1)
                V.tensor_copy(pad[:, C:C + 1], K("pad_place")).then_inc(s["pad_done"], 1)
                then(V.tensor_copy(ends[:, :], n.list_end[0:1, 1, :]))
                then(V.tensor_tensor(count[:, :], n.list_end[:, 1, :], K("list_base"), ALU.subtract))
                then(V.tensor_scalar(tiles0[:, :], count[:, :], 1.0 / P, float(P - 1) / P - 255.0 / 512.0, ALU.mult, ALU.add))
                then(V.tensor_scalar(tiles[:, :], tiles0[:, :], MAGIC, -MAGIC, ALU.add, ALU.add))
                then(V.tensor_copy(cum[0][:, :], tiles[:, :]))
                for k in range(4):
                    d = 1 << k
                    V.tensor_copy(cum[k + 1][:, 0:d], cum[k][:, 0:d])
                    then(V.tensor_tensor(cum[k + 1][:, d:E_N], cum[k][:, d:E_N], cum[k][:, 0:E_N - d], ALU.add))
                then(V.tensor_tensor(past[:, :, :], K("tile_no").unsqueeze(2).broadcast_to([P, J, E_N]),
                                     cum[4][:, :].unsqueeze(1).broadcast_to([P, J, E_N]), ALU.is_ge))
                then(V.tensor_tensor(past_tiles[:, :, :], past[:, :, :], tiles[:, :].unsqueeze(1).broadcast_to([P, J, E_N]), ALU.mult))
                then(V.tensor_reduce(which[:, :], past[:, :, :], X, ALU.add))
                then(V.tensor_reduce(first[:, :], past_tiles[:, :, :], X, ALU.add))
                then(V.tensor_tensor(tile_in[:, :], K("tile_no"), first[:, :], ALU.subtract))
                then(V.scalar_tensor_tensor(tile_at[:, :], which[:, :], float(LIST_T), tile_in[:, :], ALU.mult, ALU.add))
                then(V.tensor_scalar(clipped[:, :], tile_at[:, :], float(E_N * LIST_T), None, ALU.min))
                then(V.tensor_copy(plan[:, 0, :], clipped[:, :]))
                then(V.tensor_scalar(first[:, :], which[:, :], float(E_N - 1), None, ALU.min))
                then(V.tensor_copy(plan[:, 1, :], first[:, :]))

            @block.sync
            def _(sp):
                sp.wait_ge(s["pad_done"], 1)
                sp.wait_ge(s["planned"], PLAN_OPS)
                for k in range(2):
                    for j in range(J):
                        sp.dma_start(n.plan[k, P * j:P * j + P].rearrange("(p o) -> p o", o=1), plan[:, k, j:j + 1]).then_inc(s["plan_out"], 16)
                sp.wait_ge(s["plan_out"], 16 * 2 * J)
                sp.dma_start(plan_row[:, :, :], n.plan.rearrange("(o k) t -> o k t", o=1)).then_inc(s["plan_in"], 16)
                sp.dma_start(n.lists[E_N * LIST:E_N * LIST + P, :], pad[:, :]).then_inc(s["pads_sent"], 16)
                for e in range(E_N):
                    end = sp.value_load(ends[0:1, e:e + 1], min_val=0, max_val=E_N * LIST)
                    sp.dma_start(n.lists[bass.ds(end, P), :], pad[:, :]).then_inc(s["pads_sent"], 16)
                sp.wait_ge(s["pads_sent"], 16 * (E_N + 1))
                sp.wait_ge(s["plan_in"], 16)


        with nc.Block() as block:
            def run(engine, body):
                for u in range(2):
                    body(u, u, 0)
                with engine.Fori(1, GROUPS_E // 2) as i:
                    for u in range(2):
                        body(2 * i + u, u, i)

            @block.sync
            def _(sp):
                def body(g, u, i):
                    wait(sp, y_sent[u], 16 * J * i)
                    for j in range(J):
                        at = sp.value_load(plan_row[0:1, 0, bass.ds(g * J + j, 1)], min_val=0, max_val=E_N * LIST_T)
                        sp.dma_start(rows[:, u, j, :], n.lists[bass.ds(at * P, P), :]).then_inc(rows_in[u], 16)

                run(sp, body)

            @block.tensor
            def _(pe):
                mm = nc.tensor.matmul

                def turn(g, u, i):
                    pe.wait_ge(rows_in[u], 16 * J * (i + 1))
                    wait(pe, s["x_copied"], g - 1)
                    for j in range(J):
                        last = nc.tensor.transpose(p_xt[u][:, P * j:P * j + P], rows[:, u, j, 0:C].bitcast(FP16), n.h[:, F16_AT["ident16"][0]:F16_AT["ident16"][1]])
                    last.then_inc(s["x_turned"], 1)

                def body(g, u, i):
                    turn(g, u, i)
                    pe.wait_ge(s["x_copied"], g + 1)
                    experts_of = [pe.value_load(plan_row[0:1, 1, bass.ds(g * J + j, 1)], min_val=0, max_val=E_N - 1) for j in range(J)]
                    wait(pe, s["silu_done"], g - 1)
                    for j, e in enumerate(experts_of):
                        for part in range(2):
                            last = mm(p_h1[u][:, P * j:P * j + P], n.w12[:, bass.ds(e, 1), 0, part, :].rearrange("p o h -> p (o h)"),
                                      xt[:, u, P * j:P * j + P], start=(part == 0), stop=(part == 1))
                    last.then_inc(s["h1_ready"], 1)
                    wait(pe, s["hid_done"], g - 1)
                    for j, e in enumerate(experts_of):
                        for part in range(2):
                            last = mm(p_h2[u][:, P * j:P * j + P], n.w12[:, bass.ds(e, 1), 1, part, :].rearrange("p o h -> p (o h)"),
                                      xt[:, u, P * j:P * j + P], start=(part == 0), stop=(part == 1))
                    last.then_inc(s["h2_ready"], 1)
                    pe.wait_ge(s["hid_done"], g + 1)
                    wait(pe, s["y_done"], g - 1)
                    for j, e in enumerate(experts_of):
                        last = mm(p_y[u][:, C * j:C * j + C], hid[:, u, P * j:P * j + P], n.w[:, bass.ds(e * C + W_AT["w3"][0], C)],
                                  start=True, stop=True)
                    last.then_inc(s["y_ready"], 1)

                run(pe, body)

            @block.scalar
            def _(act):
                A = nc.scalar.activation

                def body(g, u, i):
                    act.wait_ge(s["h1_ready"], g + 1)
                    wait(act, s["hid_done"], g - 1)
                    A(act1[:, u, :], p_h1[u][:, :], ACT.Silu, scale=1.0 / (X_SCALE * W_SCALE)).then_inc(s["silu_done"], 1)

                run(act, body)

            @block.vector
            def _(dve):
                V = nc.vector

                def body(g, u, i):
                    dve.wait_ge(s["x_turned"], g + 1)
                    wait(dve, s["h2_ready"], g - 1)
                    V.tensor_copy(xt[:, u, :], p_xt[u][:, :]).then_inc(s["x_copied"], 1)
                    dve.wait_ge(s["silu_done"], g + 1)
                    dve.wait_ge(s["h2_ready"], g + 1)
                    wait(dve, s["y_ready"], g - 1)
                    V.tensor_tensor(hid[:, u, :], p_h2[u][:, :], act1[:, u, :], ALU.mult).then_inc(s["hid_done"], 1)
                    dve.wait_ge(s["y_ready"], g + 1)
                    wait(dve, y_sent[u], 16 * J * i)
                    V.tensor_tensor(y[:, u, :, :], p_y[u][:, :].rearrange("p (j c) -> p j c", j=J),
                                    rows[:, u, :, C + 1:C + 2].bitcast(FP32).broadcast_to([P, J, C]), ALU.mult).then_inc(s["y_done"], 1)

                run(dve, body)

            @block.gpsimd
            def _(pool):
                def body(g, u, i):
                    pool.wait_ge(s["y_done"], g + 1)
                    pool.sem_inc(s["y_go"], 1)
                    for j in range(J):
                        nc.gpsimd.indirect_dma_start(out=n.expert_rows, out_offset=bass.IndirectOffsetOnAxis(ap=rows[:, u, j, C:C + 1], axis=0),
                                                     in_=y[:, u, j, :], in_offset=None, bounds_check=2 * B * TOK - 1, oob_is_err=False).then_inc(y_sent[u], 16)

                run(pool, body)
                for u in range(2):
                    pool.wait_ge(y_sent[u], 16 * J * (GROUPS_E // 2))


PLAN_OPS = 19


def combine(nc, n):
    with ExitStack() as ctx:
        J = 16
        N = TILES_TOK // J
        a = ctx.enter_context(nc.sbuf_tensor("from_experts", [P, 2, 2, J, C], FP32))
        t = ctx.enter_context(nc.sbuf_tensor("one_added", [P, 2, J, C], FP32))
        o = ctx.enter_context(nc.sbuf_tensor("both_added", [P, 2, J, C], FP32))
        rows_in = [n.sem(f"z_rows_in{k}") for k in range(2)]
        out_done = [n.sem(f"z_out_done{k}") for k in range(2)]
        added1, added2 = n.sem("z_added1"), n.sem("z_added2")
        src = n.expert_rows.rearrange("(k m j p) c -> m k p j c", k=2, m=N, p=P)
        dst = n.out.rearrange("b t c -> (b t) c").rearrange("(m j p) c -> m p j c", m=N, p=P)
        with nc.Block() as block:
            @block.sync
            def _(sp):
                for m in range(N):
                    wait(sp, added2, m - 1)
                    for k in range(2):
                        sp.dma_start(a[:, m % 2, k, :, :], src[m, k]).then_inc(rows_in[m % 2], 16)

            @block.vector
            def _(dve):
                for m in range(N):
                    v = m % 2
                    dve.wait_ge(rows_in[v], 32 * (m // 2 + 1))
                    nc.vector.tensor_tensor(t[:, v, :, :], a[:, v, 0, :, :], a[:, v, 1, :, :], ALU.add).then_inc(added1, 1)
                    dve.wait_ge(added1, m + 1)
                    wait(dve, out_done[v], 16 * (m // 2))
                    nc.vector.tensor_tensor(o[:, v, :, :], t[:, v, :, :], n.tokens_t[:, J * m:J * m + J, :], ALU.add).then_inc(added2, 1)

            @block.scalar
            def _(act):
                for m in range(N):
                    act.wait_ge(added2, m + 1)
                    act.dma_start(dst[m], o[:, m % 2, :, :]).then_inc(out_done[m % 2], 16)
                for v in range(2):
                    act.wait_ge(out_done[v], 16 * (N // 2))



def build(nc, ins, out):
    n = Names()
    n.in_weights, n.in_f32, n.in_f16 = ins["weights"], ins["f32"], ins["f16"]
    n.in_w1, n.in_w2, n.in_x, n.in_ids, n.in_pos = ins["w1"], ins["w2"], ins["x"], ins["ids"], ins["pos"]
    with ExitStack() as ctx:
        def sb(name, shape, dt=FP32):
            return ctx.enter_context(nc.sbuf_tensor(name, shape, dt))

        n.sem = lambda name: ctx.enter_context(nc.semaphore(name))
        n.w = sb("w", [P, W_N])
        n.f = sb("f", [P, F32_N])
        n.h = sb("h16", [P, F16_N], FP16)
        n.wk, n.wv, n.wq = sb("wk", [P, P]), sb("wv", [P, P]), sb("wq", [P, P])
        n.bq, n.pb = sb("bq", [P, 1]), sb("pb_bias", [P, 1])
        n.mkv, n.mkv_b = sb("mkv", [P, 2, 2, C]), sb("mkv_b", [P, 2, 2, C])
        n.w12 = sb("w12", [P, E_N, 2, 2, HID], FP16)
        n.tokens = sb("tokens", [P, PAIRS, TOK])
        n.lists = nc.dram_tensor("lists", (LISTS * P, ROW), U32, kind="Internal").ap()
        n.expert_rows = nc.dram_tensor("expert_rows", (2 * B * TOK, C), FP32, kind="Internal").ap()
        n.plan = nc.dram_tensor("plan", (2, 512), I32, kind="Internal").ap()
        n.out = out
        constants(nc, n)
        text(nc, n)
        windows(nc, n)
        n.tokens_t = sb("tokens_t", [P, TILES_TOK, C])
        n.list_end = sb("list_end", [P, 2, E_N])
        mixing(nc, n)
        experts(nc, n)
        combine(nc, n)


def inputs_of(g):
    f, h = shape_constants()
    return {"weights": pack_weights(g), "f32": f, "f16": h, "w1": g["L0_ffn_w1"], "w2": g["L0_ffn_w2"],
            "x": g["x"].reshape(B, C, PIX), "ids": g["x_txt"].reshape(1, B * TXT_T),
            "pos": g["fside_BS_continuous_positions"].reshape(1, B * TXT_T)}


def kernel(**inputs):
    from concourse import bacc
    from concourse.bass_utils import run_bass_kernel_spmd

    nc = bacc.Bacc("TRN2", target_bir_lowering=False, num_devices=1)
    arrays, ins = {}, {}
    for name, value in inputs_of({k: np.asarray(v) for k, v in inputs.items()}).items():
        arrays["in_" + name] = np.ascontiguousarray(value)
        ins[name] = nc.dram_tensor("in_" + name, value.shape, mybir.dt.from_np(value.dtype), kind="ExternalInput").ap()
    out = nc.dram_tensor("out_h", (B, TOK, C), FP32, kind="ExternalOutput").ap()
    build(nc, ins, out)
    result = run_bass_kernel_spmd(nc, [arrays], core_ids=[0])
    return result.results[0]["out_h"]
```

```python
from contextlib import ExitStack

import numpy as np
import concourse.bass as bass
from concourse import mybir

FP32 = mybir.dt.float32
FP16 = mybir.dt.float16
I32 = mybir.dt.int32
U32 = mybir.dt.uint32
ACT = mybir.ActivationFunctionType
ALU = mybir.AluOpType
X = mybir.AxisListType.X

B = 64
C = 64
P = 128
PAIRS = B // 2
PIX = 64 * 64
WIN = 16
IMG_T = PIX // WIN
TXT_T = 128
TOK = IMG_T + TXT_T
HEADS = 8
EPS = 1e-5

GROUP = 2048
GROUPS = B * PIX // 2 // GROUP
CHUNK = 512
CH = GROUP // CHUNK
WG = GROUP // WIN
WC = CHUNK // WIN

E_N = 16
HID = 128
TILES_TOK = B * TOK // P
LIST_T = TILES_TOK + 1
LIST = LIST_T * P
LISTS = E_N * LIST_T + 1
RUN_T = 2 * TILES_TOK + E_N
ROW = 66
X_SCALE = 32.0
W_SCALE = 64.0
AT_UNIT = LISTS
MAGIC = 12582912.0


def pair_view(t):
    return t.rearrange("b c n -> (b c) n")


class Names:
    pass


def wait(engine, sem, value):
    if isinstance(value, int) and value <= 0:
        return
    engine.wait_ge(sem, value)


def zero(nc, sems):
    with nc.Block() as block:
        @block.gpsimd
        def _(pool):
            for sem in sems:
                pool.sem_clear(sem)



F32_PARTS = [("ident", 128), ("center", 128), ("average", 128), ("mean32", 32), ("head32", 32),
             ("center4", 64), ("mask4", 128), ("byte_pos", 1), ("eps", 1), ("tiny", 1), ("rank_e", 16),
             ("list_base", 16), ("pad_place", 1), ("tile_no", 4), ("id_unit", 4), ("at_unit", 4), ("row_no", 12), ("vocab", 1), ("row_of_ones", 128)]
F16_PARTS = [("ident16", 128), ("ones16", 128), ("before16", 128), ("spread16", 4 * 128)]


def columns(parts):
    at, out = 0, {}
    for name, n in parts:
        out[name] = (at, at + n)
        at += n
    return out, at


F32_AT, F32_N = columns(F32_PARTS)
F16_AT, F16_N = columns(F16_PARTS)


def shape_constants():
    two = np.eye(2)
    f = np.zeros((P, F32_N), np.float32)
    h = np.zeros((P, F16_N), np.float16)

    def put(name, value):
        a, b = F32_AT[name]
        f[:value.shape[0], a:b] = value

    p = np.arange(P)
    put("ident", np.eye(P))
    put("center", np.kron(two, np.eye(C) - 1.0 / C))
    put("average", np.kron(two, np.full((C, C), 1.0 / C)))
    mean32 = np.zeros((P, 32))
    head32 = np.zeros((P, 32))
    for s in range(2):
        for head in range(HEADS):
            mean32[s * C:(s + 1) * C, s * HEADS + head] = 1.0 / C
            head32[s * C + head * 8:s * C + head * 8 + 8, s * HEADS + head] = 1.0
    put("mean32", mean32)
    put("head32", head32)
    put("center4", np.kron(np.eye(16), np.eye(4) - 0.25))
    put("mask4", np.kron(np.eye(32), np.full((4, 4), 1.0 / TOK)))
    put("byte_pos", np.linspace(0.0, 1.0, TXT_T, dtype=np.float32)[:, None])
    put("eps", np.full((P, 1), EPS))
    put("tiny", np.full((P, 1), 1e-30))
    put("list_base", np.tile(np.arange(E_N) * LIST, (P, 1)))
    put("pad_place", np.full((P, 1), 2 * B * TOK + 1.0))
    put("tile_no", 4 * p[:, None] + np.arange(4)[None, :])
    put("id_unit", np.tile(float(E_N) ** np.arange(4), (P, 1)))
    put("at_unit", np.tile([1.0, AT_UNIT, 1.0, AT_UNIT], (P, 1)))
    put("rank_e", np.tile(E_N - np.arange(E_N), (P, 1)))
    k, t, smp = np.meshgrid(np.arange(2), np.arange(TOK // P), np.arange(2), indexing="ij")
    put("row_no", p[:, None] + (k * B * TOK + smp * TOK + t * P).reshape(1, -1))
    put("vocab", (p % 64)[:, None])
    put("row_of_ones", np.ones((1, P)))
    for name, value in (("ident16", np.eye(P)), ("ones16", np.ones((P, P))),
                        ("before16", (p[:, None] < p[None, :]))):
        a, b = F16_AT[name]
        h[:, a:b] = value
    a, _ = F16_AT["spread16"]
    for c in range(CH):
        for s in range(2):
            for head in range(HEADS):
                row = 32 * c + s * HEADS + head
                col = a + P * c + s * C + head * 8
                h[row, col:col + 8] = 1.0
    return f, h


W_PARTS = [("wk", 128), ("wv", 128), ("wq", 128), ("proj", 128),
           ("kv_scale", 1), ("kv_shift", 1), ("q_scale", 1), ("q_shift", 1), ("proj_b", 1),
           ("mk", 128), ("mv", 128), ("mk_b", 1), ("mv_b", 1), ("mq", 128), ("mq_b", 1),
           ("mproj", 128), ("mproj_b", 1), ("kv_ln_w", 256), ("kv_ln_b", 256),
           ("gate", 32), ("gate_b", 32), ("w3", E_N * C),
           ("c1", 4 * 128), ("c1_b", 1), ("c2", 5 * 64), ("c2_b", 1), ("c3", 3 * 2), ("c3_b", 1),
           ("embed", 68), ("widths", 4), ("scales", 4)]
W_AT, W_N = columns(W_PARTS)


def pack_weights(g):
    w = np.zeros((P, W_N), np.float32)

    def put(name, value, rows=slice(None)):
        a, b = W_AT[name]
        w[rows, a:b] = value

    def both(name, matrix):
        a, b = W_AT[name]
        n = (b - a) // 2
        w[:C, a:a + n] = matrix
        w[C:, a + n:b] = matrix

    def column(name, vector):
        put(name, np.tile(vector, P // vector.shape[0])[:, None])

    both("wk", g["L0_tok_Wkv"][:C].T)
    both("wv", g["L0_tok_Wkv"][C:].T)
    both("wq", g["L0_tok_Wq"].T)
    both("proj", g["L0_tok_proj_w"].T)
    column("kv_scale", g["L0_tok_ln_kv_w"])
    column("kv_shift", g["L0_tok_ln_kv_b"])
    column("q_scale", g["L0_tok_ln_q_w"])
    column("q_shift", g["L0_tok_ln_q_b"])
    column("proj_b", g["L0_tok_proj_b"])
    qkv = g["L0_attn_W_qkv"].reshape(16, 3, 4, C)
    qkv_b = g["L0_attn_b_qkv"].reshape(16, 3, 4)
    for name, part in (("mk", 1), ("mv", 2)):
        put(name, np.tile(qkv[:, part].reshape(C, C), (1, 2)), slice(0, C))
        put(name + "_b", qkv_b[:, part].reshape(C, 1), slice(0, C))
    both("mq", qkv[:, 0].reshape(C, C).T)
    column("mq_b", qkv_b[:, 0].reshape(C))
    both("mproj", g["L0_attn_W_proj"].T)
    column("mproj_b", g["L0_attn_b_proj"])
    for name, k, v in (("kv_ln_w", "L0_attn_kln_w", "L0_attn_vln_w"), ("kv_ln_b", "L0_attn_kln_b", "L0_attn_vln_b")):
        put(name, np.concatenate([np.tile(g[k].reshape(C), 2), np.tile(g[v].reshape(C), 2)])[None, :])
    both("gate", g["L0_ffn_gate_w"])
    put("gate_b", np.tile(g["L0_ffn_gate_b"], 2)[None, :])
    put("w3", g["L0_ffn_w3"].transpose(1, 0, 2).reshape(HID, E_N * C))
    taps = np.zeros((2, C, 4, 128), np.float32)
    w1 = g["L0_txt_w1"]
    for tap in range(7):
        taps[tap % 2, :, tap // 2] = w1[:, :, tap].T
    put("c1", taps.reshape(P, 4 * 128))
    column("c1_b", g["L0_txt_b1"])
    put("c2", g["L0_txt_w2"].transpose(1, 2, 0).reshape(P, 5 * C))
    column("c2_b", g["L0_txt_b2"])
    c3 = np.zeros((2, C, 3, 2), np.float32)
    for s in range(2):
        c3[s, :, :, s] = g["L0_txt_w3"][0]
    put("c3", c3.reshape(P, 6))
    put("c3_b", g["L0_txt_b3"][0])
    put("embed", np.concatenate([g["L0_txt_emb"], g["L0_txt_locality_shapes"]], axis=1), slice(0, C))
    put("widths", g["L0_txt_multiscale_widths"][None, :])
    put("scales", g["L0_txt_scale_weights"][None, :])
    return w


def constants(nc, n):
    with ExitStack() as ctx:
        raw = ctx.enter_context(nc.sbuf_tensor("raw12", [P, 2, E_N * HID], FP32))
        big = ctx.enter_context(nc.sbuf_tensor("big12", [P, 2, E_N * HID], FP32))
        scaled = ctx.enter_context(nc.sbuf_tensor("scaled", [P, 3, 128], FP32))
        bias_rows = ctx.enter_context(nc.sbuf_tensor("bias_rows", [C, 2, 128], FP32))
        v_bias = ctx.enter_context(nc.sbuf_tensor("v_bias", [P, 1], FP32))
        pw = ctx.enter_context(nc.psum_tensor("pw", [P, 512], FP32))
        pm = ctx.enter_context(nc.psum_tensor("pm", [P, 512], FP32))
        pb = ctx.enter_context(nc.psum_tensor("pb", [P, 8], FP32))
        sem = lambda name: ctx.enter_context(nc.semaphore(name))
        weights_in, w12_in = n.sem("weights_in"), n.sem("w12_in")
        scaled_rows, w_products, vb_product, vb_copied = (n.sem(x) for x in ("scaled_rows", "w_products", "vb_product", "vb_copied"))
        pb_product, w12_scaled, w12_high = (n.sem(x) for x in ("pb_product", "w12_scaled", "w12_high"))
        w, f = n.w, n.f

        def W(name, rows=P):
            a, b = W_AT[name]
            return w[0:rows, a:b]

        def K(name, rows=P):
            a, b = F32_AT[name]
            return f[0:rows, a:b]

        with nc.Block() as block:
            @block.sync
            def _(sp):
                sp.dma_start(w[:, :], n.in_weights).then_inc(weights_in, 16)
                sp.dma_start(f[:, :], n.in_f32).then_inc(weights_in, 16)
                sp.dma_start(n.h[:, :], n.in_f16).then_inc(weights_in, 16)
                for half in range(2):
                    for which, src in enumerate((n.in_w1, n.in_w2)):
                        sp.dma_start(raw[half * C:(half + 1) * C, which, :].rearrange("c (e j) -> c e j", e=E_N),
                                     src.rearrange("e c j -> c e j")).then_inc(w12_in, 16)

            @block.vector
            def _(dve):
                dve.wait_ge(weights_in, 48)
                nc.vector.tensor_scalar(scaled[:, 0, :], W("wk"), W("kv_scale"), None, ALU.mult).then_inc(scaled_rows, 1)
                nc.vector.tensor_scalar(scaled[:, 1, :], W("wv"), W("kv_scale"), None, ALU.mult).then_inc(scaled_rows, 1)
                nc.vector.tensor_scalar(n.wq[:, :], W("wq"), W("q_scale"), 0.125, ALU.mult, ALU.mult)
                nc.vector.tensor_scalar(scaled[:, 2, :], W("wq"), 0.125, None, ALU.mult).then_inc(scaled_rows, 1)
                for i, name in enumerate(("mk_b", "mv_b")):
                    nc.vector.tensor_scalar(bias_rows[:, i, :], f[0:C, F32_AT["average"][0]:F32_AT["average"][1]], 0.0,
                                            W(name, C), ALU.mult, ALU.add).then_inc(scaled_rows, 1)
                dve.wait_ge(w_products, 1)
                nc.vector.tensor_copy(n.wk[:, :], pw[:, 0:128])
                nc.vector.tensor_copy(n.wv[:, :], pw[:, 128:256])
                nc.vector.memset(n.mkv[:, :, :, :], 0.0).then_inc(vb_copied, 1)
                dve.wait_ge(vb_copied, 1)
                for s in range(2):
                    nc.vector.tensor_copy(n.mkv[s * C:(s + 1) * C, :, s, :],
                                          pm[s * C:(s + 1) * C, 0:128].rearrange("p (a c) -> p a c", a=2))
                    nc.vector.tensor_copy(n.mkv_b[:, :, s, :], pm[:, 128:256].rearrange("p (a c) -> p a c", a=2))
                nc.vector.tensor_copy(n.bq[:, :], pw[:, 256:257])
                nc.vector.tensor_copy(v_bias[:, :], pw[:, 257:258]).then_inc(vb_copied, 1)
                dve.wait_ge(pb_product, 1)
                nc.vector.tensor_tensor(n.pb[:, :], pb[:, 0:1], W("proj_b"), ALU.add)
                dve.wait_ge(w12_in, 64)
                nc.vector.tensor_scalar(big[:, :, :], raw[:, :, :], W_SCALE, None, ALU.mult).then_inc(w12_scaled, 1)
                dve.wait_ge(w12_scaled, 1)
                for which in range(2):
                    src = big[:, which, :].rearrange("p (e j) -> p e j", e=E_N)
                    nc.vector.tensor_copy(n.w12[:, :, which, 0, :], src).then_inc(w12_high, 1)
                    dve.wait_ge(w12_high, which + 1)
                    nc.vector.tensor_tensor(n.w12[:, :, which, 1, :], src, n.w12[:, :, which, 0, :], ALU.subtract)

            @block.tensor
            def _(pe):
                pe.wait_ge(weights_in, 48)
                pe.wait_ge(scaled_rows, 5)
                nc.tensor.matmul(pw[:, 0:128], K("center"), scaled[:, 0, :], start=True, stop=True)
                nc.tensor.matmul(pw[:, 128:256], K("center"), scaled[:, 1, :], start=True, stop=True)
                nc.tensor.matmul(pw[:, 256:257], scaled[:, 2, :], W("q_shift"), start=True, stop=True)
                nc.tensor.matmul(pw[:, 257:258], W("wv"), W("kv_shift"), start=True, stop=True)
                for i, name in enumerate(("mk", "mv")):
                    nc.tensor.matmul(pm[:, 64 * i:64 * i + 64], W(name, C), K("center4", C), start=True, stop=True)
                for i in range(2):
                    last = nc.tensor.matmul(pm[:, 128 + 64 * i:192 + 64 * i], bias_rows[:, i, :], K("center4", C),
                                            start=True, stop=True)
                last.then_inc(w_products, 1)
                pe.wait_ge(vb_copied, 2)
                nc.tensor.matmul(pb[:, 0:1], W("proj"), v_bias[:, :], start=True, stop=True).then_inc(pb_product, 1)


def text(nc, n):
    with ExitStack() as ctx:
        def sb(name, shape, dt=FP32):
            return ctx.enter_context(nc.sbuf_tensor(name, shape, dt))

        def bank(name):
            return ctx.enter_context(nc.psum_tensor(name, [P, 512], FP32))

        FOUR = 4
        SC = 4
        STEPS = B // FOUR
        PAD1, PAD2, PAD3 = TXT_T + 6, TXT_T + 4, TXT_T + 2
        UNSCALE = 1.0 / W_SCALE
        ids = sb("ids", [P, FOUR, TXT_T], I32)
        pos = sb("pos", [P, 2, FOUR, TXT_T])
        onehot = sb("onehot", [P, FOUR, PAD1], FP16)
        c1 = sb("c1_parts", [P, 2, 4, P], FP16)
        c1_big = sb("c1_big", [P, 4, P])
        emb = sb("emb_parts", [P, 3, 68], FP16)
        emb_big = sb("emb_big", [P, 2, 68])
        hidden1 = sb("hidden1", [P, FOUR, PAD2])
        hidden2 = sb("hidden2", [P, 2, PAD3])
        gates = sb("gates", [P, 2, FOUR])
        gates1 = sb("gates1", [P, 2, FOUR])
        factor = sb("factor", [P, FOUR])
        loc = sb("loc", [P, FOUR, 4])
        abs_w = sb("abs_w", [P, FOUR])
        center = sb("wave_center", [P, 2, FOUR])
        width = sb("width", [P, FOUR, SC])
        width1 = sb("width1", [P, FOUR, SC])
        inv_w = sb("inv_w", [P, 2, FOUR, SC])
        shift = sb("shift", [P, 2, FOUR])
        amps = sb("amps", [P, 2, FOUR, C])
        sw2 = sb("sw2", [P, SC])
        b3_half = sb("b3_half", [P, 1])
        dist = sb("dist", [P, FOUR, TXT_T])
        z = sb("z", [P, SC, FOUR, TXT_T])
        zc = sb("zc", [P, SC, FOUR, TXT_T])
        z_sq = sb("z_sq", [P, SC, FOUR, TXT_T])
        turns = sb("turns", [P, SC, FOUR, TXT_T])
        whole = sb("whole", [P, SC, FOUR, TXT_T])
        frac = sb("frac", [P, SC, FOUR, TXT_T])
        bell = sb("bell", [P, SC, FOUR, TXT_T])
        wave = sb("wave", [P, SC, FOUR, TXT_T])
        packet = sb("packet", [P, SC, FOUR, TXT_T])
        p_c1, p_c2, p_ctx, p_emb, p_field = (bank(x) for x in ("p_c1", "p_c2", "p_ctx", "p_emb", "p_field"))
        names = ("parts_hi parts_mid parts_done ids_in onehot_done c1_ready gelu1_done c2_ready gelu2_done ctx_ready emb_ready "
                 "gates_done loc_done gates_eased factor_done amps_done width_made width_eased params_done dist_done z_done "
                 "clamped squared bell_done turned rounded frac_done wave_done packet_done field_ready field_copied zeroed")
        s = {name: ctx.enter_context(nc.semaphore("t_" + name)) for name in names.split()}
        pos_in = [ctx.enter_context(nc.semaphore(f"t_pos_in{k}")) for k in range(2)]
        W = lambda name: n.w[:, W_AT[name][0]:W_AT[name][1]]
        K = lambda name: n.f[:, F32_AT[name][0]:F32_AT[name][1]]

        def run(engine, body):
            for i in range(2):
                body(i, i, True, i > 0)
            with engine.Fori(1, STEPS // 2) as j:
                for u in range(2):
                    body(2 * j + u, u, True, True)
            body(STEPS, 0, False, True)

        with nc.Block() as block:
            @block.sync
            def _(sp):
                def body(i, u, new, old):
                    if not new:
                        return
                    wait(sp, s["onehot_done"], 2 * i)
                    sp.dma_start(ids[:, :, :].rearrange("p b t -> p (b t)"),
                                 n.in_ids[0, bass.ds(i * 512, 512)].partition_broadcast(P)).then_inc(s["ids_in"], 16)
                    wait(sp, s["dist_done"], i - 1)
                    sp.dma_start(pos[:, u, :, :].rearrange("p b t -> p (b t)"),
                                 n.in_pos[0, bass.ds(i * 512, 512)].partition_broadcast(P)).then_inc(pos_in[u], 16)

                run(sp, body)

            @block.tensor
            def _(pe):
                mm = nc.tensor.matmul

                def body(i, u, new, old):
                    if new:
                        pe.wait_ge(s["onehot_done"], 2 * i + 2)
                        wait(pe, s["gelu1_done"], i)
                        if isinstance(i, int) and i == 0:
                            pe.wait_ge(s["parts_done"], 3)
                            pe.wait_ge(s["zeroed"], 3)
                        for j in range(4):
                            for part in range(2):
                                last = mm(p_c1[:, :], c1[:, part, j, :], onehot[:, :, 2 * j:2 * j + TXT_T],
                                          start=(j + part == 0), stop=(j == 3 and part == 1))
                        last.then_inc(s["c1_ready"], 1)
                        wait(pe, s["amps_done"], i)
                        wait(pe, s["loc_done"], i)
                        for b in range(FOUR):
                            for part in range(3):
                                last = mm(p_emb[:, 68 * b:68 * b + 68], onehot[:, b, 3:3 + TXT_T], emb[:, part, :],
                                          start=(part == 0), stop=(part == 2))
                        last.then_inc(s["emb_ready"], 1)
                    if new:
                        pe.wait_ge(s["gelu1_done"], i + 1)
                        wait(pe, s["gelu2_done"], i)
                        for k in range(2):
                            for tap in range(5):
                                last = mm(p_c2[C * k:C * k + C, 0:2 * TXT_T], n.w[:, W_AT["c2"][0] + C * tap:W_AT["c2"][0] + C * tap + C],
                                          hidden1[:, k:4:2, tap:tap + TXT_T], start=(tap == 0), stop=(tap == 4), tile_position=(0, C * k))
                        last.then_inc(s["c2_ready"], 1)
                        pe.wait_ge(s["gelu2_done"], i + 1)
                        wait(pe, s["gates_done"], i)
                        for q in range(2):
                            for tap in range(3):
                                last = mm(p_ctx[:, 2 * q:2 * q + 2], hidden2[:, q, tap:tap + TXT_T],
                                          n.w[:, W_AT["c3"][0] + 2 * tap:W_AT["c3"][0] + 2 * tap + 2], start=(tap == 0), stop=(tap == 2))
                        last.then_inc(s["ctx_ready"], 1)
                    if old:
                        pe.wait_ge(s["packet_done"], 4 * i)
                        wait(pe, s["field_copied"], i - 1)
                        for b in range(FOUR):
                            for k in range(SC):
                                last = mm(p_field[C * (b % 2):C * (b % 2) + C, P * (b // 2):P * (b // 2) + P], amps[:, 1 - u, b, :],
                                          packet[:, k, b, :], start=(k == 0), stop=(k == SC - 1), tile_position=(0, C * (b % 2)))
                        last.then_inc(s["field_ready"], 1)

                run(pe, body)

            @block.scalar
            def _(act):
                A = nc.scalar.activation

                def body(i, u, new, old):
                    emb4 = p_emb[:, 0:68 * FOUR].rearrange("p (b e) -> p b e", b=FOUR)
                    if new:
                        act.wait_ge(s["c1_ready"], i + 1)
                        wait(act, s["c2_ready"], i)
                        if isinstance(i, int) and i == 0:
                            act.wait_ge(s["zeroed"], 3)
                        A(hidden1[:, :, 2:2 + TXT_T], p_c1[:, :].rearrange("p (b t) -> p b t", b=FOUR), ACT.Gelu,
                          bias=W("c1_b"), scale=UNSCALE).then_inc(s["gelu1_done"], 1)
                    if old:
                        act.wait_ge(s["clamped"], i)
                        wait(act, s["bell_done"], i - 1)
                        A(z_sq[:, :, :, :], zc[:, :, :, :], ACT.Square).then_inc(s["squared"], 1)
                    if new:
                        act.wait_ge(s["c2_ready"], i + 1)
                        wait(act, s["ctx_ready"], i)
                        A(hidden2[:, :, 1:1 + TXT_T], p_c2[:, 0:2 * TXT_T].rearrange("p (q t) -> p q t", q=2), ACT.Gelu,
                          bias=W("c2_b")).then_inc(s["gelu2_done"], 1)
                        act.wait_ge(s["emb_ready"], i + 1)
                        wait(act, s["gates_eased"], i)
                        A(gates[:, 1, :], emb4[:, :, 66], ACT.Tanh, scale=0.5 * UNSCALE)
                        wait(act, s["params_done"], i)
                        A(loc[:, :, :], emb4[:, :, 64:68], ACT.Copy, scale=UNSCALE)
                        A(abs_w[:, :], emb4[:, :, 65], ACT.Abs, scale=UNSCALE).then_inc(s["loc_done"], 1)
                        act.wait_ge(s["ctx_ready"], i + 1)
                        A(gates[:, 0, :], p_ctx[:, 0:FOUR], ACT.Tanh, scale=0.5, bias=b3_half[:, :]).then_inc(s["gates_done"], 1)
                    if old:
                        act.wait_ge(s["squared"], i)
                        wait(act, s["packet_done"], 4 * (i - 1))
                        A(bell[:, :, :, :], z_sq[:, :, :, :], ACT.Exp, scale=-0.5).then_inc(s["bell_done"], 1)
                        act.wait_ge(s["frac_done"], i)
                        A(wave[:, :, :, :], frac[:, :, :, :], ACT.Sin, scale=6.2831845).then_inc(s["wave_done"], 1)
                        act.wait_ge(s["field_ready"], i)
                        A(n.tokens[:, bass.ds(2 * i - 2, 2), IMG_T:TOK], p_field[:, 0:2 * TXT_T].rearrange("p (q t) -> p q t", q=2),
                          ACT.Copy).then_inc(s["field_copied"], 1)

                run(act, body)

            @block.vector
            def _(dve):
                V = nc.vector
                V.tensor_scalar(c1_big[:, :, :].rearrange("p a b -> p (a b)"), W("c1"), W_SCALE, None, ALU.mult)
                V.tensor_scalar(emb_big[:, 0, :], W("embed"), W_SCALE, None, ALU.mult)
                V.tensor_tensor(sw2[:, :], W("scales"), W("scales"), ALU.mult)
                V.tensor_scalar(b3_half[:, :], W("c3_b"), 0.5, None, ALU.mult).then_inc(s["parts_hi"], 1)
                dve.wait_ge(s["parts_hi"], 1)
                V.tensor_copy(c1[:, 0, :, :], c1_big[:, :, :])
                V.tensor_copy(emb[:, 0, :], emb_big[:, 0, :]).then_inc(s["parts_hi"], 1)
                dve.wait_ge(s["parts_hi"], 2)
                V.tensor_tensor(c1[:, 1, :, :], c1_big[:, :, :], c1[:, 0, :, :], ALU.subtract).then_inc(s["parts_done"], 1)
                V.tensor_tensor(emb_big[:, 1, :], emb_big[:, 0, :], emb[:, 0, :], ALU.subtract).then_inc(s["parts_mid"], 1)
                dve.wait_ge(s["parts_mid"], 1)
                V.tensor_copy(emb[:, 1, :], emb_big[:, 1, :]).then_inc(s["parts_done"], 1)
                dve.wait_ge(s["parts_done"], 2)
                V.tensor_tensor(emb[:, 2, :], emb_big[:, 1, :], emb[:, 1, :], ALU.subtract).then_inc(s["parts_done"], 1)

                def body(i, u, new, old):
                    if new:
                        dve.wait_ge(s["ids_in"], 16 * (i + 1))
                        wait(dve, s["emb_ready"], i)
                        if isinstance(i, int) and i == 0:
                            dve.wait_ge(s["zeroed"], 1)
                        for half in range(2):
                            V.tensor_scalar(onehot[C * half:C * half + C, :, 3 - half:3 - half + TXT_T], ids[C * half:C * half + C, :, :],
                                            K("vocab")[C * half:C * half + C, :], None, ALU.is_equal).then_inc(s["onehot_done"], 1)
                    if old:
                        v = 1 - u
                        dve.wait_ge(pos_in[v], 16 * ((i + 1) // 2) if isinstance(i, int) else 16 * wave_loads(i, u))
                        V.tensor_tensor(dist[:, :, :], pos[:, v, :, :], center[:, v, :].unsqueeze(2).broadcast_to([P, FOUR, TXT_T]),
                                        ALU.subtract).then_inc(s["dist_done"], 1)
                        dve.wait_ge(s["dist_done"], i)
                        wait(dve, s["clamped"], i - 1)
                        for k in range(SC):
                            last = V.tensor_tensor(z[:, k, :, :], dist[:, :, :], inv_w[:, v, :, k:k + 1].broadcast_to([P, FOUR, TXT_T]), ALU.mult)
                        last.then_inc(s["z_done"], 1)
                        dve.wait_ge(s["z_done"], i)
                        wait(dve, s["squared"], i - 1)
                        wait(dve, s["turned"], i - 1)
                        V.tensor_scalar(zc[:, :, :, :], z[:, :, :, :], 30.0, -30.0, ALU.min, ALU.max).then_inc(s["clamped"], 1)
                    if new:
                        dve.wait_ge(s["loc_done"], i + 1)
                        wait(dve, s["dist_done"], i - 1)
                        wait(dve, s["turned"], i - 1)
                        V.tensor_scalar(center[:, u, :], loc[:, :, 0], 0.05, K("byte_pos"), ALU.mult, ALU.add)
                        V.tensor_scalar(shift[:, u, :], loc[:, :, 3], 0.5, 0.25, ALU.mult, ALU.add)
                        V.tensor_tensor(width[:, :, :], abs_w[:, :].unsqueeze(2).broadcast_to([P, FOUR, SC]),
                                        W("widths").unsqueeze(1).broadcast_to([P, FOUR, SC]), ALU.mult).then_inc(s["width_made"], 1)
                        dve.wait_ge(s["width_made"], i + 1)
                        V.tensor_scalar(width1[:, :, :], width[:, :, :], 1e-5, None, ALU.add).then_inc(s["width_eased"], 1)
                        dve.wait_ge(s["width_eased"], i + 1)
                        V.reciprocal(inv_w[:, u, :, :], width1[:, :, :]).then_inc(s["params_done"], 1)
                    if old:
                        dve.wait_ge(s["turned"], i)
                        wait(dve, s["frac_done"], i - 1)
                        V.tensor_scalar(whole[:, :, :, :], turns[:, :, :, :], MAGIC, -MAGIC, ALU.add, ALU.add).then_inc(s["rounded"], 1)
                    if new:
                        dve.wait_ge(s["gates_done"], i + 1)
                        wait(dve, s["factor_done"], i)
                        V.tensor_scalar(gates1[:, :, :], gates[:, :, :], 0.5, 0.5, ALU.mult, ALU.add).then_inc(s["gates_eased"], 1)
                        dve.wait_ge(s["gates_eased"], i + 1)
                        wait(dve, s["amps_done"], i)
                        V.scalar_tensor_tensor(factor[:, :], gates1[:, 0, :], UNSCALE, gates1[:, 1, :], ALU.mult, ALU.mult).then_inc(s["factor_done"], 1)
                        dve.wait_ge(s["factor_done"], i + 1)
                        wait(dve, s["field_ready"], i - 1)
                        V.tensor_tensor(amps[:, u, :, :], p_emb[:, 0:68 * FOUR].rearrange("p (b e) -> p b e", b=FOUR)[:, :, 0:C],
                                        factor[:, :].unsqueeze(2).broadcast_to([P, FOUR, C]), ALU.mult).then_inc(s["amps_done"], 1)
                    if old:
                        dve.wait_ge(s["wave_done"], i)
                        dve.wait_ge(s["bell_done"], i)
                        wait(dve, s["field_ready"], i - 1)
                        for k in range(SC):
                            V.scalar_tensor_tensor(packet[:, k, :, :], bell[:, k, :, :], sw2[:, k:k + 1], wave[:, k, :, :],
                                                   ALU.mult, ALU.mult).then_inc(s["packet_done"], 1)

                def wave_loads(i, u):
                    return i // 2 if u == 0 else (i + 1) // 2

                run(dve, body)

            @block.gpsimd
            def _(pool):
                G = nc.gpsimd
                G.memset(onehot[:, :, :], 0.0).then_inc(s["zeroed"], 1)
                G.memset(hidden1[:, :, :], 0.0).then_inc(s["zeroed"], 1)
                G.memset(hidden2[:, :, :], 0.0).then_inc(s["zeroed"], 1)

                def body(i, u, new, old):
                    if old:
                        v = 1 - u
                        pool.wait_ge(s["clamped"], i)
                        wait(pool, s["rounded"], i - 1)
                        wait(pool, s["frac_done"], i - 1)
                        G.tensor_tensor(turns[:, :, :, :].rearrange("p k b t -> p k b t"), zc[:, :, :, :],
                                        shift[:, v, :].unsqueeze(1).unsqueeze(3).broadcast_to([P, SC, FOUR, TXT_T]), ALU.add).then_inc(s["turned"], 1)
                        pool.wait_ge(s["rounded"], i)
                        wait(pool, s["wave_done"], i - 1)
                        G.tensor_tensor(frac[:, :, :, :], turns[:, :, :, :], whole[:, :, :, :], ALU.subtract).then_inc(s["frac_done"], 1)

                run(pool, body)

        zero(nc, [*s.values(), *pos_in])


def windows(nc, n):
    with ExitStack() as ctx:
        def sb(name, shape, dt=FP32):
            return ctx.enter_context(nc.sbuf_tensor(name, shape, dt))

        def bank(name):
            return ctx.enter_context(nc.psum_tensor(name, [P, 512], FP32))

        xs = sb("xs", [P, 4, GROUP])
        squares = sb("squares", [P, GROUP])
        tree1 = sb("tree1", [P, 1024])
        tree2 = sb("tree2", [P, 512])
        tree3 = sb("tree3", [P, 256])
        sums = sb("sums", [P, 4, WG])
        q_cent = sb("q_cent", [P, WG])
        q_square = sb("q_square", [P, WG])
        q_log = sb("q_log", [P, WG])
        q_rstd = sb("q_rstd", [P, WG])
        q_norm = sb("q_norm", [P, WG])
        qs = sb("qs", [P, 2, WG])
        mean_sq = sb("mean_sq", [P, CHUNK])
        var = sb("var", [P, CHUNK])
        var_pos = sb("var_pos", [P, CHUNK])
        var_log = sb("var_log", [P, CHUNK])
        rstd = sb("rstd", [P, 2, CHUNK])
        qk = sb("qk", [P, CH, CHUNK])
        score = sb("score", [P, CHUNK])
        top = sb("top", [P, WC])
        below = sb("below", [P, CHUNK])
        ex = sb("ex", [P, CHUNK])
        total = sb("total", [P, WC])
        inv = sb("inv", [P, WC])
        ex_rstd = sb("ex_rstd", [P, CHUNK])
        weight = sb("weight", [P, CHUNK])
        w_hi = sb("w_hi", [P, 2, CHUNK], FP16)
        w_lo = sb("w_lo", [P, 2, CHUNK], FP16)
        w_wide = sb("w_wide", [P, 2, CHUNK])
        wv = sb("wv_prod", [P, 2, CHUNK])
        agg = sb("agg", [P, WG])
        out_b = sb("out_b", [P, WG])
        p_kv = [bank("p_kv0"), bank("p_kv1"), bank("p_kv2")]
        p_w, p_mean, p_sq, p_score, p_q = (bank(x) for x in ("p_w", "p_mean", "p_sq", "p_score", "p_q"))
        cent_cols, var_cols, query_cols, out_cols = (slice(WG * k, WG * k + WG) for k in range(4))
        names = ("sums_1 sums_2 sums_3 sums_done cent_ready cent_copied q_var_ready q_log_done q_rstd_done q_normed "
                 "q_ready q_copied squared mean_ready sq_ready mean_sq_done var_done var_clamped var_logged rstd_done "
                 "k_ready qk_done scores_ready scored top_done below_done exp_done total_done inv_done ex_rstd_done "
                 "weight_done hi_done lo_done v_ready wide_ready wide_copied wv_done reduced proj_ready out_biased token_done")
        s = {name: ctx.enter_context(nc.semaphore(name)) for name in names.split()}
        x_in = [ctx.enter_context(nc.semaphore(f"x_in{k}")) for k in range(4)]
        x_dram = n.in_x.rearrange("(q b) c (h n) -> q (b c) h n", b=2, h=2)
        K = lambda name, rows=P: n.f[0:rows, F32_AT[name][0]:F32_AT[name][1]]
        spread = lambda c: n.h[:, F16_AT["spread16"][0] + P * c:F16_AT["spread16"][0] + P * c + P]
        proj = n.w[:, W_AT["proj"][0]:W_AT["proj"][1]]

        def window_order(t):
            return t.rearrange("p (row col x) -> p col row x", row=8, x=4)

        def by_window(t):
            return t.rearrange("p (col k) -> p col k", k=WIN)

        def chunk_windows(t, c):
            return t[:, WC * c:WC * c + WC].rearrange("p (row col) -> p col row", row=2)

        def steps(body):
            for g in range(-1, 4):
                body(g, g % 4, g // 4, g >= 0, g < GROUPS - 1, g >= 1, g >= 2)
            return lambda i: [body(4 * i + u, u, i, True, True, True, True) for u in range(4)]

        def tail(body):
            for g in range(GROUPS - 4, GROUPS + 2):
                body(g, g % 4, g // 4, g < GROUPS, g < GROUPS - 1, g <= GROUPS, True)

        def run(engine, body):
            loop = steps(body)
            with engine.Fori(1, GROUPS // 4 - 1) as i:
                loop(i)
            tail(body)

        with nc.Block() as block:
            @block.sync
            def _(sp):
                def load(g, u, i):
                    wait(sp, s["v_ready"], 4 * (g - 3))
                    sp.dma_start(xs[:, u, :], x_dram[2 * i + u // 2, :, u % 2, :]).then_inc(x_in[u], 16)

                for g in range(4):
                    load(g, g, 0)
                with sp.Fori(1, GROUPS // 4) as i:
                    for u in range(4):
                        load(4 * i + u, u, i)

            @block.tensor
            def _(pe):
                mm = nc.tensor.matmul

                def body(g, u, i, cur, nxt, prev, out):
                    un, uv = (u + 1) % 4, (u + 3) % 4
                    i_n = i + 1 if u == 3 else i
                    px = [slice(CHUNK * c, CHUNK * c + CHUNK) for c in range(CH)]
                    if cur:
                        for c in range(CH):
                            if c < 3:
                                wait(pe, s["wv_done"], 4 * (g - 2) + (3, 4, 2)[c])
                            else:
                                pe.wait_ge(s["qk_done"], 4 * g + 1)
                            mm(p_kv[c % 3][:, :], n.wk[:, :], window_order(xs[:, u, px[c]]), start=True, stop=True).then_inc(s["k_ready"], 1)
                    if out:
                        pe.wait_ge(s["reduced"], 4 * (g - 1))
                        pe.wait_ge(s["q_copied"], g + 1 if cur else GROUPS)
                        wait(pe, s["out_biased"], g - 2)
                        mm(p_q[:, out_cols], proj, agg[:, :], start=True, stop=True).then_inc(s["proj_ready"], 1)
                    if nxt:
                        pe.wait_ge(x_in[un], 16 * (i_n + 1))
                        wait(pe, s["mean_sq_done"], g + 1)
                        for c in range(CH):
                            last = mm(p_mean[32 * c:32 * c + 32, :], K("mean32"), window_order(xs[:, un, px[c]]), start=True, stop=True,
                                      tile_position=(0, 32 * c))
                        last.then_inc(s["mean_ready"], 1)
                    if cur:
                        pe.wait_ge(s["qk_done"], 4 * g + 4)
                        wait(pe, s["scored"], g)
                        for c in range(CH):
                            last = mm(p_score[32 * c:32 * c + 32, :], K("head32"), qk[:, c, :], start=True, stop=True,
                                      tile_position=(0, 32 * c))
                        last.then_inc(s["scores_ready"], 1)
                    if nxt:
                        pe.wait_ge(s["squared"], g + 2)
                        wait(pe, s["var_done"], g + 1)
                        for c in range(CH):
                            last = mm(p_sq[32 * c:32 * c + 32, :], K("mean32"), window_order(squares[:, px[c]]), start=True, stop=True,
                                      tile_position=(0, 32 * c))
                        last.then_inc(s["sq_ready"], 1)
                        pe.wait_ge(s["sums_done"], g + 2)
                        wait(pe, s["out_biased"], g - 1)
                        wait(pe, s["q_copied"], g + 1)
                        mm(p_q[:, cent_cols], K("center"), sums[:, un, :], start=True, stop=True).then_inc(s["cent_ready"], 1)
                    for c in range(CH):
                        if prev:
                            if c == 0:
                                pe.wait_ge(s["lo_done"], g)
                            wait(pe, s["wide_copied"], 4 * (g - 1) + c)
                            mm(p_w[:, :], spread(c), w_hi[:, uv % 2, :], start=True, stop=False)
                            mm(p_w[:, :], spread(c), w_lo[:, uv % 2, :], start=False, stop=True).then_inc(s["wide_ready"], 1)
                            if c == CH - 1:
                                pe.wait_ge(s["wv_done"], 4 * (g - 1) + 1)
                            elif cur:
                                pe.wait_ge(s["qk_done"], 4 * g + c + 2)
                            mm(p_kv[(c + 1) % 3][:, :], n.wv[:, :], window_order(xs[:, uv, px[c]]), start=True, stop=True).then_inc(s["v_ready"], 1)
                        if nxt and c == 1:
                            pe.wait_ge(s["cent_copied"], g + 2)
                            mm(p_q[:, var_cols], K("average"), q_square[:, :], start=True, stop=True).then_inc(s["q_var_ready"], 1)
                        if nxt and c == CH - 1:
                            pe.wait_ge(s["q_normed"], g + 2)
                            mm(p_q[:, query_cols], n.wq[:, :], q_norm[:, :], start=True, stop=True).then_inc(s["q_ready"], 1)

                run(pe, body)

            @block.scalar
            def _(act):
                A = nc.scalar.activation
                nc.scalar.preload_act_table_set("natural_log_exp_and_others")

                def body(g, u, i, cur, nxt, prev, out):
                    un, uv = (u + 1) % 4, (u + 3) % 4
                    i_n = i + 1 if u == 3 else i
                    if nxt:
                        act.wait_ge(x_in[un], 16 * (i_n + 1))
                        wait(act, s["sq_ready"], g + 1)
                        A(squares[:, :], xs[:, un, :], ACT.Square).then_inc(s["squared"], 1)
                    if out:
                        act.wait_ge(s["proj_ready"], g - 1)
                        wait(act, s["token_done"], g - 2)
                        A(out_b[:, :], p_q[:, out_cols], ACT.Identity, bias=n.pb[:, :]).then_inc(s["out_biased"], 1)
                    if nxt:
                        act.wait_ge(s["mean_ready"], g + 2)
                        wait(act, s["var_done"], g + 1)
                        A(mean_sq[:, :], p_mean[:, :], ACT.Square).then_inc(s["mean_sq_done"], 1)
                        act.wait_ge(s["cent_ready"], g + 2)
                        wait(act, s["q_normed"], g + 1)
                        A(q_cent[:, :], p_q[:, cent_cols], ACT.Copy, scale=1.0 / WIN)
                        A(q_square[:, :], p_q[:, cent_cols], ACT.Square, scale=1.0 / WIN).then_inc(s["cent_copied"], 1)
                    for c in range(CH):
                        if prev:
                            act.wait_ge(s["wide_ready"], 4 * (g - 1) + c + 1)
                            wait(act, s["wv_done"], 4 * (g - 1) + c - 1)
                            A(w_wide[:, c % 2, :], p_w[:, :], ACT.Copy).then_inc(s["wide_copied"], 1)
                        if c == 0 and cur:
                            act.wait_ge(s["below_done"], g + 1)
                            wait(act, s["ex_rstd_done"], g)
                            wait(act, s["total_done"], g)
                            A(ex[:, :], below[:, :], ACT.Exp).then_inc(s["exp_done"], 1)
                        if c == 1 and nxt:
                            act.wait_ge(s["var_clamped"], g + 2)
                            wait(act, s["rstd_done"], g + 1)
                            A(var_log[:, :], var_pos[:, :], ACT.Ln, bias=K("eps")).then_inc(s["var_logged"], 1)
                            act.wait_ge(s["q_var_ready"], g + 2)
                            wait(act, s["q_rstd_done"], g + 1)
                            A(q_log[:, :], p_q[:, var_cols], ACT.Ln, bias=K("eps")).then_inc(s["q_log_done"], 1)
                            act.wait_ge(s["var_logged"], g + 2)
                            wait(act, s["ex_rstd_done"], g)
                            wait(act, s["scored"], g)
                            A(rstd[:, un % 2, :], var_log[:, :], ACT.Exp, scale=-0.5).then_inc(s["rstd_done"], 1)
                            act.wait_ge(s["q_log_done"], g + 2)
                            A(q_rstd[:, :], q_log[:, :], ACT.Exp, scale=-0.5).then_inc(s["q_rstd_done"], 1)
                    if cur:
                        act.wait_ge(s["weight_done"], g + 1)
                        wait(act, s["wide_ready"], 4 * (g - 1))
                        A(w_hi[:, u % 2, :], weight[:, :], ACT.Copy).then_inc(s["hi_done"], 1)
                    if nxt:
                        act.wait_ge(s["q_ready"], g + 2)
                        wait(act, s["qk_done"], 4 * g)
                        A(qs[:, un % 2, :], p_q[:, query_cols], ACT.Identity, bias=n.bq[:, :]).then_inc(s["q_copied"], 1)

                run(act, body)

            @block.vector
            def _(dve):
                V = nc.vector

                def gather(g, c, u):
                    dve.wait_ge(s["wv_done"], 4 * (g - 1) + c + 1)
                    if c == 0:
                        wait(dve, s["proj_ready"], g - 1)
                    V.tensor_reduce(chunk_windows(agg[:, :], c), wv[:, c % 2, :].rearrange("p (col row k) -> p col row k", col=16, row=2), X, ALU.add).then_inc(s["reduced"], 1)

                def body(g, u, i, cur, nxt, prev, out):
                    uv = (u + 3) % 4
                    if out:
                        gather(g - 1, CH - 1, u)
                    if cur:
                        dve.wait_ge(s["q_copied"], g + 1)
                        wait(dve, s["scores_ready"], g)
                        for c in range(CH):
                            dve.wait_ge(s["k_ready"], 4 * g + c + 1)
                            q = chunk_windows(qs[:, u % 2, :], c).unsqueeze(3).broadcast_to([P, 16, 2, WIN])
                            V.tensor_tensor(qk[:, c, :].rearrange("p (col row k) -> p col row k", col=16, row=2),
                                            p_kv[c % 3][:, :].rearrange("p (col row k) -> p col row k", col=16, row=2), q, ALU.mult).then_inc(s["qk_done"], 1)
                    if out:
                        dve.wait_ge(s["out_biased"], g - 1)
                        pair = 2 * i + (u - 2) // 2
                        V.scalar_tensor_tensor(n.tokens[:, pair, WG * (u % 2):WG * (u % 2) + WG], sums[:, (u + 2) % 4, :], 1.0 / WIN,
                                               out_b[:, :], ALU.mult, ALU.add).then_inc(s["token_done"], 1)
                    if cur:
                        dve.wait_ge(s["scores_ready"], g + 1)
                        dve.wait_ge(s["rstd_done"], g + 1)
                        V.tensor_tensor(score[:, :], p_score[:, :], rstd[:, u % 2, :], ALU.mult).then_inc(s["scored"], 1)
                        dve.wait_ge(s["scored"], g + 1)
                        V.tensor_reduce(top[:, :], by_window(score[:, :]), X, ALU.max).then_inc(s["top_done"], 1)
                        dve.wait_ge(s["top_done"], g + 1)
                        wait(dve, s["exp_done"], g)
                        V.tensor_tensor(by_window(below[:, :]), by_window(score[:, :]), top[:, :].unsqueeze(2).broadcast_to([P, WC, WIN]),
                                        ALU.subtract).then_inc(s["below_done"], 1)
                    if nxt:
                        dve.wait_ge(s["mean_sq_done"], g + 2)
                        dve.wait_ge(s["sq_ready"], g + 2)
                        wait(dve, s["var_clamped"], g + 1)
                        V.tensor_tensor(var[:, :], p_sq[:, :], mean_sq[:, :], ALU.subtract).then_inc(s["var_done"], 1)
                    for c in range(CH):
                        if prev:
                            dve.wait_ge(s["v_ready"], 4 * (g - 1) + c + 1)
                            dve.wait_ge(s["wide_copied"], 4 * (g - 1) + c + 1)
                            wait(dve, s["reduced"], 4 * (g - 1) + c - 1)
                            V.tensor_tensor(wv[:, c % 2, :], p_kv[(c + 1) % 3][:, :], w_wide[:, c % 2, :], ALU.mult).then_inc(s["wv_done"], 1)
                        if c == 0 and nxt:
                            dve.wait_ge(s["var_done"], g + 2)
                            wait(dve, s["var_logged"], g + 1)
                            V.tensor_scalar(var_pos[:, :], var[:, :], 0.0, None, ALU.max).then_inc(s["var_clamped"], 1)
                        if c == 0 and cur:
                            dve.wait_ge(s["exp_done"], g + 1)
                            V.tensor_reduce(total[:, :], by_window(ex[:, :]), X, ALU.add).then_inc(s["total_done"], 1)
                        if c == 1 and cur:
                            dve.wait_ge(s["total_done"], g + 1)
                            wait(dve, s["weight_done"], g)
                            V.reciprocal(inv[:, :], total[:, :]).then_inc(s["inv_done"], 1)
                        if prev and c < CH - 1:
                            gather(g, c, u)

                run(dve, body)

            @block.gpsimd
            def _(pool):
                G = nc.gpsimd

                def body(g, u, i, cur, nxt, prev, out):
                    un = (u + 1) % 4
                    i_n = i + 1 if u == 3 else i
                    if nxt:
                        pool.wait_ge(x_in[un], 16 * (i_n + 1))
                        a = xs[:, un, :].rearrange("p (y h row x) -> p y h row x", h=2, row=2, x=64)
                        t1 = tree1[:, :].rearrange("p (y row x) -> p y row x", row=2, x=64)
                        wait(pool, s["sums_2"], g + 1)
                        G.tensor_tensor(tree1[:, :].rearrange("p (y rowx) -> p y rowx", y=8), xs[:, un, :].rearrange("p (y h rowx) -> p y h rowx", h=2, rowx=128)[:, :, 0, :],
                                        xs[:, un, :].rearrange("p (y h rowx) -> p y h rowx", h=2, rowx=128)[:, :, 1, :], ALU.add).then_inc(s["sums_1"], 1)
                        pool.wait_ge(s["sums_1"], g + 2)
                        wait(pool, s["sums_3"], g + 1)
                        G.tensor_tensor(tree2[:, :].rearrange("p (y x) -> p y x", y=8), t1[:, :, 0, :], t1[:, :, 1, :], ALU.add).then_inc(s["sums_2"], 1)
                        pool.wait_ge(s["sums_2"], g + 2)
                        wait(pool, s["sums_done"], g + 1)
                        t2 = tree2[:, :].rearrange("p (col h x) -> p col h x", h=2, x=2)
                        G.tensor_tensor(tree3[:, :].rearrange("p (col x) -> p col x", x=2), t2[:, :, 0, :], t2[:, :, 1, :], ALU.add).then_inc(s["sums_3"], 1)
                        pool.wait_ge(s["sums_3"], g + 2)
                        wait(pool, s["token_done"], g - 2)
                        t3 = tree3[:, :].rearrange("p (col x) -> p col x", x=2)
                        G.tensor_tensor(sums[:, un, :], t3[:, :, 0], t3[:, :, 1], ALU.add).then_inc(s["sums_done"], 1)
                    if cur:
                        pool.wait_ge(s["exp_done"], g + 1)
                        wait(pool, s["weight_done"], g)
                        G.tensor_tensor(ex_rstd[:, :], ex[:, :], rstd[:, u % 2, :], ALU.mult).then_inc(s["ex_rstd_done"], 1)
                    if nxt:
                        pool.wait_ge(s["q_rstd_done"], g + 2)
                        wait(pool, s["q_ready"], g + 1)
                        G.tensor_tensor(q_norm[:, :], q_cent[:, :], q_rstd[:, :], ALU.mult).then_inc(s["q_normed"], 1)
                    if cur:
                        pool.wait_ge(s["inv_done"], g + 1)
                        pool.wait_ge(s["ex_rstd_done"], g + 1)
                        wait(pool, s["lo_done"], g)
                        G.tensor_tensor(by_window(weight[:, :]), by_window(ex_rstd[:, :]), inv[:, :].unsqueeze(2).broadcast_to([P, WC, WIN]),
                                        ALU.mult).then_inc(s["weight_done"], 1)
                        pool.wait_ge(s["hi_done"], g + 1)
                        wait(pool, s["wide_ready"], 4 * (g - 1))
                        G.tensor_tensor(w_lo[:, u % 2, :], weight[:, :], w_hi[:, u % 2, :], ALU.subtract).then_inc(s["lo_done"], 1)

                run(pool, body)

        zero(nc, [*s.values(), *x_in])


def mixing(nc, n):
    with ExitStack() as ctx:
        def sb(name, shape, dt=FP32):
            return ctx.enter_context(nc.sbuf_tensor(name, shape, dt))

        bank = [ctx.enter_context(nc.psum_tensor(f"mix{k}", [P, 512], FP32)) for k in range(8)]
        T3 = TOK // P
        R = 2 * T3
        p_cent, p_var, p_cent2, p_var2, p_kv0, p_kv1, p_q, p_kvkv = bank
        xn = sb("xn", [P, 4, TOK])
        sq1, log1, rstd1 = sb("sq1", [P, TOK]), sb("log1", [P, TOK]), sb("rstd1", [P, TOK])
        sq2, log2, rstd2 = sb("sq2", [P, TOK]), sb("log2", [P, TOK]), sb("rstd2", [P, TOK])
        xn2 = sb("xn2", [P, TOK])
        kv_sq = sb("kv_sq", [P, T3, 4 * C])
        kv_ss, kv_log, kv_std, kv_eased, kv_inv = (sb(x, [P, T3 * C]) for x in ("kv_ss", "kv_log", "kv_std", "kv_eased", "kv_inv"))
        kv_n, kv_w, kv_f = (sb(x, [P, T3, 4 * C]) for x in ("kv_n", "kv_w", "kv_f"))
        kv_m = sb("kv_m", [P, P])
        mixed = sb("mixed", [P, 2, TOK])
        q_sb, ret, gel = sb("q_sb", [P, TOK]), sb("ret", [P, TOK]), sb("gel", [P, TOK])
        rows = sb("rows", [P, 4, 2, R, ROW], U32)
        logits = sb("logits", [P, 2, R, E_N])
        eq, cand, lower = (sb(x, [P, R, E_N]) for x in ("eq", "cand", "lower"))
        eq2, cand2 = sb("eq2", [P, R, E_N]), sb("cand2", [P, R, E_N])
        top1, top2, no1, no2 = (sb(x, [P, R]) for x in ("top1", "top2", "no1", "no2"))
        hot = sb("hot", [P, 2, 2, R, E_N])
        hot16 = sb("hot16", [P, 2, R, E_N], FP16)
        gap = sb("gap", [P, 2, R])
        gap_exp, one_more = sb("gap_exp", [P, R]), sb("one_more", [P, R])
        gate = sb("gate_v", [P, 2, R])
        seat, seat_hot = sb("seat", [P, R, E_N]), sb("seat_hot", [P, 2, R, E_N])
        place = sb("place", [P, 2, R])
        place_i = sb("place_i", [P, 4, 2, R], U32)
        place_no = sb("place_no", [P, 2, 2, R])
        names = ("a_cent a_sq a_var a_log a_rstd a_xn a_added b_kv b_sq b_ss b_log b_std b_eased b_inv b_n b_w b_f "
                 "c_q c_qb c_kv c_kvm c_out c_ret c_proj c_gelu c_added d_cent d_sq d_var d_log d_rstd d_xn d_logits d_xt d_ht "
                 "d_hi d_lo d_hcopy d_biased e_top1 e_eq e_cand e_no1 e_hot1 e_lower e_top2 e_eq2 e_cand2 e_no2 e_hot2 e_hot16 e_gap "
                 "f_rank f_exp f_more f_gate1 f_gate2 f_seat f_seathot f_place f_placei f_meta f_base f_start f_meta_no f_go")
        s = {name: n.sem("m_" + name) for name in names.split()}
        sent = [n.sem(f"m_sent{k}") for k in range(4)]
        W = lambda name, rows=P: n.w[0:rows, W_AT[name][0]:W_AT[name][1]]
        K = lambda name: n.f[:, F32_AT[name][0]:F32_AT[name][1]]
        H16 = lambda name: n.h[:, F16_AT[name][0]:F16_AT[name][1]]
        STEPS = PAIRS + 5

        def uses_before(d, u):
            return d // 4 if isinstance(d, int) else (d - u % 4) // 4

        def run(engine, body):
            def static(j):
                body(j, j % 4, [0 <= j - k < PAIRS for k in range(6)])

            for j in range(8):
                static(j)
            with engine.Fori(2, PAIRS // 4) as i:
                for u in range(4):
                    body(4 * i + u, u, [True] * 6)
            for j in range(PAIRS, STEPS):
                static(j)

        with nc.Block() as block:
            @block.tensor
            def _(pe):
                mm = nc.tensor.matmul

                def body(j, u, on):
                    a, b, c, d, e, f = (j - k for k in range(6))
                    if on[2]:
                        wait(pe, s["c_ret"], c)
                        mm(p_q[:, 0:TOK], W("mq"), xn[:, (u - 2) % 4, :], start=True, stop=True).then_inc(s["c_q"], 1)
                        pe.wait_ge(s["b_f"], c + 1)
                        wait(pe, s["c_gelu"], c)
                        for t in range(T3):
                            last = mm(p_kvkv[:, 0:P], kv_f[:, t, 0:P], kv_f[:, t, P:2 * P], start=(t == 0), stop=(t == T3 - 1))
                        last.then_inc(s["c_kv"], 1)
                    if on[0]:
                        wait(pe, s["a_xn"], a)
                        mm(p_cent[:, 0:TOK], K("center"), n.tokens[:, a, :], start=True, stop=True).then_inc(s["a_cent"], 1)
                    if on[5]:
                        pe.wait_ge(s["e_hot16"], f + 1)
                        pe.wait_ge(s["d_biased"], f + 2 if on[4] else PAIRS)
                        hots = hot16[:, (u - 5) % 2, :, :].rearrange("p r e -> p (r e)")
                        mm(p_var2[:, 0:R * E_N], H16("before16"), hots, start=True, stop=False, skip_group_check=True)
                        for k in range(1, R):
                            mm(p_var2[:, E_N * k:R * E_N], H16("ones16"), hots[:, 0:(R - k) * E_N], start=False, stop=(k == R - 1),
                               skip_group_check=True)
                        for k in range(R):
                            last = mm(p_var2[:, R * E_N:(R + 1) * E_N], H16("ones16"), hots[:, E_N * k:E_N * k + E_N], start=False,
                                      stop=(k == R - 1), skip_group_check=True)
                        last.then_inc(s["f_rank"], 1)
                    if on[3]:
                        pe.wait_ge(s["c_added"], d + 1)
                        wait(pe, s["d_lo"], d)
                        mm(p_cent2[:, 0:TOK], K("center"), mixed[:, (u - 3) % 2, :], start=True, stop=True).then_inc(s["d_cent"], 1)
                    if on[0]:
                        pe.wait_ge(s["a_sq"], a + 1)
                        wait(pe, s["d_hcopy"], a - 3)
                        mm(p_var[:, 0:TOK], K("average"), sq1[:, :], start=True, stop=True).then_inc(s["a_var"], 1)
                    if on[2]:
                        pe.wait_ge(s["c_qb"], c + 1)
                        pe.wait_ge(s["c_kvm"], c + 1)
                        mm(p_q[:, 0:TOK], kv_m[:, :], q_sb[:, :], start=True, stop=True).then_inc(s["c_out"], 1)
                    if on[3]:
                        pe.wait_ge(s["d_sq"], d + 1)
                        wait(pe, s["d_biased"], d)
                        if on[5]:
                            pe.wait_ge(s["f_base"], f + 1)
                            pe.wait_ge(s["f_seat"], f + 1)
                        mm(p_var2[:, 0:TOK], K("average"), sq2[:, :], start=True, stop=True).then_inc(s["d_var"], 1)
                    if on[2]:
                        pe.wait_ge(s["c_ret"], c + 1)
                        mm(p_kvkv[:, 0:TOK], W("mproj"), ret[:, :], start=True, stop=True).then_inc(s["c_proj"], 1)
                    if on[3]:
                        wait(pe, s["a_log"], a + 1 if on[0] else PAIRS)
                        for t in range(T3):
                            last = nc.tensor.transpose(p_var[:, P * t:P * t + P], mixed[:, (u - 3) % 2, P * t:P * t + P], K("ident"))
                        last.then_inc(s["d_ht"], 1)
                        pe.wait_ge(s["d_xn"], d + 1)
                        for t in range(T3):
                            last = mm(p_var2[:, 32 * t:32 * t + 32], xn2[:, P * t:P * t + P], W("gate"), start=True, stop=True)
                        last.then_inc(s["d_logits"], 1)
                        for t in range(T3):
                            last = nc.tensor.transpose(p_cent2[:, P * t:P * t + P], xn2[:, P * t:P * t + P], K("ident"))
                        last.then_inc(s["d_xt"], 1)
                    if on[0]:
                        pe.wait_ge(s["a_xn"], a + 1)
                        wait(pe, s["b_n"], a)
                        for t in range(T3):
                            out = (p_kv0 if t < 2 else p_kv1)[:, 256 * (t % 2):256 * (t % 2) + 256]
                            mm(out, xn[:, u, P * t:P * t + P], n.mkv[:, :, :, :].rearrange("p a b c -> p (a b c)"),
                               start=True, stop=False)
                            last = mm(out, K("row_of_ones"), n.mkv_b[:, :, :, :].rearrange("p a b c -> p (a b c)"),
                                      start=False, stop=True)
                        last.then_inc(s["b_kv"], 1)

                run(pe, body)

            @block.scalar
            def _(act):
                A = nc.scalar.activation
                nc.scalar.preload_act_table_set("natural_log_exp_and_others")

                def body(j, u, on):
                    a, b, c, d, e, f = (j - k for k in range(6))
                    nc.scalar.preload_act_table_set("natural_log_exp_and_others")
                    if on[1]:
                        act.wait_ge(s["b_kv"], b + 1)
                        wait(act, s["b_ss"], b)
                        A(kv_sq[:, 0:2, :], p_kv0[:, :].rearrange("p (t c) -> p t c", t=2), ACT.Square)
                        A(kv_sq[:, 2, :], p_kv1[:, 0:4 * C], ACT.Square).then_inc(s["b_sq"], 1)
                    if on[2]:
                        act.wait_ge(s["c_q"], c + 1)
                        wait(act, s["c_out"], c)
                        A(q_sb[:, :], p_q[:, 0:TOK], ACT.Identity, bias=W("mq_b")).then_inc(s["c_qb"], 1)
                    if on[0]:
                        act.wait_ge(s["a_cent"], a + 1)
                        wait(act, s["a_var"], a)
                        A(sq1[:, :], p_cent[:, 0:TOK], ACT.Square).then_inc(s["a_sq"], 1)
                    if on[3]:
                        act.wait_ge(s["d_cent"], d + 1)
                        wait(act, s["d_var"], d)
                        A(sq2[:, :], p_cent2[:, 0:TOK], ACT.Square).then_inc(s["d_sq"], 1)
                    if on[5]:
                        act.wait_ge(s["e_gap"], f + 1)
                        wait(act, s["f_gate2"], f)
                        A(gap_exp[:, :], gap[:, (u - 5) % 2, :], ACT.Exp).then_inc(s["f_exp"], 1)
                    if on[0]:
                        act.wait_ge(s["a_var"], a + 1)
                        wait(act, s["a_rstd"], a)
                        A(log1[:, :], p_var[:, 0:TOK], ACT.Ln, bias=K("eps")).then_inc(s["a_log"], 1)
                    if on[1]:
                        act.wait_ge(s["b_ss"], b + 1)
                        wait(act, s["b_std"], b)
                        A(kv_log[:, :], kv_ss[:, :], ACT.Ln, bias=K("tiny"), scale=1.0 / 3.0).then_inc(s["b_log"], 1)
                    if on[0]:
                        act.wait_ge(s["a_log"], a + 1)
                        wait(act, s["a_xn"], a)
                        A(rstd1[:, :], log1[:, :], ACT.Exp, scale=-0.5).then_inc(s["a_rstd"], 1)
                    if on[1]:
                        act.wait_ge(s["b_log"], b + 1)
                        wait(act, s["b_eased"], b)
                        A(kv_std[:, :], kv_log[:, :], ACT.Exp, scale=0.5).then_inc(s["b_std"], 1)
                    if on[3]:
                        act.wait_ge(s["d_var"], d + 1)
                        wait(act, s["d_rstd"], d)
                        A(log2[:, :], p_var2[:, 0:TOK], ACT.Ln, bias=K("eps")).then_inc(s["d_log"], 1)
                    if on[1]:
                        act.wait_ge(s["b_std"], b + 1)
                        A(kv_eased[:, :], kv_std[:, :], ACT.Ln, bias=K("eps")).then_inc(s["b_eased"], 1)
                    if on[3]:
                        act.wait_ge(s["d_log"], d + 1)
                        wait(act, s["d_xn"], d)
                        A(rstd2[:, :], log2[:, :], ACT.Exp, scale=-0.5).then_inc(s["d_rstd"], 1)
                    if on[1]:
                        act.wait_ge(s["b_eased"], b + 1)
                        wait(act, s["b_n"], b)
                        A(kv_inv[:, :], kv_eased[:, :], ACT.Exp, scale=-1.0).then_inc(s["b_inv"], 1)
                    if on[2]:
                        act.wait_ge(s["c_proj"], c + 1)
                        wait(act, s["c_added"], c)
                        A(gel[:, :], p_kvkv[:, 0:TOK], ACT.Gelu, bias=W("mproj_b")).then_inc(s["c_gelu"], 1)
                    if on[3]:
                        act.wait_ge(s["d_ht"], d + 1)
                        A(n.tokens_t[:, bass.ds(d * R, R), :].rearrange("p (s t) c -> p t s c", s=2),
                          p_var[:, 0:TOK].rearrange("p (t s c) -> p t s c", t=T3, s=2), ACT.Copy).then_inc(s["d_hcopy"], 1)
                        act.wait_ge(s["d_xt"], d + 1)
                        slot = (u - 3) % 4
                        wait(act, sent[slot], 16 * 2 * R * uses_before(d, u - 3))
                        x3 = p_cent2[:, 0:TOK].rearrange("p (ts c) -> p ts c", c=C)
                        for k in range(2):
                            last = A(rows[:, slot, k, :, 0:C // 2].bitcast(FP16), x3, ACT.Copy, scale=X_SCALE)
                        last.then_inc(s["d_hi"], 1)

                run(act, body)

            @block.vector
            def _(dve):
                V = nc.vector
                V.tensor_copy(n.list_end[:, 1, :], K("list_base"))
                V.tensor_copy(place_no[:, 1, :, :], K("row_no").rearrange("p (k r) -> p k r", k=2)).then_inc(s["f_start"], 1)
                dve.wait_ge(s["f_start"], 1)
                wide = lambda t: t.unsqueeze(2).broadcast_to([P, R, E_N])
                rank = K("rank_e").unsqueeze(1).broadcast_to([P, R, E_N])

                def best_two(e, v):
                    def then(name, op):
                        op.then_inc(s[name], 1)
                        dve.wait_ge(s[name], e + 1)

                    then("e_top1", V.tensor_reduce(top1[:, :], logits[:, v, :, :], X, ALU.max))
                    then("e_eq", V.tensor_tensor(eq[:, :, :], logits[:, v, :, :], wide(top1[:, :]), ALU.is_equal))
                    then("e_cand", V.tensor_tensor(cand[:, :, :], eq[:, :, :], rank, ALU.mult))
                    then("e_no1", V.tensor_reduce(no1[:, :], cand[:, :, :], X, ALU.max))
                    wait(dve, s["f_seathot"], e - 1)
                    then("e_hot1", V.tensor_tensor(hot[:, v, 0, :, :], rank, wide(no1[:, :]), ALU.is_equal))
                    then("e_lower", V.scalar_tensor_tensor(lower[:, :, :], hot[:, v, 0, :, :], -1e30, logits[:, v, :, :], ALU.mult, ALU.add))
                    then("e_top2", V.tensor_reduce(top2[:, :], lower[:, :, :], X, ALU.max))
                    then("e_eq2", V.tensor_tensor(eq2[:, :, :], lower[:, :, :], wide(top2[:, :]), ALU.is_equal))
                    then("e_cand2", V.tensor_tensor(cand2[:, :, :], eq2[:, :, :], rank, ALU.mult))
                    then("e_no2", V.tensor_reduce(no2[:, :], cand2[:, :, :], X, ALU.max))
                    wait(dve, s["f_exp"], e - 1)
                    V.tensor_tensor(gap[:, v, :], top2[:, :], top1[:, :], ALU.subtract).then_inc(s["e_gap"], 1)
                    then("e_hot2", V.tensor_tensor(hot[:, v, 1, :, :], rank, wide(no2[:, :]), ALU.is_equal))
                    wait(dve, s["f_rank"], e - 1)
                    V.tensor_tensor(hot16[:, v, :, :], hot[:, v, 0, :, :], hot[:, v, 1, :, :], ALU.add).then_inc(s["e_hot16"], 1)

                def body(j, u, on):
                    a, b, c, d, e, f = (j - k for k in range(6))
                    ve, vf, wf = (u - 4) % 2, (u - 5) % 2, (u - 4) % 2
                    if on[2]:
                        dve.wait_ge(s["c_kv"], c + 1)
                        wait(dve, s["c_out"], c)
                        V.tensor_tensor(kv_m[:, :], p_kvkv[:, 0:P], K("mask4"), ALU.mult).then_inc(s["c_kvm"], 1)
                    if on[1]:
                        dve.wait_ge(s["b_sq"], b + 1)
                        wait(dve, s["b_log"], b)
                        V.tensor_reduce(kv_ss[:, :], kv_sq[:, :, :].rearrange("p t (g k) -> p (t g) k", k=4), X, ALU.add).then_inc(s["b_ss"], 1)
                    if on[5]:
                        dve.wait_ge(s["f_rank"], f + 1)
                        wait(dve, s["f_seathot"], f)
                        wait(dve, s["f_base"], f)
                        V.tensor_tensor(seat[:, :, :], p_var2[:, 0:R * E_N].rearrange("p (r e) -> p r e", r=R),
                                        n.list_end[:, wf, :].unsqueeze(1).broadcast_to([P, R, E_N]), ALU.add).then_inc(s["f_seat"], 1)
                        V.tensor_tensor(n.list_end[:, vf, :], p_var2[:, R * E_N:(R + 1) * E_N], n.list_end[:, wf, :], ALU.add).then_inc(s["f_base"], 1)
                        dve.wait_ge(s["f_seat"], f + 1)
                        wait(dve, s["f_place"], f)
                        for k in range(2):
                            last = V.tensor_tensor(seat_hot[:, k, :, :], seat[:, :, :], hot[:, vf, k, :, :], ALU.mult)
                        last.then_inc(s["f_seathot"], 1)
                        dve.wait_ge(s["f_exp"], f + 1)
                        wait(dve, s["f_gate1"], f)
                        V.tensor_scalar(one_more[:, :], gap_exp[:, :], 1.0, None, ALU.add).then_inc(s["f_more"], 1)
                        dve.wait_ge(s["f_seathot"], f + 1)
                        wait(dve, s["f_placei"], f)
                        V.tensor_reduce(place[:, :, :], seat_hot[:, :, :, :], X, ALU.add).then_inc(s["f_place"], 1)
                        dve.wait_ge(s["f_more"], f + 1)
                        wait(dve, s["f_meta"], f)
                        V.reciprocal(gate[:, 0, :], one_more[:, :]).then_inc(s["f_gate1"], 1)
                        dve.wait_ge(s["f_place"], f + 1)
                        V.tensor_copy(place_i[:, (u - 5) % 4, :, :], place[:, :, :]).then_inc(s["f_placei"], 1)
                        dve.wait_ge(s["f_gate1"], f + 1)
                        V.tensor_tensor(gate[:, 1, :], gate[:, 0, :], gap_exp[:, :], ALU.mult).then_inc(s["f_gate2"], 1)
                        wait(dve, s["f_meta_no"], f)
                        V.tensor_copy(rows[:, (u - 5) % 4, :, :, C:C + 1].rearrange("p k r o -> p k (r o)"), place_no[:, wf, :, :])
                        dve.wait_ge(s["f_gate2"], f + 1)
                        V.tensor_scalar(rows[:, (u - 5) % 4, :, :, C + 1:C + 2].rearrange("p k r o -> p k (r o)").bitcast(FP32), gate[:, :, :],
                                        1.0 / (X_SCALE * W_SCALE), None, ALU.mult).then_inc(s["f_meta"], 1)
                        V.tensor_scalar(place_no[:, vf, :, :], place_no[:, wf, :, :], float(2 * TOK), None, ALU.add).then_inc(s["f_meta_no"], 1)
                    if on[2]:
                        dve.wait_ge(s["c_out"], c + 1)
                        wait(dve, s["c_proj"], c)
                        V.tensor_tensor(ret[:, :], p_q[:, 0:TOK], xn[:, (u - 2) % 4, :], ALU.add).then_inc(s["c_ret"], 1)
                    if on[0]:
                        dve.wait_ge(s["a_rstd"], a + 1)
                        wait(dve, s["c_ret"], a - 3)
                        wait(dve, s["a_added"], a - 3)
                        V.tensor_tensor(xn[:, u, :], p_cent[:, 0:TOK], rstd1[:, :], ALU.mult).then_inc(s["a_xn"], 1)
                    if on[3]:
                        dve.wait_ge(s["d_rstd"], d + 1)
                        wait(dve, s["d_xt"], d)
                        V.tensor_tensor(xn2[:, :], p_cent2[:, 0:TOK], rstd2[:, :], ALU.mult).then_inc(s["d_xn"], 1)
                    if on[1]:
                        dve.wait_ge(s["b_inv"], b + 1)
                        wait(dve, s["b_w"], b)
                        half = P // 2
                        four = lambda t: t.rearrange("p (g k) -> p g k", k=4)
                        V.tensor_tensor(four(kv_n[:, 0:2, :].rearrange("p t c -> p (t c)")), four(p_kv0[:, :]),
                                        kv_inv[:, 0:P].unsqueeze(2).broadcast_to([P, P, 4]), ALU.mult)
                        V.tensor_tensor(four(kv_n[:, 2, :]), four(p_kv1[:, 0:4 * C]),
                                        kv_inv[:, P:P + half].unsqueeze(2).broadcast_to([P, half, 4]), ALU.mult).then_inc(s["b_n"], 1)
                    if on[0]:
                        dve.wait_ge(s["a_xn"], a + 1)
                        V.tensor_tensor(n.tokens[:, a, :], n.tokens[:, a, :], xn[:, u, :], ALU.add).then_inc(s["a_added"], 1)
                    if on[1]:
                        dve.wait_ge(s["b_n"], b + 1)
                        wait(dve, s["b_f"], b)
                        V.tensor_tensor(kv_w[:, :, :], kv_n[:, :, :], W("kv_ln_w").unsqueeze(1).broadcast_to([P, T3, 4 * C]), ALU.mult).then_inc(s["b_w"], 1)
                        dve.wait_ge(s["b_w"], b + 1)
                        wait(dve, s["c_kv"], b)
                        V.tensor_tensor(kv_f[:, :, :], kv_w[:, :, :], W("kv_ln_b").unsqueeze(1).broadcast_to([P, T3, 4 * C]), ALU.add).then_inc(s["b_f"], 1)
                    if on[2]:
                        dve.wait_ge(s["c_gelu"], c + 1)
                        dve.wait_ge(s["a_added"], c + 1)
                        wait(dve, s["d_ht"], c - 1)
                        V.tensor_tensor(mixed[:, u % 2, :], n.tokens[:, c, :], gel[:, :], ALU.add).then_inc(s["c_added"], 1)
                    if on[3]:
                        dve.wait_ge(s["d_logits"], d + 1)
                        wait(dve, s["e_lower"], d - 1)
                        V.tensor_tensor(logits[:, (u - 3) % 2, :, :].rearrange("p r e -> p (r e)").rearrange("p (t x) -> p t x", t=T3),
                                        p_var2[:, 0:R * E_N].rearrange("p (t x) -> p t x", t=T3),
                                        W("gate_b").unsqueeze(1).broadcast_to([P, T3, 2 * E_N]), ALU.add).then_inc(s["d_biased"], 1)
                    if on[3]:
                        dve.wait_ge(s["d_hi"], d + 1)
                        slot = (u - 3) % 4
                        for k in range(2):
                            last = V.scalar_tensor_tensor(rows[:, slot, k, :, C // 2:C].bitcast(FP16), p_cent2[:, 0:TOK].rearrange("p (ts c) -> p ts c", c=C),
                                                          X_SCALE, rows[:, slot, k, :, 0:C // 2].bitcast(FP16), ALU.mult, ALU.subtract)
                        last.then_inc(s["d_lo"], 1)
                    if on[4]:
                        best_two(e, ve)

                run(dve, body)

            @block.gpsimd
            def _(pool):
                G = nc.gpsimd

                def body(j, u, on):
                    f, slot = j - 5, (u - 5) % 4
                    if on[5]:
                        pool.wait_ge(s["f_meta"], f + 1)
                        pool.wait_ge(s["f_placei"], f + 1)
                        pool.wait_ge(s["d_lo"], f + 1)
                        pool.sem_inc(s["f_go"], 1)
                        for k in range(2):
                            for tile in range(R):
                                G.indirect_dma_start(out=n.lists, out_offset=bass.IndirectOffsetOnAxis(ap=place_i[:, slot, k, tile:tile + 1], axis=0),
                                                     in_=rows[:, slot, k, tile, :], in_offset=None).then_inc(sent[slot], 16)

                run(pool, body)
                for k in range(4):
                    pool.wait_ge(sent[k], 16 * 2 * R * (PAIRS // 4))


def experts(nc, n):
    with ExitStack() as ctx:
        def sb(name, shape, dt=FP32):
            return ctx.enter_context(nc.sbuf_tensor(name, shape, dt))

        J = 4
        GROUPS_E = -(-RUN_T // J)
        SLOTS = 8
        pad = sb("pad", [P, ROW], U32)
        count, tiles0, tiles = sb("count", [P, E_N]), sb("tiles0", [P, E_N]), sb("tiles", [P, E_N])
        cum = [sb(f"cum{k}", [P, E_N]) for k in range(5)]
        past, past_tiles = sb("past", [P, J, E_N]), sb("past_tiles", [P, J, E_N])
        first, which, clipped, tile_at, tile_in = (sb(x, [P, J]) for x in ("first", "which", "clipped", "tile_at", "tile_in"))
        expert, ids_wide, at_wide, words = sb("expert", [P, J]), sb("ids_wide", [P, J]), sb("at_wide", [P, J]), sb("words", [P, 3])
        plan = sb("plan_cols", [P, 3], I32)
        ends = sb("ends", [1, E_N], I32)
        plan_row = sb("plan_row", [1, 3, P], I32)
        rows = sb("x_rows", [P, SLOTS, J, ROW], U32)
        xt = sb("xt", [P, 2, J * P], FP16)
        act1 = sb("act1", [P, 2, J * P])
        hid = sb("hid", [P, 2, J * P])
        y = sb("y", [P, SLOTS, J, C])
        p_xt = [ctx.enter_context(nc.psum_tensor(f"p_xt{k}", [P, J * P], FP16)) for k in range(2)]
        p_h1 = [ctx.enter_context(nc.psum_tensor(f"p_h1_{k}", [P, J * P], FP32)) for k in range(2)]
        p_h2 = [ctx.enter_context(nc.psum_tensor(f"p_h2_{k}", [P, J * P], FP32)) for k in range(2)]
        p_y = [ctx.enter_context(nc.psum_tensor(f"p_y{k}", [P, J * C], FP32)) for k in range(2)]
        names = ("pad_zero pad_done planned plan_out plan_in pads_sent x_turned x_copied h1_ready h2_ready silu_done hid_done y_ready y_done y_go")
        s = {name: n.sem("x_" + name) for name in names.split()}
        rows_in = [n.sem(f"x_rows_in{k}") for k in range(SLOTS)]
        y_sent = [n.sem(f"x_y_sent{k}") for k in range(SLOTS)]
        K = lambda name: n.f[:, F32_AT[name][0]:F32_AT[name][1]]

        with nc.Block() as block:
            @block.gpsimd
            def _(pool):
                nc.gpsimd.memset(pad[:, :], 0).then_inc(s["pad_zero"], 1)

            @block.vector
            def _(dve):
                V = nc.vector
                step = [0]

                def then(op):
                    step[0] += 1
                    op.then_inc(s["planned"], 1)
                    dve.wait_ge(s["planned"], step[0])

                dve.wait_ge(s["pad_zero"], 1)
                V.tensor_copy(pad[:, C:C + 1], K("pad_place")).then_inc(s["pad_done"], 1)
                then(V.tensor_copy(ends[:, :], n.list_end[0:1, 1, :]))
                then(V.tensor_tensor(count[:, :], n.list_end[:, 1, :], K("list_base"), ALU.subtract))
                then(V.tensor_scalar(tiles0[:, :], count[:, :], 1.0 / P, float(P - 1) / P - 255.0 / 512.0, ALU.mult, ALU.add))
                then(V.tensor_scalar(tiles[:, :], tiles0[:, :], MAGIC, -MAGIC, ALU.add, ALU.add))
                then(V.tensor_copy(cum[0][:, :], tiles[:, :]))
                for k in range(4):
                    d = 1 << k
                    V.tensor_copy(cum[k + 1][:, 0:d], cum[k][:, 0:d])
                    then(V.tensor_tensor(cum[k + 1][:, d:E_N], cum[k][:, d:E_N], cum[k][:, 0:E_N - d], ALU.add))
                then(V.tensor_tensor(past[:, :, :], K("tile_no").unsqueeze(2).broadcast_to([P, J, E_N]),
                                     cum[4][:, :].unsqueeze(1).broadcast_to([P, J, E_N]), ALU.is_ge))
                then(V.tensor_tensor(past_tiles[:, :, :], past[:, :, :], tiles[:, :].unsqueeze(1).broadcast_to([P, J, E_N]), ALU.mult))
                then(V.tensor_reduce(which[:, :], past[:, :, :], X, ALU.add))
                then(V.tensor_reduce(first[:, :], past_tiles[:, :, :], X, ALU.add))
                then(V.tensor_tensor(tile_in[:, :], K("tile_no"), first[:, :], ALU.subtract))
                then(V.scalar_tensor_tensor(tile_at[:, :], which[:, :], float(LIST_T), tile_in[:, :], ALU.mult, ALU.add))
                then(V.tensor_scalar(clipped[:, :], tile_at[:, :], float(E_N * LIST_T), None, ALU.min))
                then(V.tensor_scalar(expert[:, :], which[:, :], float(E_N - 1), None, ALU.min))
                then(V.tensor_tensor(ids_wide[:, :], expert[:, :], K("id_unit"), ALU.mult))
                then(V.tensor_tensor(at_wide[:, :], clipped[:, :], K("at_unit"), ALU.mult))
                then(V.tensor_reduce(words[:, 0:1], ids_wide[:, :], X, ALU.add))
                then(V.tensor_reduce(words[:, 1:3], at_wide[:, :].rearrange("p (a b) -> p a b", b=2), X, ALU.add))
                then(V.tensor_copy(plan[:, :], words[:, :]))

            @block.sync
            def _(sp):
                sp.wait_ge(s["pad_done"], 1)
                sp.wait_ge(s["planned"], PLAN_OPS)
                for k in range(3):
                    sp.dma_start(n.plan[k].rearrange("(p o) -> p o", o=1), plan[:, k:k + 1]).then_inc(s["plan_out"], 16)
                sp.wait_ge(s["plan_out"], 16 * 3)
                sp.dma_start(plan_row[:, :, :], n.plan.rearrange("(o k) t -> o k t", o=1)).then_inc(s["plan_in"], 16)
                sp.dma_start(n.lists[E_N * LIST:E_N * LIST + P, :], pad[:, :]).then_inc(s["pads_sent"], 16)
                for e in range(E_N):
                    end = sp.value_load(ends[0:1, e:e + 1], min_val=0, max_val=E_N * LIST)
                    sp.dma_start(n.lists[bass.ds(end, P), :], pad[:, :]).then_inc(s["pads_sent"], 16)
                sp.wait_ge(s["pads_sent"], 16 * (E_N + 1))
                sp.wait_ge(s["plan_in"], 16)


        with nc.Block() as block:
            def run(engine, body):
                for g in range(-1, SLOTS):
                    body(g, g % SLOTS, g // SLOTS, True, g >= 0, g >= 1)
                with engine.Fori(1, (GROUPS_E - 1) // SLOTS) as i:
                    for u in range(SLOTS):
                        body(SLOTS * i + u, u, i, True, True, True)
                for g in range((GROUPS_E - 1) // SLOTS * SLOTS, GROUPS_E + 1):
                    body(g, g % SLOTS, g // SLOTS, g < GROUPS_E - 1, g < GROUPS_E, True)

            @block.sync
            def _(sp):
                def load(g, u, i):
                    wait(sp, y_sent[u], 16 * J * i)
                    for k in range(2):
                        two = sp.value_load(plan_row[0:1, 1 + k, bass.ds(g, 1)], min_val=0, max_val=E_N * LIST_T * (AT_UNIT + 1))
                        for j, at in enumerate((two % AT_UNIT, two // AT_UNIT)):
                            sp.dma_start(rows[:, u, 2 * k + j, :], n.lists[bass.ds(at * P, P), :]).then_inc(rows_in[u], 16)

                for g in range(SLOTS):
                    load(g, g, 0)
                with sp.Fori(1, GROUPS_E // SLOTS) as i:
                    for u in range(SLOTS):
                        load(SLOTS * i + u, u, i)
                for g in range(GROUPS_E // SLOTS * SLOTS, GROUPS_E):
                    load(g, g % SLOTS, g // SLOTS)

            @block.tensor
            def _(pe):
                mm = nc.tensor.matmul

                def experts_of(g):
                    four = pe.value_load(plan_row[0:1, 0, bass.ds(g, 1)], min_val=0, max_val=E_N ** 4 - 1)
                    return [(four // E_N ** j) % E_N for j in range(J)]

                loaded = {}

                def body(g, u, i, nxt, cur, prev):
                    v = u % 2
                    if nxt:
                        un, i_n = (u + 1) % SLOTS, i + 1 if u == SLOTS - 1 else i
                        pe.wait_ge(rows_in[un], 16 * J * (i_n + 1))
                        wait(pe, s["x_copied"], g)
                        for j in range(J):
                            last = nc.tensor.transpose(p_xt[1 - v][:, P * j:P * j + P], rows[:, un, j, 0:C].bitcast(FP16),
                                                       n.h[:, F16_AT["ident16"][0]:F16_AT["ident16"][1]])
                        last.then_inc(s["x_turned"], 1)
                    if cur:
                        pe.wait_ge(s["x_copied"], g + 1)
                        wait(pe, s["silu_done"], g - 1)
                        chosen = loaded[u] = experts_of(g)
                        for j, e in enumerate(chosen):
                            for part in range(2):
                                last = mm(p_h1[v][:, P * j:P * j + P], n.w12[:, bass.ds(e, 1), 0, part, :].rearrange("p o h -> p (o h)"),
                                          xt[:, v, P * j:P * j + P], start=(part == 0), stop=(part == 1))
                        last.then_inc(s["h1_ready"], 1)
                        wait(pe, s["hid_done"], g - 1)
                        for j, e in enumerate(chosen):
                            for part in range(2):
                                last = mm(p_h2[v][:, P * j:P * j + P], n.w12[:, bass.ds(e, 1), 1, part, :].rearrange("p o h -> p (o h)"),
                                          xt[:, v, P * j:P * j + P], start=(part == 0), stop=(part == 1))
                        last.then_inc(s["h2_ready"], 1)
                    if prev:
                        pe.wait_ge(s["hid_done"], g)
                        wait(pe, s["y_done"], g - 2)
                        for j, e in enumerate(loaded[u - 1] if u else experts_of(g - 1)):
                            last = mm(p_y[1 - v][:, C * j:C * j + C], hid[:, 1 - v, P * j:P * j + P], n.w[:, bass.ds(e * C + W_AT["w3"][0], C)],
                                      start=True, stop=True)
                        last.then_inc(s["y_ready"], 1)

                run(pe, body)

            @block.scalar
            def _(act):
                A = nc.scalar.activation

                def body(g, u, i, nxt, cur, prev):
                    if cur:
                        act.wait_ge(s["h1_ready"], g + 1)
                        wait(act, s["hid_done"], g - 1)
                        A(act1[:, u % 2, :], p_h1[u % 2][:, :], ACT.Silu, scale=1.0 / (X_SCALE * W_SCALE)).then_inc(s["silu_done"], 1)

                run(act, body)

            @block.vector
            def _(dve):
                V = nc.vector

                def body(g, u, i, nxt, cur, prev):
                    v = u % 2
                    if nxt:
                        dve.wait_ge(s["x_turned"], g + 2)
                        wait(dve, s["h2_ready"], g)
                        V.tensor_copy(xt[:, 1 - v, :], p_xt[1 - v][:, :]).then_inc(s["x_copied"], 1)
                    if prev:
                        up = (u - 1) % SLOTS
                        dve.wait_ge(s["y_ready"], g)
                        V.tensor_tensor(y[:, up, :, :], p_y[1 - v][:, :].rearrange("p (j c) -> p j c", j=J),
                                        rows[:, up, :, C + 1:C + 2].bitcast(FP32).broadcast_to([P, J, C]), ALU.mult).then_inc(s["y_done"], 1)
                    if cur:
                        dve.wait_ge(s["silu_done"], g + 1)
                        dve.wait_ge(s["h2_ready"], g + 1)
                        wait(dve, s["y_ready"], g - 1)
                        V.tensor_tensor(hid[:, v, :], p_h2[v][:, :], act1[:, v, :], ALU.mult).then_inc(s["hid_done"], 1)

                run(dve, body)

            @block.gpsimd
            def _(pool):
                def body(g, u, i, nxt, cur, prev):
                    if prev:
                        up = (u - 1) % SLOTS
                        pool.wait_ge(s["y_done"], g)
                        pool.sem_inc(s["y_go"], 1)
                        for j in range(J):
                            nc.gpsimd.indirect_dma_start(out=n.expert_rows, out_offset=bass.IndirectOffsetOnAxis(ap=rows[:, up, j, C:C + 1], axis=0),
                                                         in_=y[:, up, j, :], in_offset=None, bounds_check=2 * B * TOK - 1,
                                                         oob_is_err=False).then_inc(y_sent[up], 16)

                run(pool, body)
                for u in range(SLOTS):
                    pool.wait_ge(y_sent[u], 16 * J * ((GROUPS_E - u + SLOTS - 1) // SLOTS))


PLAN_OPS = 22


def combine(nc, n):
    with ExitStack() as ctx:
        J = 16
        N = TILES_TOK // J
        a = ctx.enter_context(nc.sbuf_tensor("from_experts", [P, 2, 2, J, C], FP32))
        t = ctx.enter_context(nc.sbuf_tensor("one_added", [P, 2, J, C], FP32))
        o = ctx.enter_context(nc.sbuf_tensor("both_added", [P, 2, J, C], FP32))
        rows_in = [n.sem(f"z_rows_in{k}") for k in range(2)]
        out_done = [n.sem(f"z_out_done{k}") for k in range(2)]
        added1, added2 = n.sem("z_added1"), n.sem("z_added2")
        src = n.expert_rows.rearrange("(k m j p) c -> m k p j c", k=2, m=N, p=P)
        dst = n.out.rearrange("b t c -> (b t) c").rearrange("(m j p) c -> m p j c", m=N, p=P)
        with nc.Block() as block:
            @block.sync
            def _(sp):
                for m in range(N):
                    wait(sp, added2, m - 1)
                    for k in range(2):
                        sp.dma_start(a[:, m % 2, k, :, :], src[m, k]).then_inc(rows_in[m % 2], 16)

            @block.vector
            def _(dve):
                for m in range(N):
                    v = m % 2
                    dve.wait_ge(rows_in[v], 32 * (m // 2 + 1))
                    nc.vector.tensor_tensor(t[:, v, :, :], a[:, v, 0, :, :], a[:, v, 1, :, :], ALU.add).then_inc(added1, 1)
                    dve.wait_ge(added1, m + 1)
                    wait(dve, out_done[v], 16 * (m // 2))
                    nc.vector.tensor_tensor(o[:, v, :, :], t[:, v, :, :], n.tokens_t[:, J * m:J * m + J, :], ALU.add).then_inc(added2, 1)

            @block.scalar
            def _(act):
                for m in range(N):
                    act.wait_ge(added2, m + 1)
                    act.dma_start(dst[m], o[:, m % 2, :, :]).then_inc(out_done[m % 2], 16)
                for v in range(2):
                    act.wait_ge(out_done[v], 16 * (N // 2))



def build(nc, ins, out):
    n = Names()
    n.in_weights, n.in_f32, n.in_f16 = ins["weights"], ins["f32"], ins["f16"]
    n.in_w1, n.in_w2, n.in_x, n.in_ids, n.in_pos = ins["w1"], ins["w2"], ins["x"], ins["ids"], ins["pos"]
    with ExitStack() as ctx:
        def sb(name, shape, dt=FP32):
            return ctx.enter_context(nc.sbuf_tensor(name, shape, dt))

        n.sem = lambda name: ctx.enter_context(nc.semaphore(name))
        n.w = sb("w", [P, W_N])
        n.f = sb("f", [P, F32_N])
        n.h = sb("h16", [P, F16_N], FP16)
        n.wk, n.wv, n.wq = sb("wk", [P, P]), sb("wv", [P, P]), sb("wq", [P, P])
        n.bq, n.pb = sb("bq", [P, 1]), sb("pb_bias", [P, 1])
        n.mkv, n.mkv_b = sb("mkv", [P, 2, 2, C]), sb("mkv_b", [P, 2, 2, C])
        n.w12 = sb("w12", [P, E_N, 2, 2, HID], FP16)
        n.tokens = sb("tokens", [P, PAIRS, TOK])
        n.lists = nc.dram_tensor("lists", (LISTS * P, ROW), U32, kind="Internal").ap()
        n.expert_rows = nc.dram_tensor("expert_rows", (2 * B * TOK, C), FP32, kind="Internal").ap()
        n.plan = nc.dram_tensor("plan", (3, P), I32, kind="Internal").ap()
        n.out = out
        constants(nc, n)
        text(nc, n)
        windows(nc, n)
        n.tokens_t = sb("tokens_t", [P, TILES_TOK, C])
        n.list_end = sb("list_end", [P, 2, E_N])
        mixing(nc, n)
        experts(nc, n)
        combine(nc, n)


def inputs_of(g):
    f, h = shape_constants()
    return {"weights": pack_weights(g), "f32": f, "f16": h, "w1": g["L0_ffn_w1"], "w2": g["L0_ffn_w2"],
            "x": g["x"].reshape(B, C, PIX), "ids": g["x_txt"].reshape(1, B * TXT_T),
            "pos": g["fside_BS_continuous_positions"].reshape(1, B * TXT_T)}


def kernel(**inputs):
    from concourse import bacc
    from concourse.bass_utils import run_bass_kernel_spmd

    nc = bacc.Bacc("TRN2", target_bir_lowering=False, num_devices=1)
    arrays, ins = {}, {}
    for name, value in inputs_of({k: np.asarray(v) for k, v in inputs.items()}).items():
        arrays["in_" + name] = np.ascontiguousarray(value)
        ins[name] = nc.dram_tensor("in_" + name, value.shape, mybir.dt.from_np(value.dtype), kind="ExternalInput").ap()
    out = nc.dram_tensor("out_h", (B, TOK, C), FP32, kind="ExternalOutput").ap()
    build(nc, ins, out)
    result = run_bass_kernel_spmd(nc, [arrays], core_ids=[0])
    return result.results[0]["out_h"]
```

```python
from contextlib import ExitStack

import numpy as np
import concourse.bass as bass
from concourse import mybir

FP32 = mybir.dt.float32
FP16 = mybir.dt.float16
I32 = mybir.dt.int32
U32 = mybir.dt.uint32
ACT = mybir.ActivationFunctionType
ALU = mybir.AluOpType
X = mybir.AxisListType.X

B = 64
C = 64
P = 128
PAIRS = B // 2
PIX = 64 * 64
WIN = 16
IMG_T = PIX // WIN
TXT_T = 128
TOK = IMG_T + TXT_T
HEADS = 8
EPS = 1e-5

GROUP = 2048
GROUPS = B * PIX // 2 // GROUP
CHUNK = 512
CH = GROUP // CHUNK
WG = GROUP // WIN
WC = CHUNK // WIN

E_N = 16
HID = 128
TILES_TOK = B * TOK // P
PLAN_OPS = 22
LIST_T = TILES_TOK + 1
LIST = LIST_T * P
LISTS = E_N * LIST_T + 1
RUN_T = 2 * TILES_TOK + E_N
PER_GROUP = 4
ROW = 66
X_SCALE = 32.0
W_SCALE = 64.0
AT_UNIT = LISTS
MAGIC = 12582912.0


class Names:
    pass


def wait(engine, sem, value):
    if isinstance(value, int) and value <= 0:
        return
    engine.wait_ge(sem, value)


def zero(nc, sems):
    with nc.Block() as block:
        @block.gpsimd
        def _(pool):
            for sem in sems:
                pool.sem_clear(sem)



F32_PARTS = [("ident", 128), ("center", 128), ("average", 128), ("mean32", 32), ("head32", 32),
             ("center4", 64), ("mask4", 128), ("byte_pos", 1), ("eps", 1), ("tiny", 1), ("rank_e", 16),
             ("list_base", 16), ("pad_place", 1), ("tile_no", 4), ("id_unit", 4), ("at_unit", 4), ("row_no", 12), ("vocab", 1), ("row_of_ones", 128), ("low_rows", 1)]
F16_PARTS = [("ident16", 128), ("ones16", 128), ("before16", 128), ("spread16", 4 * 128)]


def columns(parts):
    at, out = 0, {}
    for name, n in parts:
        out[name] = (at, at + n)
        at += n
    return out, at


F32_AT, F32_N = columns(F32_PARTS)
F16_AT, F16_N = columns(F16_PARTS)


def shape_constants():
    two = np.eye(2)
    f = np.zeros((P, F32_N), np.float32)
    h = np.zeros((P, F16_N), np.float16)

    def put(name, value):
        a, b = F32_AT[name]
        f[:value.shape[0], a:b] = value

    p = np.arange(P)
    put("ident", np.eye(P))
    put("center", np.kron(two, np.eye(C) - 1.0 / C))
    put("average", np.kron(two, np.full((C, C), 1.0 / C)))
    mean32 = np.zeros((P, 32))
    head32 = np.zeros((P, 32))
    for s in range(2):
        for head in range(HEADS):
            for part in range(2):
                mean32[s * C:(s + 1) * C, 16 * part + s * HEADS + head] = 1.0 / C
                head32[s * C + head * 8:s * C + head * 8 + 8, 16 * part + s * HEADS + head] = 1.0
    put("mean32", mean32)
    put("head32", head32)
    put("center4", np.kron(np.eye(16), np.eye(4) - 0.25))
    put("mask4", np.kron(np.eye(32), np.full((4, 4), 1.0 / TOK)))
    put("byte_pos", np.linspace(0.0, 1.0, TXT_T, dtype=np.float32)[:, None])
    put("eps", np.full((P, 1), EPS))
    put("tiny", np.full((P, 1), 1e-30))
    put("list_base", np.tile(np.arange(E_N) * LIST, (P, 1)))
    put("pad_place", np.full((P, 1), 2 * B * TOK + 1.0))
    put("tile_no", 4 * p[:, None] + np.arange(4)[None, :])
    put("id_unit", np.tile(float(E_N) ** np.arange(4), (P, 1)))
    put("at_unit", np.tile([1.0, AT_UNIT, 1.0, AT_UNIT], (P, 1)))
    put("rank_e", np.tile(E_N - np.arange(E_N), (P, 1)))
    k, t, smp = np.meshgrid(np.arange(2), np.arange(TOK // P), np.arange(2), indexing="ij")
    put("row_no", TOK // P * p[:, None] + (k * B * TOK + smp * TOK + t).reshape(1, -1))
    put("vocab", (p % 64)[:, None])
    put("low_rows", (p // 16 % 2)[:, None])
    put("row_of_ones", np.ones((1, P)))
    for name, value in (("ident16", np.eye(P)), ("ones16", np.ones((P, P))),
                        ("before16", (p[:, None] < p[None, :]))):
        a, b = F16_AT[name]
        h[:, a:b] = value
    a, _ = F16_AT["spread16"]
    for c in range(CH):
        for s in range(2):
            for head in range(HEADS):
                col = a + P * c + s * C + head * 8
                for part in range(2):
                    h[32 * c + 16 * part + s * HEADS + head, col:col + 8] = 1.0
    return f, h


W_PARTS = [("wk", 128), ("wv", 128), ("wq", 128), ("proj", 128),
           ("kv_scale", 1), ("kv_shift", 1), ("q_scale", 1), ("q_shift", 1), ("proj_b", 1),
           ("mk", 128), ("mv", 128), ("mk_b", 1), ("mv_b", 1), ("mq", 128), ("mq_b", 1),
           ("mproj", 128), ("mproj_b", 1), ("kv_ln_w", 256), ("kv_ln_b", 256),
           ("gate", 32), ("gate_b", 32), ("w3", E_N * C),
           ("c1", 4 * 128), ("c1_b", 1), ("c2", 5 * 64), ("c2_b", 1), ("c3", 3 * 2), ("c3_b", 1),
           ("embed", 68), ("widths", 4), ("scales", 4)]
W_AT, W_N = columns(W_PARTS)


def pack_weights(g):
    w = np.zeros((P, W_N), np.float32)

    def put(name, value, rows=slice(None)):
        a, b = W_AT[name]
        w[rows, a:b] = value

    def both(name, matrix):
        a, b = W_AT[name]
        n = (b - a) // 2
        w[:C, a:a + n] = matrix
        w[C:, a + n:b] = matrix

    def column(name, vector):
        put(name, np.tile(vector, P // vector.shape[0])[:, None])

    both("wk", g["L0_tok_Wkv"][:C].T)
    both("wv", g["L0_tok_Wkv"][C:].T)
    both("wq", g["L0_tok_Wq"].T)
    both("proj", g["L0_tok_proj_w"].T)
    column("kv_scale", g["L0_tok_ln_kv_w"])
    column("kv_shift", g["L0_tok_ln_kv_b"])
    column("q_scale", g["L0_tok_ln_q_w"])
    column("q_shift", g["L0_tok_ln_q_b"])
    column("proj_b", g["L0_tok_proj_b"])
    qkv = g["L0_attn_W_qkv"].reshape(16, 3, 4, C)
    qkv_b = g["L0_attn_b_qkv"].reshape(16, 3, 4)
    for name, part in (("mk", 1), ("mv", 2)):
        put(name, np.tile(qkv[:, part].reshape(C, C), (1, 2)), slice(0, C))
        put(name + "_b", qkv_b[:, part].reshape(C, 1), slice(0, C))
    both("mq", qkv[:, 0].reshape(C, C).T)
    column("mq_b", qkv_b[:, 0].reshape(C))
    both("mproj", g["L0_attn_W_proj"].T)
    column("mproj_b", g["L0_attn_b_proj"])
    for name, k, v in (("kv_ln_w", "L0_attn_kln_w", "L0_attn_vln_w"), ("kv_ln_b", "L0_attn_kln_b", "L0_attn_vln_b")):
        put(name, np.concatenate([np.tile(g[k].reshape(C), 2), np.tile(g[v].reshape(C), 2)])[None, :])
    both("gate", g["L0_ffn_gate_w"])
    put("gate_b", np.tile(g["L0_ffn_gate_b"], 2)[None, :])
    put("w3", g["L0_ffn_w3"].transpose(1, 0, 2).reshape(HID, E_N * C))
    taps = np.zeros((2, C, 4, 128), np.float32)
    w1 = g["L0_txt_w1"]
    for tap in range(7):
        taps[tap % 2, :, tap // 2] = w1[:, :, tap].T
    put("c1", taps.reshape(P, 4 * 128))
    column("c1_b", g["L0_txt_b1"])
    put("c2", g["L0_txt_w2"].transpose(1, 2, 0).reshape(P, 5 * C))
    column("c2_b", g["L0_txt_b2"])
    c3 = np.zeros((2, C, 3, 2), np.float32)
    for s in range(2):
        c3[s, :, :, s] = g["L0_txt_w3"][0]
    put("c3", c3.reshape(P, 6))
    put("c3_b", g["L0_txt_b3"][0])
    put("embed", np.concatenate([g["L0_txt_emb"], g["L0_txt_locality_shapes"]], axis=1), slice(0, C))
    put("widths", g["L0_txt_multiscale_widths"][None, :])
    put("scales", g["L0_txt_scale_weights"][None, :])
    return w


def constants(nc, n):
    with ExitStack() as ctx:
        raw = ctx.enter_context(nc.sbuf_tensor("raw12", [P, 2, E_N * HID], FP32))
        scaled = ctx.enter_context(nc.sbuf_tensor("scaled", [P, 3, 128], FP32))
        bias_rows = ctx.enter_context(nc.sbuf_tensor("bias_rows", [C, 2, 128], FP32))
        v_bias = ctx.enter_context(nc.sbuf_tensor("v_bias", [P, 1], FP32))
        pw = ctx.enter_context(nc.psum_tensor("pw", [P, 512], FP32))
        pm = ctx.enter_context(nc.psum_tensor("pm", [P, 512], FP32))
        pb = ctx.enter_context(nc.psum_tensor("pb", [P, 8], FP32))
        weights_in = n.sem("weights_in")
        w12_in = [n.sem(f"w12_in{k}") for k in range(2)]
        scaled_rows, w_products, vb_copied = (n.sem(x) for x in ("scaled_rows", "w_products", "vb_copied"))
        pb_product, w12_high = n.sem("pb_product"), n.sem("w12_high")
        w, f = n.w, n.f

        def W(name, rows=P):
            a, b = W_AT[name]
            return w[0:rows, a:b]

        def K(name, rows=P):
            a, b = F32_AT[name]
            return f[0:rows, a:b]

        with nc.Block() as block:
            @block.sync
            def _(sp):
                sp.dma_start(w[:, :], n.in_weights).then_inc(weights_in, 16)
                sp.dma_start(f[:, :], n.in_f32).then_inc(weights_in, 16)
                sp.dma_start(n.h[:, :], n.in_f16).then_inc(weights_in, 16)
                for which, src in enumerate((n.in_w1, n.in_w2)):
                    for half in range(2):
                        sp.dma_start(raw[half * C:(half + 1) * C, which, :].rearrange("c (e j) -> c e j", e=E_N),
                                     src.rearrange("e c j -> c e j")).then_inc(w12_in[which], 16)

            @block.vector
            def _(dve):
                dve.wait_ge(weights_in, 48)
                nc.vector.tensor_scalar(scaled[:, 0, :], W("wk"), W("kv_scale"), None, ALU.mult).then_inc(scaled_rows, 1)
                nc.vector.tensor_scalar(scaled[:, 1, :], W("wv"), W("kv_scale"), None, ALU.mult).then_inc(scaled_rows, 1)
                nc.vector.tensor_scalar(n.wq[:, :], W("wq"), W("q_scale"), 0.125, ALU.mult, ALU.mult)
                nc.vector.tensor_scalar(scaled[:, 2, :], W("wq"), 0.125, None, ALU.mult).then_inc(scaled_rows, 1)
                for i, name in enumerate(("mk_b", "mv_b")):
                    nc.vector.tensor_scalar(bias_rows[:, i, :], f[0:C, F32_AT["average"][0]:F32_AT["average"][1]], 0.0,
                                            W(name, C), ALU.mult, ALU.add).then_inc(scaled_rows, 1)
                dve.wait_ge(w_products, 1)
                nc.vector.tensor_copy(n.wk[:, :], pw[:, 0:128])
                nc.vector.tensor_copy(n.wv[:, :], pw[:, 128:256])
                nc.vector.memset(n.mkv[:, :, :, :], 0.0).then_inc(vb_copied, 1)
                dve.wait_ge(vb_copied, 1)
                for s in range(2):
                    nc.vector.tensor_copy(n.mkv[s * C:(s + 1) * C, :, s, :],
                                          pm[s * C:(s + 1) * C, 0:128].rearrange("p (a c) -> p a c", a=2))
                    nc.vector.tensor_copy(n.mkv_b[:, :, s, :], pm[:, 128:256].rearrange("p (a c) -> p a c", a=2))
                nc.vector.tensor_copy(n.bq[:, :], pw[:, 256:257])
                nc.vector.tensor_copy(v_bias[:, :], pw[:, 257:258]).then_inc(vb_copied, 1)
                dve.wait_ge(pb_product, 1)
                nc.vector.tensor_tensor(n.pb[:, :], pb[:, 0:1], W("proj_b"), ALU.add)
                for which in range(2):
                    dve.wait_ge(w12_high, which + 1)
                    nc.vector.scalar_tensor_tensor(n.w12[:, :, which, 1, :], raw[:, which, :].rearrange("p (e j) -> p e j", e=E_N), W_SCALE,
                                                   n.w12[:, :, which, 0, :], ALU.mult, ALU.subtract)

            @block.scalar
            def _(act):
                for which in range(2):
                    act.wait_ge(w12_in[which], 32)
                    nc.scalar.activation(n.w12[:, :, which, 0, :], raw[:, which, :].rearrange("p (e j) -> p e j", e=E_N), ACT.Copy,
                                         scale=W_SCALE).then_inc(w12_high, 1)

            @block.tensor
            def _(pe):
                pe.wait_ge(weights_in, 48)
                pe.wait_ge(scaled_rows, 5)
                nc.tensor.matmul(pw[:, 0:128], K("center"), scaled[:, 0, :], start=True, stop=True)
                nc.tensor.matmul(pw[:, 128:256], K("center"), scaled[:, 1, :], start=True, stop=True)
                nc.tensor.matmul(pw[:, 256:257], scaled[:, 2, :], W("q_shift"), start=True, stop=True)
                nc.tensor.matmul(pw[:, 257:258], W("wv"), W("kv_shift"), start=True, stop=True)
                for i, name in enumerate(("mk", "mv")):
                    nc.tensor.matmul(pm[:, 64 * i:64 * i + 64], W(name, C), K("center4", C), start=True, stop=True)
                for i in range(2):
                    last = nc.tensor.matmul(pm[:, 128 + 64 * i:192 + 64 * i], bias_rows[:, i, :], K("center4", C),
                                            start=True, stop=True)
                last.then_inc(w_products, 1)
                pe.wait_ge(vb_copied, 2)
                nc.tensor.matmul(pb[:, 0:1], W("proj"), v_bias[:, :], start=True, stop=True).then_inc(pb_product, 1)


def text(nc, n):
    with ExitStack() as ctx:
        def sb(name, shape, dt=FP32):
            return ctx.enter_context(nc.sbuf_tensor(name, shape, dt))

        def bank(name):
            return ctx.enter_context(nc.psum_tensor(name, [P, 512], FP32))

        FOUR = 4
        SC = 4
        STEPS = B // FOUR
        PAD1, PAD2, PAD3 = TXT_T + 6, TXT_T + 4, TXT_T + 2
        UNSCALE = 1.0 / W_SCALE
        ids = sb("ids", [P, FOUR, TXT_T], I32)
        pos = sb("pos", [P, 2, FOUR, TXT_T])
        onehot = sb("onehot", [P, FOUR, PAD1], FP16)
        c1 = sb("c1_parts", [P, 2, 4, P], FP16)
        c1_big = sb("c1_big", [P, 4, P])
        emb = sb("emb_parts", [P, 3, 68], FP16)
        emb_big = sb("emb_big", [P, 2, 68])
        hidden1 = sb("hidden1", [P, FOUR, PAD2])
        hidden2 = sb("hidden2", [P, 2, PAD3])
        gates = sb("gates", [P, 2, 2, FOUR])
        gates1 = sb("gates1", [P, 2, FOUR])
        factor = sb("factor", [P, FOUR])
        loc = sb("loc", [P, FOUR, 4])
        abs_w = sb("abs_w", [P, FOUR])
        center = sb("wave_center", [P, 2, FOUR])
        width = sb("width", [P, FOUR, SC])
        width1 = sb("width1", [P, FOUR, SC])
        inv_w = sb("inv_w", [P, 2, FOUR, SC])
        shift = sb("shift", [P, 2, FOUR])
        amps = sb("amps", [P, 4, FOUR, C])
        sw2 = sb("sw2", [P, SC])
        b3_half = sb("b3_half", [P, 1])
        dist = sb("dist", [P, FOUR, TXT_T])
        z = sb("z", [P, SC, FOUR, TXT_T])
        z_sq = sb("z_sq", [P, SC, FOUR, TXT_T])
        turns = sb("turns", [P, SC, FOUR, TXT_T])
        whole = sb("whole", [P, SC, FOUR, TXT_T])
        frac = sb("frac", [P, SC, FOUR, TXT_T])
        bell = sb("bell", [P, SC, FOUR, TXT_T])
        wave = sb("wave", [P, SC, FOUR, TXT_T])
        packet = sb("packet", [P, SC, FOUR, TXT_T])
        p_c1, p_c2, p_ctx, p_field = (bank(x) for x in ("p_c1", "p_c2", "p_ctx", "p_field"))
        p_emb = [bank("p_emb0"), bank("p_emb1")]
        names = ("parts_hi parts_mid parts_done ids_in onehot_done c1_ready gelu1_done c2_ready gelu2_done ctx_ready emb_ready "
                 "gates_done loc_done gates_eased factor_done amps_done width_made width_eased params_done dist_done z_done "
                 "clamped squared bell_done turned rounded frac_done wave_done packet_done field_ready field_copied zeroed")
        s = {name: ctx.enter_context(nc.semaphore("t_" + name)) for name in names.split()}
        pos_in = [ctx.enter_context(nc.semaphore(f"t_pos_in{k}")) for k in range(2)]
        W = lambda name: n.w[:, W_AT[name][0]:W_AT[name][1]]
        K = lambda name: n.f[:, F32_AT[name][0]:F32_AT[name][1]]

        def run(engine, body):
            def static(i):
                body(i, i % 4, *[0 <= i - k < STEPS for k in range(-1, 4)])

            for i in range(-1, 4):
                static(i)
            with engine.Fori(1, STEPS // 4 - 1) as j:
                for u in range(4):
                    body(4 * j + u, u, True, True, True, True, True)
            for i in range(STEPS - 4, STEPS + 3):
                static(i)

        with nc.Block() as block:
            @block.sync
            def _(sp):
                def body(i, u, pre, new, old, fin, out):
                    if not new:
                        return
                    wait(sp, s["onehot_done"], 2 * i)
                    sp.dma_start(ids[:, :, :].rearrange("p b t -> p (b t)"),
                                 n.in_ids[0, bass.ds(i * 512, 512)].partition_broadcast(P)).then_inc(s["ids_in"], 16)
                    wait(sp, s["dist_done"], i - 1)
                    sp.dma_start(pos[:, u % 2, :, :].rearrange("p b t -> p (b t)"),
                                 n.in_pos[0, bass.ds(i * 512, 512)].partition_broadcast(P)).then_inc(pos_in[u % 2], 16)

                run(sp, body)
                for u in range(4):
                    load_group(sp, n, u, 0)

            @block.tensor
            def _(pe):
                mm = nc.tensor.matmul

                def body(i, u, pre, new, old, fin, out):
                    if new:
                        wait(pe, s["amps_done"], i - 1)
                        wait(pe, s["loc_done"], i - 1)
                        for b in range(FOUR):
                            for part in range(3):
                                last = mm(p_emb[u % 2][:, 68 * b:68 * b + 68], onehot[:, b, 3:3 + TXT_T], emb[:, part, :],
                                          start=(part == 0), stop=(part == 2))
                        last.then_inc(s["emb_ready"], 1)
                    if old:
                        pe.wait_ge(s["gelu2_done"], i)
                        wait(pe, s["gates_done"], i - 1)
                        for q in range(2):
                            for tap in range(3):
                                last = mm(p_ctx[:, 2 * q:2 * q + 2], hidden2[:, q, tap:tap + TXT_T],
                                          n.w[:, W_AT["c3"][0] + 2 * tap:W_AT["c3"][0] + 2 * tap + 2], start=(tap == 0), stop=(tap == 2))
                        last.then_inc(s["ctx_ready"], 1)
                    if new:
                        pe.wait_ge(s["gelu1_done"], i + 1)
                        wait(pe, s["gelu2_done"], i)
                        for k in range(2):
                            for tap in range(5):
                                last = mm(p_c2[C * k:C * k + C, 0:2 * TXT_T], n.w[:, W_AT["c2"][0] + C * tap:W_AT["c2"][0] + C * tap + C],
                                          hidden1[:, k:4:2, tap:tap + TXT_T], start=(tap == 0), stop=(tap == 4), tile_position=(0, C * k))
                        last.then_inc(s["c2_ready"], 1)
                    if pre:
                        pe.wait_ge(s["onehot_done"], 2 * i + 4)
                        wait(pe, s["gelu1_done"], i + 1)
                        if isinstance(i, int) and i < 0:
                            pe.wait_ge(s["parts_done"], 3)
                            pe.wait_ge(s["zeroed"], 3)
                        for j in range(4):
                            for part in range(2):
                                last = mm(p_c1[:, :], c1[:, part, j, :], onehot[:, :, 2 * j:2 * j + TXT_T],
                                          start=(j + part == 0), stop=(j == 3 and part == 1))
                        last.then_inc(s["c1_ready"], 1)
                    if fin:
                        pe.wait_ge(s["packet_done"], 4 * (i - 1))
                        pe.wait_ge(s["amps_done"], i - 1)
                        wait(pe, s["field_copied"], i - 2)
                        for b in range(FOUR):
                            for k in range(SC):
                                last = mm(p_field[C * (b % 2):C * (b % 2) + C, P * (b // 2):P * (b // 2) + P], amps[:, (u - 2) % 4, b, :],
                                          packet[:, k, b, :], start=(k == 0), stop=(k == SC - 1), tile_position=(0, C * (b % 2)))
                        last.then_inc(s["field_ready"], 1)

                run(pe, body)

            @block.scalar
            def _(act):
                A = nc.scalar.activation

                def body(i, u, pre, new, old, fin, out):
                    emb4 = p_emb[u % 2][:, 0:68 * FOUR].rearrange("p (b e) -> p b e", b=FOUR)
                    if fin:
                        act.wait_ge(s["squared"], i - 1)
                        wait(act, s["packet_done"], 4 * (i - 2))
                        A(bell[:, :, :, :], z_sq[:, :, :, :], ACT.Exp, scale=-0.5).then_inc(s["bell_done"], 1)
                    if fin:
                        act.wait_ge(s["frac_done"], i - 1)
                        A(wave[:, :, :, :], frac[:, :, :, :], ACT.Sin, scale=6.2831845).then_inc(s["wave_done"], 1)
                    if old:
                        act.wait_ge(s["c2_ready"], i)
                        wait(act, s["ctx_ready"], i - 1)
                        A(hidden2[:, :, 1:1 + TXT_T], p_c2[:, 0:2 * TXT_T].rearrange("p (q t) -> p q t", q=2), ACT.Gelu,
                          bias=W("c2_b")).then_inc(s["gelu2_done"], 1)
                    if new:
                        act.wait_ge(s["c1_ready"], i + 1)
                        wait(act, s["c2_ready"], i)
                        if isinstance(i, int) and i == 0:
                            act.wait_ge(s["zeroed"], 3)
                        A(hidden1[:, :, 2:2 + TXT_T], p_c1[:, :].rearrange("p (b t) -> p b t", b=FOUR), ACT.Gelu,
                          bias=W("c1_b"), scale=UNSCALE).then_inc(s["gelu1_done"], 1)
                    if old:
                        act.wait_ge(s["clamped"], i)
                        wait(act, s["bell_done"], i - 1)
                        A(z_sq[:, :, :, :], z[:, :, :, :], ACT.Square).then_inc(s["squared"], 1)
                    if out:
                        act.wait_ge(s["field_ready"], i - 2)
                        A(n.tokens[:, bass.ds(2 * i - 6, 2), IMG_T:TOK], p_field[:, 0:2 * TXT_T].rearrange("p (q t) -> p q t", q=2),
                          ACT.Copy).then_inc(s["field_copied"], 1)
                    if new:
                        act.wait_ge(s["emb_ready"], i + 1)
                        wait(act, s["gates_eased"], i - 1)
                        A(gates[:, u % 2, 1, :], emb4[:, :, 66], ACT.Tanh, scale=0.5 * UNSCALE)
                        wait(act, s["params_done"], i)
                        A(loc[:, :, :], emb4[:, :, 64:68], ACT.Copy, scale=UNSCALE)
                        A(abs_w[:, :], emb4[:, :, 65], ACT.Abs, scale=UNSCALE).then_inc(s["loc_done"], 1)
                    if old:
                        act.wait_ge(s["ctx_ready"], i)
                        A(gates[:, (u - 1) % 2, 0, :], p_ctx[:, 0:FOUR], ACT.Tanh, scale=0.5, bias=b3_half[:, :]).then_inc(s["gates_done"], 1)

                run(act, body)

            @block.vector
            def _(dve):
                V = nc.vector
                V.tensor_scalar(c1_big[:, :, :].rearrange("p a b -> p (a b)"), W("c1"), W_SCALE, None, ALU.mult)
                V.tensor_scalar(emb_big[:, 0, :], W("embed"), W_SCALE, None, ALU.mult)
                V.tensor_tensor(sw2[:, :], W("scales"), W("scales"), ALU.mult)
                V.tensor_scalar(b3_half[:, :], W("c3_b"), 0.5, None, ALU.mult).then_inc(s["parts_hi"], 1)
                dve.wait_ge(s["parts_hi"], 1)
                V.tensor_copy(c1[:, 0, :, :], c1_big[:, :, :])
                V.tensor_copy(emb[:, 0, :], emb_big[:, 0, :]).then_inc(s["parts_hi"], 1)
                dve.wait_ge(s["parts_hi"], 2)
                V.tensor_tensor(c1[:, 1, :, :], c1_big[:, :, :], c1[:, 0, :, :], ALU.subtract).then_inc(s["parts_done"], 1)
                V.tensor_tensor(emb_big[:, 1, :], emb_big[:, 0, :], emb[:, 0, :], ALU.subtract).then_inc(s["parts_mid"], 1)
                dve.wait_ge(s["parts_mid"], 1)
                V.tensor_copy(emb[:, 1, :], emb_big[:, 1, :]).then_inc(s["parts_done"], 1)
                dve.wait_ge(s["parts_done"], 2)
                V.tensor_tensor(emb[:, 2, :], emb_big[:, 1, :], emb[:, 1, :], ALU.subtract).then_inc(s["parts_done"], 1)

                def body(i, u, pre, new, old, fin, out):
                    if old:
                        v = (u + 1) % 2
                        dve.wait_ge(pos_in[v], 16 * ((i - u) // 2 + (u + 1) // 2))
                        V.tensor_tensor(dist[:, :, :], pos[:, v, :, :], center[:, v, :].unsqueeze(2).broadcast_to([P, FOUR, TXT_T]),
                                        ALU.subtract).then_inc(s["dist_done"], 1)
                        dve.wait_ge(s["dist_done"], i)
                        wait(dve, s["squared"], i - 1)
                        wait(dve, s["turned"], i - 1)
                        for k in range(SC):
                            last = V.tensor_tensor(z[:, k, :, :], dist[:, :, :], inv_w[:, v, :, k:k + 1].broadcast_to([P, FOUR, TXT_T]), ALU.mult)
                        last.then_inc(s["z_done"], 1)
                        dve.wait_ge(s["z_done"], i)
                        V.tensor_scalar(z[:, :, :, :], z[:, :, :, :], 30.0, -30.0, ALU.min, ALU.max).then_inc(s["clamped"], 1)
                    if fin:
                        dve.wait_ge(s["wave_done"], i - 1)
                        dve.wait_ge(s["bell_done"], i - 1)
                        wait(dve, s["field_ready"], i - 2)
                        for k in range(SC):
                            V.scalar_tensor_tensor(packet[:, k, :, :], bell[:, k, :, :], sw2[:, k:k + 1], wave[:, k, :, :],
                                                   ALU.mult, ALU.mult).then_inc(s["packet_done"], 1)
                    if pre:
                        dve.wait_ge(s["ids_in"], 16 * (i + 2))
                        wait(dve, s["emb_ready"], i + 1)
                        if isinstance(i, int) and i < 0:
                            dve.wait_ge(s["zeroed"], 1)
                        for half in range(2):
                            V.tensor_scalar(onehot[C * half:C * half + C, :, 3 - half:3 - half + TXT_T], ids[C * half:C * half + C, :, :],
                                            K("vocab")[C * half:C * half + C, :], None, ALU.is_equal).then_inc(s["onehot_done"], 1)
                    if old:
                        dve.wait_ge(s["turned"], i)
                        wait(dve, s["frac_done"], i - 1)
                        V.tensor_scalar(whole[:, :, :, :], turns[:, :, :, :], MAGIC, -MAGIC, ALU.add, ALU.add).then_inc(s["rounded"], 1)
                    if new:
                        dve.wait_ge(s["loc_done"], i + 1)
                        wait(dve, s["dist_done"], i - 1)
                        wait(dve, s["turned"], i - 1)
                        V.tensor_scalar(center[:, u % 2, :], loc[:, :, 0], 0.05, K("byte_pos"), ALU.mult, ALU.add)
                        V.tensor_scalar(shift[:, u % 2, :], loc[:, :, 3], 0.5, 0.25, ALU.mult, ALU.add)
                        V.tensor_tensor(width[:, :, :], abs_w[:, :].unsqueeze(2).broadcast_to([P, FOUR, SC]),
                                        W("widths").unsqueeze(1).broadcast_to([P, FOUR, SC]), ALU.mult).then_inc(s["width_made"], 1)
                        dve.wait_ge(s["width_made"], i + 1)
                        V.tensor_scalar(width1[:, :, :], width[:, :, :], 1e-5, None, ALU.add).then_inc(s["width_eased"], 1)
                        dve.wait_ge(s["width_eased"], i + 1)
                        V.reciprocal(inv_w[:, u % 2, :, :], width1[:, :, :]).then_inc(s["params_done"], 1)
                    if old:
                        dve.wait_ge(s["gates_done"], i)
                        dve.wait_ge(s["loc_done"], i)
                        wait(dve, s["factor_done"], i - 1)
                        V.tensor_scalar(gates1[:, :, :], gates[:, (u - 1) % 2, :, :], 0.5, 0.5, ALU.mult, ALU.add).then_inc(s["gates_eased"], 1)
                        dve.wait_ge(s["gates_eased"], i)
                        wait(dve, s["amps_done"], i - 1)
                        V.scalar_tensor_tensor(factor[:, :], gates1[:, 0, :], UNSCALE, gates1[:, 1, :], ALU.mult, ALU.mult).then_inc(s["factor_done"], 1)
                        dve.wait_ge(s["factor_done"], i)
                        V.tensor_tensor(amps[:, (u - 1) % 4, :, :], p_emb[(u - 1) % 2][:, 0:68 * FOUR].rearrange("p (b e) -> p b e", b=FOUR)[:, :, 0:C],
                                        factor[:, :].unsqueeze(2).broadcast_to([P, FOUR, C]), ALU.mult).then_inc(s["amps_done"], 1)

                run(dve, body)

            @block.gpsimd
            def _(pool):
                G = nc.gpsimd
                G.memset(onehot[:, :, :], 0.0).then_inc(s["zeroed"], 1)
                G.memset(hidden1[:, :, :], 0.0).then_inc(s["zeroed"], 1)
                G.memset(hidden2[:, :, :], 0.0).then_inc(s["zeroed"], 1)

                def body(i, u, pre, new, old, fin, out):
                    if old:
                        v = (u + 1) % 2
                        pool.wait_ge(s["clamped"], i)
                        wait(pool, s["rounded"], i - 1)
                        wait(pool, s["frac_done"], i - 1)
                        G.tensor_tensor(turns[:, :, :, :].rearrange("p k b t -> p k b t"), z[:, :, :, :],
                                        shift[:, v, :].unsqueeze(1).unsqueeze(3).broadcast_to([P, SC, FOUR, TXT_T]), ALU.add).then_inc(s["turned"], 1)
                        pool.wait_ge(s["rounded"], i)
                        wait(pool, s["wave_done"], i - 1)
                        G.tensor_tensor(frac[:, :, :, :], turns[:, :, :, :], whole[:, :, :, :], ALU.subtract).then_inc(s["frac_done"], 1)

                run(pool, body)

        zero(nc, [*s.values(), *pos_in])


def load_group(engine, n, u, i):
    x_dram = n.in_x.rearrange("(q b) c (h n) -> q (b c) h n", b=2, h=2)
    engine.dma_start(n.xs[:, u, :], x_dram[2 * i + u // 2, :, u % 2, :]).then_inc(n.x_in[u], 16)


def windows(nc, n):
    with ExitStack() as ctx:
        def sb(name, shape, dt=FP32):
            return ctx.enter_context(nc.sbuf_tensor(name, shape, dt))

        def bank(name):
            return ctx.enter_context(nc.psum_tensor(name, [P, 512], FP32))

        xs, x_in = n.xs, n.x_in
        squares = sb("squares", [P, GROUP])
        tree1 = sb("tree1", [P, 1024])
        tree2 = sb("tree2", [P, 512])
        tree3 = sb("tree3", [P, 256])
        sums = sb("sums", [P, 4, WG])
        q_cent = sb("q_cent", [P, WG])
        q_square = sb("q_square", [P, WG])
        q_log = sb("q_log", [P, WG])
        q_rstd = sb("q_rstd", [P, WG])
        q_norm = sb("q_norm", [P, WG])
        qs = sb("qs", [P, 2, WG])
        mean_sq = sb("mean_sq", [P, CHUNK])
        var = sb("var", [P, CHUNK])
        var_pos = sb("var_pos", [P, CHUNK])
        var_log = sb("var_log", [P, CHUNK])
        rstd = sb("rstd", [P, 2, CHUNK])
        qk = sb("qk", [P, CH, CHUNK])
        score = sb("score", [P, CHUNK])
        top = sb("top", [P, WC])
        below = sb("below", [P, CHUNK])
        ex = sb("ex", [P, CHUNK])
        total = sb("total", [P, WC])
        inv = sb("inv", [P, WC])
        ex_rstd = sb("ex_rstd", [P, CHUNK])
        weight = sb("weight", [P, CHUNK])
        w_hi = sb("w_hi", [P, CHUNK], FP16)
        w_parts = sb("w_parts", [P, 2, CHUNK], FP16)
        w_wide = sb("w_wide", [P, 2, CHUNK])
        wv = sb("wv_prod", [P, 2, CHUNK])
        agg = sb("agg", [P, WG])
        out_b = sb("out_b", [P, WG])
        p_kv = [bank("p_kv0"), bank("p_kv1"), bank("p_kv2")]
        p_w, p_mean, p_sq, p_score, p_q = (bank(x) for x in ("p_w", "p_mean", "p_sq", "p_score", "p_q"))
        cent_cols, var_cols, query_cols, out_cols = (slice(WG * k, WG * k + WG) for k in range(4))
        names = ("sums_1 sums_2 sums_3 sums_done cent_ready cent_copied q_var_ready q_log_done q_rstd_done q_normed "
                 "q_ready q_copied squared mean_ready sq_ready mean_sq_done var_done var_clamped var_logged rstd_done "
                 "k_ready qk_done scores_ready scored top_done below_done exp_done total_done inv_done ex_rstd_done "
                 "weight_done hi_done parts_done v_ready wide_ready wide_copied wv_done reduced proj_ready out_biased token_done")
        s = {name: ctx.enter_context(nc.semaphore(name)) for name in names.split()}
        K = lambda name, rows=P: n.f[0:rows, F32_AT[name][0]:F32_AT[name][1]]
        spread = lambda c: n.h[:, F16_AT["spread16"][0] + P * c:F16_AT["spread16"][0] + P * c + P]
        proj = n.w[:, W_AT["proj"][0]:W_AT["proj"][1]]

        def window_order(t):
            return t.rearrange("p (row col x) -> p col row x", row=8, x=4)

        def by_window(t):
            return t.rearrange("p (col k) -> p col k", k=WIN)

        def chunk_windows(t, c):
            return t[:, WC * c:WC * c + WC].rearrange("p (row col) -> p col row", row=2)

        def steps(body):
            for g in range(-1, 4):
                body(g, g % 4, g // 4, g >= 0, g < GROUPS - 1, g >= 1, g >= 2)
            return lambda i: [body(4 * i + u, u, i, True, True, True, True) for u in range(4)]

        def tail(body):
            for g in range(GROUPS - 4, GROUPS + 2):
                body(g, g % 4, g // 4, g < GROUPS, g < GROUPS - 1, g <= GROUPS, True)

        def run(engine, body):
            loop = steps(body)
            with engine.Fori(1, GROUPS // 4 - 1) as i:
                loop(i)
            tail(body)

        with nc.Block() as block:
            @block.sync
            def _(sp):
                def load(g, u, i):
                    wait(sp, s["v_ready"], 4 * (g - 3))
                    load_group(sp, n, u, i)

                with sp.Fori(1, GROUPS // 4) as i:
                    for u in range(4):
                        load(4 * i + u, u, i)

            @block.tensor
            def _(pe):
                mm = nc.tensor.matmul

                def body(g, u, i, cur, nxt, prev, out):
                    un, uv = (u + 1) % 4, (u + 3) % 4
                    i_n = i + 1 if u == 3 else i
                    px = [slice(CHUNK * c, CHUNK * c + CHUNK) for c in range(CH)]
                    if cur:
                        for c in range(CH):
                            if c < 3:
                                wait(pe, s["wv_done"], 4 * (g - 2) + (3, 4, 2)[c])
                            else:
                                pe.wait_ge(s["qk_done"], 4 * g + 1)
                            mm(p_kv[c % 3][:, :], n.wk[:, :], window_order(xs[:, u, px[c]]), start=True, stop=True).then_inc(s["k_ready"], 1)
                    if nxt:
                        pe.wait_ge(x_in[un], 16 * (i_n + 1))
                        wait(pe, s["mean_sq_done"], g + 1)
                        for k in range(CH):
                            last = mm(p_mean[32 * k:32 * k + 32, :], K("mean32"), window_order(xs[:, un, px[k]]), start=True, stop=True,
                                      tile_position=(0, 32 * k))
                        last.then_inc(s["mean_ready"], 1)
                    if cur:
                        pe.wait_ge(s["qk_done"], 4 * g + 4)
                        wait(pe, s["scored"], g)
                        for c in range(CH):
                            last = mm(p_score[32 * c:32 * c + 32, :], K("head32"), qk[:, c, :], start=True, stop=True,
                                      tile_position=(0, 32 * c))
                        last.then_inc(s["scores_ready"], 1)
                    for c in range(CH):
                        if prev:
                            if c == 0:
                                pe.wait_ge(s["parts_done"], g)
                            wait(pe, s["wide_copied"], 4 * (g - 1) + c)
                            mm(p_w[:, :], spread(c), w_parts[:, uv % 2, :], start=True, stop=True).then_inc(s["wide_ready"], 1)
                        if out and c == 0:
                            pe.wait_ge(s["reduced"], 4 * (g - 1))
                            pe.wait_ge(s["q_copied"], g + 1 if cur else GROUPS)
                            wait(pe, s["out_biased"], g - 2)
                            mm(p_q[:, out_cols], proj, agg[:, :], start=True, stop=True).then_inc(s["proj_ready"], 1)
                        if prev:
                            if c == CH - 1:
                                pe.wait_ge(s["wv_done"], 4 * (g - 1) + 1)
                            elif cur:
                                pe.wait_ge(s["qk_done"], 4 * g + c + 2)
                            mm(p_kv[(c + 1) % 3][:, :], n.wv[:, :], window_order(xs[:, uv, px[c]]), start=True, stop=True).then_inc(s["v_ready"], 1)
                        if nxt and c == 0:
                            pe.wait_ge(s["sums_done"], g + 2)
                            wait(pe, s["out_biased"], g - 1)
                            wait(pe, s["q_copied"], g + 1)
                            mm(p_q[:, cent_cols], K("center"), sums[:, un, :], start=True, stop=True).then_inc(s["cent_ready"], 1)
                        if nxt and c == 1:
                            pe.wait_ge(s["cent_copied"], g + 2)
                            mm(p_q[:, var_cols], K("average"), q_square[:, :], start=True, stop=True).then_inc(s["q_var_ready"], 1)
                        if nxt and c == CH - 1:
                            pe.wait_ge(s["squared"], g + 2)
                            wait(pe, s["var_done"], g + 1)
                            for k in range(CH):
                                last = mm(p_sq[32 * k:32 * k + 32, :], K("mean32"), window_order(squares[:, px[k]]), start=True, stop=True,
                                          tile_position=(0, 32 * k))
                            last.then_inc(s["sq_ready"], 1)
                        if nxt and c == CH - 1:
                            pe.wait_ge(s["q_normed"], g + 2)
                            mm(p_q[:, query_cols], n.wq[:, :], q_norm[:, :], start=True, stop=True).then_inc(s["q_ready"], 1)

                run(pe, body)

            @block.scalar
            def _(act):
                A = nc.scalar.activation
                nc.scalar.preload_act_table_set("natural_log_exp_and_others")

                def body(g, u, i, cur, nxt, prev, out):
                    un, uv = (u + 1) % 4, (u + 3) % 4
                    i_n = i + 1 if u == 3 else i
                    if nxt:
                        act.wait_ge(x_in[un], 16 * (i_n + 1))
                        wait(act, s["sq_ready"], g + 1)
                        A(squares[:, :], xs[:, un, :], ACT.Square).then_inc(s["squared"], 1)
                    for c in range(CH):
                        if prev:
                            act.wait_ge(s["wide_ready"], 4 * (g - 1) + c + 1)
                            wait(act, s["wv_done"], 4 * (g - 1) + c - 1)
                            A(w_wide[:, c % 2, :], p_w[:, :], ACT.Copy).then_inc(s["wide_copied"], 1)
                        if c == 0 and out:
                            act.wait_ge(s["proj_ready"], g - 1)
                            wait(act, s["token_done"], g - 2)
                            A(out_b[:, :], p_q[:, out_cols], ACT.Identity, bias=n.pb[:, :]).then_inc(s["out_biased"], 1)
                        if c == 0 and nxt:
                            act.wait_ge(s["cent_ready"], g + 2)
                            wait(act, s["q_normed"], g + 1)
                            A(q_cent[:, :], p_q[:, cent_cols], ACT.Copy, scale=1.0 / WIN)
                            A(q_square[:, :], p_q[:, cent_cols], ACT.Square, scale=1.0 / WIN).then_inc(s["cent_copied"], 1)
                        if c == 1 and cur:
                            act.wait_ge(s["below_done"], g + 1)
                            wait(act, s["ex_rstd_done"], g)
                            wait(act, s["total_done"], g)
                            A(ex[:, :], below[:, :], ACT.Exp).then_inc(s["exp_done"], 1)
                        if c == 1 and nxt:
                            act.wait_ge(s["q_var_ready"], g + 2)
                            wait(act, s["q_rstd_done"], g + 1)
                            A(q_log[:, :], p_q[:, var_cols], ACT.Ln, bias=K("eps")).then_inc(s["q_log_done"], 1)
                            act.wait_ge(s["q_log_done"], g + 2)
                            A(q_rstd[:, :], q_log[:, :], ACT.Exp, scale=-0.5).then_inc(s["q_rstd_done"], 1)
                        if c == 2 and nxt:
                            act.wait_ge(s["mean_ready"], g + 2)
                            wait(act, s["var_done"], g + 1)
                            A(mean_sq[:, :], p_mean[:, :], ACT.Square).then_inc(s["mean_sq_done"], 1)
                    if cur:
                        act.wait_ge(s["weight_done"], g + 1)
                        wait(act, s["parts_done"], g)
                        A(w_hi[:, :], weight[:, :], ACT.Copy, scale=K("low_rows")).then_inc(s["hi_done"], 1)
                    if nxt:
                        act.wait_ge(s["q_ready"], g + 2)
                        wait(act, s["qk_done"], 4 * g)
                        A(qs[:, un % 2, :], p_q[:, query_cols], ACT.Identity, bias=n.bq[:, :]).then_inc(s["q_copied"], 1)
                    if nxt:
                        act.wait_ge(s["var_clamped"], g + 2)
                        wait(act, s["rstd_done"], g + 1)
                        A(var_log[:, :], var_pos[:, :], ACT.Ln, bias=K("eps")).then_inc(s["var_logged"], 1)
                        act.wait_ge(s["var_logged"], g + 2)
                        wait(act, s["ex_rstd_done"], g)
                        wait(act, s["scored"], g)
                        A(rstd[:, un % 2, :], var_log[:, :], ACT.Exp, scale=-0.5).then_inc(s["rstd_done"], 1)

                run(act, body)

            @block.vector
            def _(dve):
                V = nc.vector

                def gather(g, c, u):
                    dve.wait_ge(s["wv_done"], 4 * (g - 1) + c + 1)
                    if c == 0:
                        wait(dve, s["proj_ready"], g - 1)
                    V.tensor_reduce(chunk_windows(agg[:, :], c), wv[:, c % 2, :].rearrange("p (col row k) -> p col row k", col=16, row=2), X, ALU.add).then_inc(s["reduced"], 1)

                def body(g, u, i, cur, nxt, prev, out):
                    uv = (u + 3) % 4
                    if cur:
                        dve.wait_ge(s["q_copied"], g + 1)
                        wait(dve, s["scores_ready"], g)
                        for c in range(CH):
                            dve.wait_ge(s["k_ready"], 4 * g + c + 1)
                            q = chunk_windows(qs[:, u % 2, :], c).unsqueeze(3).broadcast_to([P, 16, 2, WIN])
                            V.tensor_tensor(qk[:, c, :].rearrange("p (col row k) -> p col row k", col=16, row=2),
                                            p_kv[c % 3][:, :].rearrange("p (col row k) -> p col row k", col=16, row=2), q, ALU.mult).then_inc(s["qk_done"], 1)
                    if out:
                        for c in (2, 3):
                            gather(g - 1, c, u)
                    if cur:
                        dve.wait_ge(s["scores_ready"], g + 1)
                        dve.wait_ge(s["rstd_done"], g + 1)
                        V.tensor_tensor(score[:, :], p_score[:, :], rstd[:, u % 2, :], ALU.mult).then_inc(s["scored"], 1)
                        dve.wait_ge(s["scored"], g + 1)
                        V.tensor_reduce(top[:, :], by_window(score[:, :]), X, ALU.max).then_inc(s["top_done"], 1)
                        dve.wait_ge(s["top_done"], g + 1)
                        wait(dve, s["exp_done"], g)
                        V.tensor_tensor(by_window(below[:, :]), by_window(score[:, :]), top[:, :].unsqueeze(2).broadcast_to([P, WC, WIN]),
                                        ALU.subtract).then_inc(s["below_done"], 1)
                    if out:
                        dve.wait_ge(s["out_biased"], g - 1)
                        pair = 2 * i + (u - 2) // 2
                        V.scalar_tensor_tensor(n.tokens[:, pair, WG * (u % 2):WG * (u % 2) + WG], sums[:, (u + 2) % 4, :], 1.0 / WIN,
                                               out_b[:, :], ALU.mult, ALU.add).then_inc(s["token_done"], 1)
                    for c in range(CH):
                        if c == 1 and cur:
                            dve.wait_ge(s["exp_done"], g + 1)
                            V.tensor_reduce(total[:, :], by_window(ex[:, :]), X, ALU.add).then_inc(s["total_done"], 1)
                        if prev:
                            dve.wait_ge(s["v_ready"], 4 * (g - 1) + c + 1)
                            dve.wait_ge(s["wide_copied"], 4 * (g - 1) + c + 1)
                            wait(dve, s["reduced"], 4 * (g - 1) + c - 1)
                            V.tensor_tensor(wv[:, c % 2, :], p_kv[(c + 1) % 3][:, :], w_wide[:, c % 2, :], ALU.mult).then_inc(s["wv_done"], 1)
                        if c == 1 and cur:
                            dve.wait_ge(s["total_done"], g + 1)
                            wait(dve, s["weight_done"], g)
                            V.reciprocal(inv[:, :], total[:, :]).then_inc(s["inv_done"], 1)
                        if prev and c < 2:
                            gather(g, c, u)
                    if nxt:
                        dve.wait_ge(s["mean_sq_done"], g + 2)
                        dve.wait_ge(s["sq_ready"], g + 2)
                        wait(dve, s["var_clamped"], g + 1)
                        V.tensor_tensor(var[:, :], p_sq[:, :], mean_sq[:, :], ALU.subtract).then_inc(s["var_done"], 1)
                        dve.wait_ge(s["var_done"], g + 2)
                        wait(dve, s["var_logged"], g + 1)
                        V.tensor_scalar(var_pos[:, :], var[:, :], 0.0, None, ALU.max).then_inc(s["var_clamped"], 1)

                run(dve, body)

            @block.gpsimd
            def _(pool):
                G = nc.gpsimd

                def body(g, u, i, cur, nxt, prev, out):
                    un = (u + 1) % 4
                    i_n = i + 1 if u == 3 else i
                    if nxt:
                        pool.wait_ge(x_in[un], 16 * (i_n + 1))
                        t1 = tree1[:, :].rearrange("p (y row x) -> p y row x", row=2, x=64)
                        wait(pool, s["sums_2"], g + 1)
                        G.tensor_tensor(tree1[:, :].rearrange("p (y rowx) -> p y rowx", y=8), xs[:, un, :].rearrange("p (y h rowx) -> p y h rowx", h=2, rowx=128)[:, :, 0, :],
                                        xs[:, un, :].rearrange("p (y h rowx) -> p y h rowx", h=2, rowx=128)[:, :, 1, :], ALU.add).then_inc(s["sums_1"], 1)
                        pool.wait_ge(s["sums_1"], g + 2)
                        wait(pool, s["sums_3"], g + 1)
                        G.tensor_tensor(tree2[:, :].rearrange("p (y x) -> p y x", y=8), t1[:, :, 0, :], t1[:, :, 1, :], ALU.add).then_inc(s["sums_2"], 1)
                        pool.wait_ge(s["sums_2"], g + 2)
                        wait(pool, s["sums_done"], g + 1)
                        t2 = tree2[:, :].rearrange("p (col h x) -> p col h x", h=2, x=2)
                        G.tensor_tensor(tree3[:, :].rearrange("p (col x) -> p col x", x=2), t2[:, :, 0, :], t2[:, :, 1, :], ALU.add).then_inc(s["sums_3"], 1)
                        pool.wait_ge(s["sums_3"], g + 2)
                        wait(pool, s["token_done"], g - 2)
                        t3 = tree3[:, :].rearrange("p (col x) -> p col x", x=2)
                        G.tensor_tensor(sums[:, un, :], t3[:, :, 0], t3[:, :, 1], ALU.add).then_inc(s["sums_done"], 1)
                    if cur:
                        pool.wait_ge(s["exp_done"], g + 1)
                        wait(pool, s["weight_done"], g)
                        G.tensor_tensor(ex_rstd[:, :], ex[:, :], rstd[:, u % 2, :], ALU.mult).then_inc(s["ex_rstd_done"], 1)
                    if nxt:
                        pool.wait_ge(s["q_rstd_done"], g + 2)
                        wait(pool, s["q_ready"], g + 1)
                        G.tensor_tensor(q_norm[:, :], q_cent[:, :], q_rstd[:, :], ALU.mult).then_inc(s["q_normed"], 1)
                    if cur:
                        pool.wait_ge(s["inv_done"], g + 1)
                        pool.wait_ge(s["ex_rstd_done"], g + 1)
                        wait(pool, s["parts_done"], g)
                        G.tensor_tensor(by_window(weight[:, :]), by_window(ex_rstd[:, :]), inv[:, :].unsqueeze(2).broadcast_to([P, WC, WIN]),
                                        ALU.mult).then_inc(s["weight_done"], 1)
                        pool.wait_ge(s["hi_done"], g + 1)
                        wait(pool, s["wide_ready"], 4 * (g - 1))
                        G.tensor_tensor(w_parts[:, u % 2, :], weight[:, :], w_hi[:, :], ALU.subtract).then_inc(s["parts_done"], 1)

                run(pool, body)

        zero(nc, [*s.values()])


def mixing(nc, n):
    with ExitStack() as ctx:
        def sb(name, shape, dt=FP32):
            return ctx.enter_context(nc.sbuf_tensor(name, shape, dt))

        bank = [ctx.enter_context(nc.psum_tensor(f"mix{k}", [P, 512], FP32)) for k in range(8)]
        T3 = TOK // P
        R = 2 * T3
        p_cent, p_var, p_cent2, p_var2, p_kv0, p_kv1, p_q, p_kvkv = bank
        xn = sb("xn", [P, 4, TOK])
        sq1, log1, rstd1 = sb("sq1", [P, TOK]), sb("log1", [P, TOK]), sb("rstd1", [P, TOK])
        sq2, log2, rstd2 = sb("sq2", [P, TOK]), sb("log2", [P, TOK]), sb("rstd2", [P, TOK])
        xn2 = sb("xn2", [P, TOK])
        kv_sq = sb("kv_sq", [P, T3, 4 * C])
        kv_ss, kv_log, kv_std, kv_eased, kv_inv = (sb(x, [P, T3 * C]) for x in ("kv_ss", "kv_log", "kv_std", "kv_eased", "kv_inv"))
        kv_n, kv_w, kv_f = (sb(x, [P, T3, 4 * C]) for x in ("kv_n", "kv_w", "kv_f"))
        kv_m = sb("kv_m", [P, P])
        mixed = sb("mixed", [P, 2, TOK])
        q_sb, ret, gel = sb("q_sb", [P, TOK]), sb("ret", [P, TOK]), sb("gel", [P, TOK])
        rows = sb("rows", [P, 4, 2, R, ROW], U32)
        logits = sb("logits", [P, 2, R, E_N])
        eq, cand, lower = (sb(x, [P, R, E_N]) for x in ("eq", "cand", "lower"))
        eq2, cand2 = sb("eq2", [P, R, E_N]), sb("cand2", [P, R, E_N])
        top1, top2, no1, no2 = (sb(x, [P, R]) for x in ("top1", "top2", "no1", "no2"))
        hot = sb("hot", [P, 2, 2, R, E_N])
        hot16 = sb("hot16", [P, 2, R, E_N], FP16)
        gap = sb("gap", [P, 2, R])
        gap_exp, one_more = sb("gap_exp", [P, R]), sb("one_more", [P, R])
        gate = sb("gate_v", [P, 2, R])
        seat, seat_hot = sb("seat", [P, R, E_N]), sb("seat_hot", [P, 2, R, E_N])
        place = sb("place", [P, 2, R])
        place_i = sb("place_i", [P, 4, 2, R], U32)
        place_no = sb("place_no", [P, 2, 2, R])
        pad = sb("pad", [P, ROW], U32)
        J = PER_GROUP
        count, tiles0, tiles = sb("count", [P, E_N]), sb("tiles0", [P, E_N]), sb("tiles", [P, E_N])
        cum = [sb(f"cum{k}", [P, E_N]) for k in range(5)]
        past, past_tiles = sb("past", [P, J, E_N]), sb("past_tiles", [P, J, E_N])
        first, which, clipped, tile_at, tile_in = (sb(x, [P, J]) for x in ("first", "which", "clipped", "tile_at", "tile_in"))
        expert, ids_wide, at_wide, words = sb("expert", [P, J]), sb("ids_wide", [P, J]), sb("at_wide", [P, J]), sb("words", [P, 3])
        plan = sb("plan_cols", [P, 3], I32)
        ends = sb("ends", [1, E_N], I32)
        names = ("a_cent a_sq a_var a_log a_rstd a_xn a_added b_kv b_sq b_ss b_log b_std b_eased b_inv b_n b_w b_f "
                 "c_q c_qb c_kv c_kvm c_out c_ret c_proj c_gelu c_added d_cent d_sq d_var d_log d_rstd d_xn d_logits d_xt d_ht "
                 "d_hi d_lo d_hcopy d_biased e_top1 e_eq e_cand e_no1 e_hot1 e_lower e_top2 e_eq2 e_cand2 e_no2 e_hot2 e_hot16 e_gap "
                 "f_rank f_exp f_more f_gate1 f_gate2 f_seat f_seathot f_place f_placei f_meta f_base f_start f_meta_no f_go "
                 "pad_zero pad_done planned plan_out plan_in")
        s = {name: n.sem("m_" + name) for name in names.split()}
        sent = [n.sem(f"m_sent{k}") for k in range(4)]
        pads_sent = [n.sem(f"pads_sent{k}") for k in range(2)]
        W = lambda name, rows=P: n.w[0:rows, W_AT[name][0]:W_AT[name][1]]
        K = lambda name: n.f[:, F32_AT[name][0]:F32_AT[name][1]]
        H16 = lambda name: n.h[:, F16_AT[name][0]:F16_AT[name][1]]
        STEPS = PAIRS + 5

        def uses_before(d, u):
            return d // 4 if isinstance(d, int) else (d - u % 4) // 4

        def run(engine, body):
            def static(j):
                body(j, j % 4, [0 <= j - k < PAIRS for k in range(6)])

            for j in range(8):
                static(j)
            with engine.Fori(2, PAIRS // 4) as i:
                for u in range(4):
                    body(4 * i + u, u, [True] * 6)
            for j in range(PAIRS, STEPS):
                static(j)

        def pad_lists(engine, lists):
            engine.wait_ge(s["pad_done"], 1)
            for e in lists:
                end = engine.value_load(ends[0:1, e:e + 1], min_val=0, max_val=E_N * LIST)
                engine.dma_start(n.lists[bass.ds(end, P), :], pad[:, :]).then_inc(pads_sent[e // (E_N // 2)], 16)

        with nc.Block() as block:
            @block.tensor
            def _(pe):
                mm = nc.tensor.matmul

                def body(j, u, on):
                    a, b, c, d, e, f = (j - k for k in range(6))
                    if on[2]:
                        wait(pe, s["c_ret"], c)
                        mm(p_q[:, 0:TOK], W("mq"), xn[:, (u - 2) % 4, :], start=True, stop=True).then_inc(s["c_q"], 1)
                        pe.wait_ge(s["b_f"], c + 1)
                        wait(pe, s["c_gelu"], c)
                        for t in range(T3):
                            last = mm(p_kvkv[:, 0:P], kv_f[:, t, 0:P], kv_f[:, t, P:2 * P], start=(t == 0), stop=(t == T3 - 1))
                        last.then_inc(s["c_kv"], 1)
                    if on[0]:
                        wait(pe, s["a_xn"], a)
                        mm(p_cent[:, 0:TOK], K("center"), n.tokens[:, a, :], start=True, stop=True).then_inc(s["a_cent"], 1)
                    if on[3]:
                        pe.wait_ge(s["c_added"], d + 1)
                        wait(pe, s["d_lo"], d)
                        mm(p_cent2[:, 0:TOK], K("center"), mixed[:, (u - 3) % 2, :], start=True, stop=True).then_inc(s["d_cent"], 1)
                    if on[0]:
                        pe.wait_ge(s["a_sq"], a + 1)
                        wait(pe, s["d_hcopy"], a - 3)
                        mm(p_var[:, 0:TOK], K("average"), sq1[:, :], start=True, stop=True).then_inc(s["a_var"], 1)
                    if on[5]:
                        pe.wait_ge(s["e_hot16"], f + 1)
                        pe.wait_ge(s["d_biased"], f + 2 if on[4] else PAIRS)
                        hots = hot16[:, (u - 5) % 2, :, :].rearrange("p r e -> p (r e)")
                        mm(p_var2[:, 0:R * E_N], H16("before16"), hots, start=True, stop=False, skip_group_check=True)
                        for k in range(1, R):
                            mm(p_var2[:, E_N * k:R * E_N], H16("ones16"), hots[:, 0:(R - k) * E_N], start=False, stop=(k == R - 1),
                               skip_group_check=True)
                        for k in range(R):
                            last = mm(p_var2[:, R * E_N:(R + 1) * E_N], H16("ones16"), hots[:, E_N * k:E_N * k + E_N], start=False,
                                      stop=(k == R - 1), skip_group_check=True)
                        last.then_inc(s["f_rank"], 1)
                    if on[2]:
                        pe.wait_ge(s["c_qb"], c + 1)
                        pe.wait_ge(s["c_kvm"], c + 1)
                        mm(p_q[:, 0:TOK], kv_m[:, :], q_sb[:, :], start=True, stop=True).then_inc(s["c_out"], 1)
                    if on[3]:
                        pe.wait_ge(s["d_sq"], d + 1)
                        wait(pe, s["d_biased"], d)
                        if on[5]:
                            pe.wait_ge(s["f_base"], f + 1)
                            pe.wait_ge(s["f_seat"], f + 1)
                        mm(p_var2[:, 0:TOK], K("average"), sq2[:, :], start=True, stop=True).then_inc(s["d_var"], 1)
                    if on[2]:
                        pe.wait_ge(s["c_ret"], c + 1)
                        mm(p_kvkv[:, 0:TOK], W("mproj"), ret[:, :], start=True, stop=True).then_inc(s["c_proj"], 1)
                    if on[3]:
                        wait(pe, s["a_log"], a + 1 if on[0] else PAIRS)
                        for t in range(T3):
                            last = nc.tensor.transpose(p_var[:, P * t:P * t + P], mixed[:, (u - 3) % 2, t:TOK:T3], K("ident"))
                        last.then_inc(s["d_ht"], 1)
                        pe.wait_ge(s["d_xn"], d + 1)
                        for t in range(T3):
                            last = mm(p_var2[:, 32 * t:32 * t + 32], xn2[:, t:TOK:T3], W("gate"), start=True, stop=True)
                        last.then_inc(s["d_logits"], 1)
                        for t in range(T3):
                            last = nc.tensor.transpose(p_cent2[:, P * t:P * t + P], xn2[:, t:TOK:T3], K("ident"))
                        last.then_inc(s["d_xt"], 1)
                    if on[0]:
                        pe.wait_ge(s["a_xn"], a + 1)
                        wait(pe, s["b_n"], a)
                        for t in range(T3):
                            out = (p_kv0 if t < 2 else p_kv1)[:, 256 * (t % 2):256 * (t % 2) + 256]
                            mm(out, xn[:, u, P * t:P * t + P], n.mkv[:, :, :, :].rearrange("p a b c -> p (a b c)"),
                               start=True, stop=False)
                            last = mm(out, K("row_of_ones"), n.mkv_b[:, :, :, :].rearrange("p a b c -> p (a b c)"),
                                      start=False, stop=True)
                        last.then_inc(s["b_kv"], 1)

                run(pe, body)

            @block.sync
            def _(sp):
                sp.wait_ge(s["planned"], 1)
                pad_lists(sp, range(E_N // 2))
                sp.dma_start(n.lists[E_N * LIST:E_N * LIST + P, :], pad[:, :]).then_inc(pads_sent[0], 16)
                sp.wait_ge(s["planned"], PLAN_OPS)
                for k in range(3):
                    sp.dma_start(n.plan[k].rearrange("(p o) -> p o", o=1), plan[:, k:k + 1]).then_inc(s["plan_out"], 16)
                sp.wait_ge(s["plan_out"], 16 * 3)
                sp.dma_start(n.plan_row[:, :, :], n.plan.rearrange("(o k) t -> o k t", o=1)).then_inc(s["plan_in"], 16)
                sp.wait_ge(pads_sent[0], 16 * (E_N // 2 + 1))
                sp.wait_ge(s["plan_in"], 16)

            @block.scalar
            def _(act):
                A = nc.scalar.activation
                nc.scalar.preload_act_table_set("natural_log_exp_and_others")

                def body(j, u, on):
                    a, b, c, d, e, f = (j - k for k in range(6))
                    nc.scalar.preload_act_table_set("natural_log_exp_and_others")
                    if on[1]:
                        act.wait_ge(s["b_kv"], b + 1)
                        wait(act, s["b_ss"], b)
                        A(kv_sq[:, 0:2, :], p_kv0[:, :].rearrange("p (t c) -> p t c", t=2), ACT.Square)
                        A(kv_sq[:, 2, :], p_kv1[:, 0:4 * C], ACT.Square).then_inc(s["b_sq"], 1)
                    if on[2]:
                        act.wait_ge(s["c_q"], c + 1)
                        wait(act, s["c_out"], c)
                        A(q_sb[:, :], p_q[:, 0:TOK], ACT.Identity, bias=W("mq_b")).then_inc(s["c_qb"], 1)
                    if on[0]:
                        act.wait_ge(s["a_cent"], a + 1)
                        wait(act, s["a_var"], a)
                        A(sq1[:, :], p_cent[:, 0:TOK], ACT.Square).then_inc(s["a_sq"], 1)
                    if on[3]:
                        act.wait_ge(s["d_cent"], d + 1)
                        wait(act, s["d_var"], d)
                        A(sq2[:, :], p_cent2[:, 0:TOK], ACT.Square).then_inc(s["d_sq"], 1)
                    if on[5]:
                        act.wait_ge(s["e_gap"], f + 1)
                        wait(act, s["f_gate2"], f)
                        A(gap_exp[:, :], gap[:, (u - 5) % 2, :], ACT.Exp).then_inc(s["f_exp"], 1)
                    if on[0]:
                        act.wait_ge(s["a_var"], a + 1)
                        wait(act, s["a_rstd"], a)
                        A(log1[:, :], p_var[:, 0:TOK], ACT.Ln, bias=K("eps")).then_inc(s["a_log"], 1)
                    if on[1]:
                        act.wait_ge(s["b_ss"], b + 1)
                        wait(act, s["b_std"], b)
                        A(kv_log[:, :], kv_ss[:, :], ACT.Ln, bias=K("tiny"), scale=1.0 / 3.0).then_inc(s["b_log"], 1)
                    if on[0]:
                        act.wait_ge(s["a_log"], a + 1)
                        wait(act, s["a_xn"], a)
                        A(rstd1[:, :], log1[:, :], ACT.Exp, scale=-0.5).then_inc(s["a_rstd"], 1)
                    if on[1]:
                        act.wait_ge(s["b_log"], b + 1)
                        wait(act, s["b_eased"], b)
                        A(kv_std[:, :], kv_log[:, :], ACT.Exp, scale=0.5).then_inc(s["b_std"], 1)
                    if on[3]:
                        act.wait_ge(s["d_var"], d + 1)
                        wait(act, s["d_rstd"], d)
                        A(log2[:, :], p_var2[:, 0:TOK], ACT.Ln, bias=K("eps")).then_inc(s["d_log"], 1)
                    if on[1]:
                        act.wait_ge(s["b_std"], b + 1)
                        A(kv_eased[:, :], kv_std[:, :], ACT.Ln, bias=K("eps")).then_inc(s["b_eased"], 1)
                    if on[3]:
                        act.wait_ge(s["d_log"], d + 1)
                        wait(act, s["d_xn"], d)
                        A(rstd2[:, :], log2[:, :], ACT.Exp, scale=-0.5).then_inc(s["d_rstd"], 1)
                    if on[1]:
                        act.wait_ge(s["b_eased"], b + 1)
                        wait(act, s["b_n"], b)
                        A(kv_inv[:, :], kv_eased[:, :], ACT.Exp, scale=-1.0).then_inc(s["b_inv"], 1)
                    if on[2]:
                        act.wait_ge(s["c_proj"], c + 1)
                        wait(act, s["c_added"], c)
                        A(gel[:, :], p_kvkv[:, 0:TOK], ACT.Gelu, bias=W("mproj_b")).then_inc(s["c_gelu"], 1)
                    if on[3]:
                        act.wait_ge(s["d_ht"], d + 1)
                        A(n.tokens_t[:, bass.ds(d * R, R), :].rearrange("p (s t) c -> p t s c", s=2),
                          p_var[:, 0:TOK].rearrange("p (t s c) -> p t s c", t=T3, s=2), ACT.Copy).then_inc(s["d_hcopy"], 1)
                        act.wait_ge(s["d_xt"], d + 1)
                        slot = (u - 3) % 4
                        wait(act, sent[slot], 16 * 2 * R * uses_before(d, u - 3))
                        x3 = p_cent2[:, 0:TOK].rearrange("p (ts c) -> p ts c", c=C)
                        for k in range(2):
                            last = A(rows[:, slot, k, :, 0:C // 2].bitcast(FP16), x3, ACT.Copy, scale=X_SCALE)
                        last.then_inc(s["d_hi"], 1)

                run(act, body)
                act.wait_ge(s["planned"], 1)
                pad_lists(act, range(E_N // 2, E_N))
                act.wait_ge(pads_sent[1], 16 * (E_N // 2))

            @block.vector
            def _(dve):
                V = nc.vector
                V.tensor_copy(n.list_end[:, 1, :], K("list_base"))
                V.tensor_copy(place_no[:, 1, :, :], K("row_no").rearrange("p (k r) -> p k r", k=2)).then_inc(s["f_start"], 1)
                dve.wait_ge(s["f_start"], 1)
                wide = lambda t: t.unsqueeze(2).broadcast_to([P, R, E_N])
                rank = K("rank_e").unsqueeze(1).broadcast_to([P, R, E_N])

                def best_two(e, v):
                    def then(name, op):
                        op.then_inc(s[name], 1)
                        dve.wait_ge(s[name], e + 1)

                    then("e_top1", V.tensor_reduce(top1[:, :], logits[:, v, :, :], X, ALU.max))
                    then("e_eq", V.tensor_tensor(eq[:, :, :], logits[:, v, :, :], wide(top1[:, :]), ALU.is_equal))
                    then("e_cand", V.tensor_tensor(cand[:, :, :], eq[:, :, :], rank, ALU.mult))
                    then("e_no1", V.tensor_reduce(no1[:, :], cand[:, :, :], X, ALU.max))
                    wait(dve, s["f_seathot"], e - 1)
                    then("e_hot1", V.tensor_tensor(hot[:, v, 0, :, :], rank, wide(no1[:, :]), ALU.is_equal))
                    then("e_lower", V.scalar_tensor_tensor(lower[:, :, :], hot[:, v, 0, :, :], -1e30, logits[:, v, :, :], ALU.mult, ALU.add))
                    then("e_top2", V.tensor_reduce(top2[:, :], lower[:, :, :], X, ALU.max))
                    then("e_eq2", V.tensor_tensor(eq2[:, :, :], lower[:, :, :], wide(top2[:, :]), ALU.is_equal))
                    then("e_cand2", V.tensor_tensor(cand2[:, :, :], eq2[:, :, :], rank, ALU.mult))
                    then("e_no2", V.tensor_reduce(no2[:, :], cand2[:, :, :], X, ALU.max))
                    wait(dve, s["f_exp"], e - 1)
                    V.tensor_tensor(gap[:, v, :], top2[:, :], top1[:, :], ALU.subtract).then_inc(s["e_gap"], 1)
                    then("e_hot2", V.tensor_tensor(hot[:, v, 1, :, :], rank, wide(no2[:, :]), ALU.is_equal))
                    wait(dve, s["f_rank"], e - 1)
                    V.tensor_tensor(hot16[:, v, :, :], hot[:, v, 0, :, :], hot[:, v, 1, :, :], ALU.add).then_inc(s["e_hot16"], 1)

                def body(j, u, on):
                    a, b, c, d, e, f = (j - k for k in range(6))
                    ve, vf, wf = (u - 4) % 2, (u - 5) % 2, (u - 4) % 2
                    if on[2]:
                        dve.wait_ge(s["c_kv"], c + 1)
                        wait(dve, s["c_out"], c)
                        V.tensor_tensor(kv_m[:, :], p_kvkv[:, 0:P], K("mask4"), ALU.mult).then_inc(s["c_kvm"], 1)
                    if on[1]:
                        dve.wait_ge(s["b_sq"], b + 1)
                        wait(dve, s["b_log"], b)
                        V.tensor_reduce(kv_ss[:, :], kv_sq[:, :, :].rearrange("p t (g k) -> p (t g) k", k=4), X, ALU.add).then_inc(s["b_ss"], 1)
                    if on[5]:
                        dve.wait_ge(s["f_rank"], f + 1)
                        wait(dve, s["f_seathot"], f)
                        wait(dve, s["f_base"], f)
                        V.tensor_tensor(seat[:, :, :], p_var2[:, 0:R * E_N].rearrange("p (r e) -> p r e", r=R),
                                        n.list_end[:, wf, :].unsqueeze(1).broadcast_to([P, R, E_N]), ALU.add).then_inc(s["f_seat"], 1)
                        V.tensor_tensor(n.list_end[:, vf, :], p_var2[:, R * E_N:(R + 1) * E_N], n.list_end[:, wf, :], ALU.add).then_inc(s["f_base"], 1)
                        dve.wait_ge(s["f_seat"], f + 1)
                        wait(dve, s["f_place"], f)
                        for k in range(2):
                            last = V.tensor_tensor(seat_hot[:, k, :, :], seat[:, :, :], hot[:, vf, k, :, :], ALU.mult)
                        last.then_inc(s["f_seathot"], 1)
                        dve.wait_ge(s["f_exp"], f + 1)
                        wait(dve, s["f_gate1"], f)
                        V.tensor_scalar(one_more[:, :], gap_exp[:, :], 1.0, None, ALU.add).then_inc(s["f_more"], 1)
                        dve.wait_ge(s["f_seathot"], f + 1)
                        wait(dve, s["f_placei"], f)
                        V.tensor_reduce(place[:, :, :], seat_hot[:, :, :, :], X, ALU.add).then_inc(s["f_place"], 1)
                        dve.wait_ge(s["f_more"], f + 1)
                        wait(dve, s["f_meta"], f)
                        V.reciprocal(gate[:, 0, :], one_more[:, :]).then_inc(s["f_gate1"], 1)
                        dve.wait_ge(s["f_place"], f + 1)
                        V.tensor_copy(place_i[:, (u - 5) % 4, :, :], place[:, :, :]).then_inc(s["f_placei"], 1)
                        dve.wait_ge(s["f_gate1"], f + 1)
                        V.tensor_tensor(gate[:, 1, :], gate[:, 0, :], gap_exp[:, :], ALU.mult).then_inc(s["f_gate2"], 1)
                        wait(dve, s["f_meta_no"], f)
                        V.tensor_copy(rows[:, (u - 5) % 4, :, :, C:C + 1].rearrange("p k r o -> p k (r o)"), place_no[:, wf, :, :])
                        dve.wait_ge(s["f_gate2"], f + 1)
                        V.tensor_scalar(rows[:, (u - 5) % 4, :, :, C + 1:C + 2].rearrange("p k r o -> p k (r o)").bitcast(FP32), gate[:, :, :],
                                        1.0 / (X_SCALE * W_SCALE), None, ALU.mult).then_inc(s["f_meta"], 1)
                        V.tensor_scalar(place_no[:, vf, :, :], place_no[:, wf, :, :], float(2 * TOK), None, ALU.add).then_inc(s["f_meta_no"], 1)
                    if on[2]:
                        dve.wait_ge(s["c_out"], c + 1)
                        wait(dve, s["c_proj"], c)
                        V.tensor_tensor(ret[:, :], p_q[:, 0:TOK], xn[:, (u - 2) % 4, :], ALU.add).then_inc(s["c_ret"], 1)
                    if on[0]:
                        dve.wait_ge(s["a_rstd"], a + 1)
                        wait(dve, s["c_ret"], a - 3)
                        wait(dve, s["a_added"], a - 3)
                        V.tensor_tensor(xn[:, u, :], p_cent[:, 0:TOK], rstd1[:, :], ALU.mult).then_inc(s["a_xn"], 1)
                    if on[3]:
                        dve.wait_ge(s["d_rstd"], d + 1)
                        wait(dve, s["d_xt"], d)
                        V.tensor_tensor(xn2[:, :], p_cent2[:, 0:TOK], rstd2[:, :], ALU.mult).then_inc(s["d_xn"], 1)
                    if on[1]:
                        dve.wait_ge(s["b_inv"], b + 1)
                        wait(dve, s["b_w"], b)
                        half = P // 2
                        four = lambda t: t.rearrange("p (g k) -> p g k", k=4)
                        V.tensor_tensor(four(kv_n[:, 0:2, :].rearrange("p t c -> p (t c)")), four(p_kv0[:, :]),
                                        kv_inv[:, 0:P].unsqueeze(2).broadcast_to([P, P, 4]), ALU.mult)
                        V.tensor_tensor(four(kv_n[:, 2, :]), four(p_kv1[:, 0:4 * C]),
                                        kv_inv[:, P:P + half].unsqueeze(2).broadcast_to([P, half, 4]), ALU.mult).then_inc(s["b_n"], 1)
                    if on[0]:
                        dve.wait_ge(s["a_xn"], a + 1)
                        V.tensor_tensor(n.tokens[:, a, :], n.tokens[:, a, :], xn[:, u, :], ALU.add).then_inc(s["a_added"], 1)
                    if on[1]:
                        dve.wait_ge(s["b_n"], b + 1)
                        wait(dve, s["b_f"], b)
                        V.tensor_tensor(kv_w[:, :, :], kv_n[:, :, :], W("kv_ln_w").unsqueeze(1).broadcast_to([P, T3, 4 * C]), ALU.mult).then_inc(s["b_w"], 1)
                        dve.wait_ge(s["b_w"], b + 1)
                        wait(dve, s["c_kv"], b)
                        V.tensor_tensor(kv_f[:, :, :], kv_w[:, :, :], W("kv_ln_b").unsqueeze(1).broadcast_to([P, T3, 4 * C]), ALU.add).then_inc(s["b_f"], 1)
                    if on[2]:
                        dve.wait_ge(s["c_gelu"], c + 1)
                        dve.wait_ge(s["a_added"], c + 1)
                        wait(dve, s["d_ht"], c - 1)
                        V.tensor_tensor(mixed[:, u % 2, :], n.tokens[:, c, :], gel[:, :], ALU.add).then_inc(s["c_added"], 1)
                    if on[3]:
                        dve.wait_ge(s["d_logits"], d + 1)
                        wait(dve, s["e_lower"], d - 1)
                        V.tensor_tensor(logits[:, (u - 3) % 2, :, :].rearrange("p r e -> p (r e)").rearrange("p (t x) -> p t x", t=T3),
                                        p_var2[:, 0:R * E_N].rearrange("p (t x) -> p t x", t=T3),
                                        W("gate_b").unsqueeze(1).broadcast_to([P, T3, 2 * E_N]), ALU.add).then_inc(s["d_biased"], 1)
                    if on[3]:
                        dve.wait_ge(s["d_hi"], d + 1)
                        slot = (u - 3) % 4
                        for k in range(2):
                            last = V.scalar_tensor_tensor(rows[:, slot, k, :, C // 2:C].bitcast(FP16), p_cent2[:, 0:TOK].rearrange("p (ts c) -> p ts c", c=C),
                                                          X_SCALE, rows[:, slot, k, :, 0:C // 2].bitcast(FP16), ALU.mult, ALU.subtract)
                        last.then_inc(s["d_lo"], 1)
                    if on[4]:
                        best_two(e, ve)

                run(dve, body)

                dve.wait_ge(s["f_base"], PAIRS)
                step = [0]

                def then(op):
                    step[0] += 1
                    op.then_inc(s["planned"], 1)
                    dve.wait_ge(s["planned"], step[0])

                dve.wait_ge(s["pad_zero"], 1)
                V.tensor_copy(pad[:, C:C + 1], K("pad_place")).then_inc(s["pad_done"], 1)
                then(V.tensor_copy(ends[:, :], n.list_end[0:1, 1, :]))
                then(V.tensor_tensor(count[:, :], n.list_end[:, 1, :], K("list_base"), ALU.subtract))
                then(V.tensor_scalar(tiles0[:, :], count[:, :], 1.0 / P, float(P - 1) / P - 255.0 / 512.0, ALU.mult, ALU.add))
                then(V.tensor_scalar(tiles[:, :], tiles0[:, :], MAGIC, -MAGIC, ALU.add, ALU.add))
                then(V.tensor_copy(cum[0][:, :], tiles[:, :]))
                for k in range(4):
                    d = 1 << k
                    V.tensor_copy(cum[k + 1][:, 0:d], cum[k][:, 0:d])
                    then(V.tensor_tensor(cum[k + 1][:, d:E_N], cum[k][:, d:E_N], cum[k][:, 0:E_N - d], ALU.add))
                then(V.tensor_tensor(past[:, :, :], K("tile_no").unsqueeze(2).broadcast_to([P, J, E_N]),
                                     cum[4][:, :].unsqueeze(1).broadcast_to([P, J, E_N]), ALU.is_ge))
                then(V.tensor_tensor(past_tiles[:, :, :], past[:, :, :], tiles[:, :].unsqueeze(1).broadcast_to([P, J, E_N]), ALU.mult))
                then(V.tensor_reduce(which[:, :], past[:, :, :], X, ALU.add))
                then(V.tensor_reduce(first[:, :], past_tiles[:, :, :], X, ALU.add))
                then(V.tensor_tensor(tile_in[:, :], K("tile_no"), first[:, :], ALU.subtract))
                then(V.scalar_tensor_tensor(tile_at[:, :], which[:, :], float(LIST_T), tile_in[:, :], ALU.mult, ALU.add))
                then(V.tensor_scalar(clipped[:, :], tile_at[:, :], float(E_N * LIST_T), None, ALU.min))
                then(V.tensor_scalar(expert[:, :], which[:, :], float(E_N - 1), None, ALU.min))
                then(V.tensor_tensor(ids_wide[:, :], expert[:, :], K("id_unit"), ALU.mult))
                then(V.tensor_tensor(at_wide[:, :], clipped[:, :], K("at_unit"), ALU.mult))
                then(V.tensor_reduce(words[:, 0:1], ids_wide[:, :], X, ALU.add))
                then(V.tensor_reduce(words[:, 1:3], at_wide[:, :].rearrange("p (a b) -> p a b", b=2), X, ALU.add))
                then(V.tensor_copy(plan[:, :], words[:, :]))

            @block.gpsimd
            def _(pool):
                G = nc.gpsimd
                G.memset(pad[:, :], 0).then_inc(s["pad_zero"], 1)

                def body(j, u, on):
                    f, slot = j - 5, (u - 5) % 4
                    if on[5]:
                        pool.wait_ge(s["f_meta"], f + 1)
                        pool.wait_ge(s["f_placei"], f + 1)
                        pool.wait_ge(s["d_lo"], f + 1)
                        pool.sem_inc(s["f_go"], 1)
                        for k in range(2):
                            for tile in range(R):
                                G.indirect_dma_start(out=n.lists, out_offset=bass.IndirectOffsetOnAxis(ap=place_i[:, slot, k, tile:tile + 1], axis=0),
                                                     in_=rows[:, slot, k, tile, :], in_offset=None).then_inc(sent[slot], 16)

                run(pool, body)
                for k in range(4):
                    pool.wait_ge(sent[k], 16 * 2 * R * (PAIRS // 4))


def experts(nc, n):
    with ExitStack() as ctx:
        def sb(name, shape, dt=FP32):
            return ctx.enter_context(nc.sbuf_tensor(name, shape, dt))

        J = PER_GROUP
        GROUPS_E = -(-RUN_T // J)
        SLOTS = 8
        rows = sb("x_rows", [P, SLOTS, J, ROW], U32)
        xt = sb("xt", [P, 2, J * P], FP16)
        act1 = sb("act1", [P, 2, J * P])
        hid = sb("hid", [P, 2, J * P])
        y = sb("y", [P, SLOTS, J, C])
        p_xt = [ctx.enter_context(nc.psum_tensor(f"p_xt{k}", [P, J * P], FP16)) for k in range(2)]
        p_h1 = [ctx.enter_context(nc.psum_tensor(f"p_h1_{k}", [P, J * P], FP32)) for k in range(2)]
        p_h2 = [ctx.enter_context(nc.psum_tensor(f"p_h2_{k}", [P, J * P], FP32)) for k in range(2)]
        p_y = [ctx.enter_context(nc.psum_tensor(f"p_y{k}", [P, J * C], FP32)) for k in range(2)]
        names = ("x_turned x_copied h1_ready h2_ready silu_done hid_done y_ready y_done y_go")
        s = {name: n.sem("x_" + name) for name in names.split()}
        rows_in = [n.sem(f"x_rows_in{k}") for k in range(SLOTS)]
        y_sent = [n.sem(f"x_y_sent{k}") for k in range(SLOTS)]

        with nc.Block() as block:
            def run(engine, body):
                for g in range(-1, SLOTS):
                    body(g, g % SLOTS, g // SLOTS, True, g >= 0, g >= 1)
                with engine.Fori(1, (GROUPS_E - 1) // SLOTS) as i:
                    for u in range(SLOTS):
                        body(SLOTS * i + u, u, i, True, True, True)
                for g in range((GROUPS_E - 1) // SLOTS * SLOTS, GROUPS_E + 1):
                    body(g, g % SLOTS, g // SLOTS, g < GROUPS_E - 1, g < GROUPS_E, True)

            @block.sync
            def _(sp):
                def load(g, u, i):
                    wait(sp, y_sent[u], 16 * J * i)
                    for k in range(2):
                        two = sp.value_load(n.plan_row[0:1, 1 + k, bass.ds(g, 1)], min_val=0, max_val=E_N * LIST_T * (AT_UNIT + 1))
                        for j, at in enumerate((two % AT_UNIT, two // AT_UNIT)):
                            sp.dma_start(rows[:, u, 2 * k + j, :], n.lists[bass.ds(at * P, P), :]).then_inc(rows_in[u], 16)

                for g in range(SLOTS):
                    load(g, g, 0)
                with sp.Fori(1, GROUPS_E // SLOTS) as i:
                    for u in range(SLOTS):
                        load(SLOTS * i + u, u, i)
                for g in range(GROUPS_E // SLOTS * SLOTS, GROUPS_E):
                    load(g, g % SLOTS, g // SLOTS)

            @block.tensor
            def _(pe):
                mm = nc.tensor.matmul

                def experts_of(g):
                    four = pe.value_load(n.plan_row[0:1, 0, bass.ds(g, 1)], min_val=0, max_val=E_N ** 4 - 1)
                    return [(four // E_N ** j) % E_N for j in range(J)]

                loaded = {}

                def body(g, u, i, nxt, cur, prev):
                    v = u % 2
                    if nxt:
                        un, i_n = (u + 1) % SLOTS, i + 1 if u == SLOTS - 1 else i
                        pe.wait_ge(rows_in[un], 16 * J * (i_n + 1))
                        wait(pe, s["x_copied"], g)
                        for j in range(J):
                            last = nc.tensor.transpose(p_xt[1 - v][:, P * j:P * j + P], rows[:, un, j, 0:C].bitcast(FP16),
                                                       n.h[:, F16_AT["ident16"][0]:F16_AT["ident16"][1]])
                        last.then_inc(s["x_turned"], 1)
                    if cur:
                        pe.wait_ge(s["x_copied"], g + 1)
                        wait(pe, s["silu_done"], g - 1)
                        chosen = loaded[u] = experts_of(g)
                        for j, e in enumerate(chosen):
                            for part in range(2):
                                last = mm(p_h1[v][:, P * j:P * j + P], n.w12[:, bass.ds(e, 1), 0, part, :].rearrange("p o h -> p (o h)"),
                                          xt[:, v, P * j:P * j + P], start=(part == 0), stop=(part == 1))
                        last.then_inc(s["h1_ready"], 1)
                        wait(pe, s["hid_done"], g - 1)
                        for j, e in enumerate(chosen):
                            for part in range(2):
                                last = mm(p_h2[v][:, P * j:P * j + P], n.w12[:, bass.ds(e, 1), 1, part, :].rearrange("p o h -> p (o h)"),
                                          xt[:, v, P * j:P * j + P], start=(part == 0), stop=(part == 1))
                        last.then_inc(s["h2_ready"], 1)
                    if prev:
                        pe.wait_ge(s["hid_done"], g)
                        wait(pe, s["y_done"], g - 2)
                        for j, e in enumerate(loaded[u - 1] if u else experts_of(g - 1)):
                            last = mm(p_y[1 - v][:, C * j:C * j + C], hid[:, 1 - v, P * j:P * j + P], n.w[:, bass.ds(e * C + W_AT["w3"][0], C)],
                                      start=True, stop=True)
                        last.then_inc(s["y_ready"], 1)

                run(pe, body)

            @block.scalar
            def _(act):
                A = nc.scalar.activation

                def body(g, u, i, nxt, cur, prev):
                    if cur:
                        act.wait_ge(s["h1_ready"], g + 1)
                        wait(act, s["hid_done"], g - 1)
                        A(act1[:, u % 2, :], p_h1[u % 2][:, :], ACT.Silu, scale=1.0 / (X_SCALE * W_SCALE)).then_inc(s["silu_done"], 1)

                run(act, body)

            @block.vector
            def _(dve):
                V = nc.vector

                def body(g, u, i, nxt, cur, prev):
                    v = u % 2
                    if nxt:
                        dve.wait_ge(s["x_turned"], g + 2)
                        wait(dve, s["h2_ready"], g)
                        V.tensor_copy(xt[:, 1 - v, :], p_xt[1 - v][:, :]).then_inc(s["x_copied"], 1)
                    if prev:
                        up = (u - 1) % SLOTS
                        dve.wait_ge(s["y_ready"], g)
                        V.tensor_tensor(y[:, up, :, :], p_y[1 - v][:, :].rearrange("p (j c) -> p j c", j=J),
                                        rows[:, up, :, C + 1:C + 2].bitcast(FP32).broadcast_to([P, J, C]), ALU.mult).then_inc(s["y_done"], 1)
                    if cur:
                        dve.wait_ge(s["silu_done"], g + 1)
                        dve.wait_ge(s["h2_ready"], g + 1)
                        wait(dve, s["y_ready"], g - 1)
                        V.tensor_tensor(hid[:, v, :], p_h2[v][:, :], act1[:, v, :], ALU.mult).then_inc(s["hid_done"], 1)

                run(dve, body)

            @block.gpsimd
            def _(pool):
                def body(g, u, i, nxt, cur, prev):
                    if prev:
                        up = (u - 1) % SLOTS
                        pool.wait_ge(s["y_done"], g)
                        pool.sem_inc(s["y_go"], 1)
                        for j in range(J):
                            nc.gpsimd.indirect_dma_start(out=n.expert_rows, out_offset=bass.IndirectOffsetOnAxis(ap=rows[:, up, j, C:C + 1], axis=0),
                                                         in_=y[:, up, j, :], in_offset=None, bounds_check=2 * B * TOK - 1,
                                                         oob_is_err=False).then_inc(y_sent[up], 16)

                run(pool, body)
                for u in range(SLOTS):
                    pool.wait_ge(y_sent[u], 16 * J * ((GROUPS_E - u + SLOTS - 1) // SLOTS))




def combine(nc, n):
    with ExitStack() as ctx:
        T3 = TOK // P
        Q = 8
        J = Q * T3
        N = TILES_TOK // J
        a = ctx.enter_context(nc.sbuf_tensor("from_experts", [P, 2, 2, J, C], FP32))
        t = ctx.enter_context(nc.sbuf_tensor("one_added", [P, 2, J, C], FP32))
        o = ctx.enter_context(nc.sbuf_tensor("both_added", [P, 2, J, C], FP32))
        rows_in = [n.sem(f"z_rows_in{k}") for k in range(2)]
        out_done = [n.sem(f"z_out_done{k}") for k in range(2)]
        added1, added2 = n.sem("z_added1"), n.sem("z_added2")
        src = n.expert_rows.rearrange("(k m q p t) c -> m k p q (t c)", k=2, m=N, q=Q, t=T3)
        dst = n.out.rearrange("(m q) (p t) c -> m p q (t c)", m=N, t=T3)
        by_sample = lambda x: x.rearrange("p (q t) c -> p q (t c)", q=Q)
        with nc.Block() as block:
            @block.sync
            def _(sp):
                for m in range(N):
                    wait(sp, added2, m - 1)
                    for k in range(2):
                        sp.dma_start(by_sample(a[:, m % 2, k, :, :]), src[m, k]).then_inc(rows_in[m % 2], 16)

            @block.vector
            def _(dve):
                for m in range(N):
                    v = m % 2
                    dve.wait_ge(rows_in[v], 32 * (m // 2 + 1))
                    nc.vector.tensor_tensor(t[:, v, :, :], a[:, v, 0, :, :], a[:, v, 1, :, :], ALU.add).then_inc(added1, 1)
                    dve.wait_ge(added1, m + 1)
                    wait(dve, out_done[v], 16 * (m // 2))
                    nc.vector.tensor_tensor(o[:, v, :, :], t[:, v, :, :], n.tokens_t[:, J * m:J * m + J, :], ALU.add).then_inc(added2, 1)

            @block.scalar
            def _(act):
                for m in range(N):
                    act.wait_ge(added2, m + 1)
                    act.dma_start(dst[m], by_sample(o[:, m % 2, :, :])).then_inc(out_done[m % 2], 16)
                for v in range(2):
                    act.wait_ge(out_done[v], 16 * (N // 2))



def build(nc, ins, out):
    n = Names()
    n.in_weights, n.in_f32, n.in_f16 = ins["weights"], ins["f32"], ins["f16"]
    n.in_w1, n.in_w2, n.in_x, n.in_ids, n.in_pos = ins["w1"], ins["w2"], ins["x"], ins["ids"], ins["pos"]
    with ExitStack() as ctx:
        def sb(name, shape, dt=FP32):
            return ctx.enter_context(nc.sbuf_tensor(name, shape, dt))

        n.sem = lambda name: ctx.enter_context(nc.semaphore(name))
        n.w = sb("w", [P, W_N])
        n.f = sb("f", [P, F32_N])
        n.h = sb("h16", [P, F16_N], FP16)
        n.wk, n.wv, n.wq = sb("wk", [P, P]), sb("wv", [P, P]), sb("wq", [P, P])
        n.bq, n.pb = sb("bq", [P, 1]), sb("pb_bias", [P, 1])
        n.mkv, n.mkv_b = sb("mkv", [P, 2, 2, C]), sb("mkv_b", [P, 2, 2, C])
        n.w12 = sb("w12", [P, E_N, 2, 2, HID], FP16)
        n.tokens = sb("tokens", [P, PAIRS, TOK])
        n.lists = nc.dram_tensor("lists", (LISTS * P, ROW), U32, kind="Internal").ap()
        n.expert_rows = nc.dram_tensor("expert_rows", (2 * B * TOK, C), FP32, kind="Internal").ap()
        n.plan = nc.dram_tensor("plan", (3, P), I32, kind="Internal").ap()
        n.out = out
        constants(nc, n)
        with nc.sbuf_tensor("xs", [P, 4, GROUP], FP32) as n.xs:
            n.x_in = [n.sem(f"x_in{k}") for k in range(4)]
            text(nc, n)
            windows(nc, n)
        n.tokens_t = sb("tokens_t", [P, TILES_TOK, C])
        n.list_end = sb("list_end", [P, 2, E_N])
        n.plan_row = sb("plan_row", [1, 3, P], I32)
        mixing(nc, n)
        experts(nc, n)
        combine(nc, n)


def inputs_of(g):
    f, h = shape_constants()
    return {"weights": pack_weights(g), "f32": f, "f16": h, "w1": g["L0_ffn_w1"], "w2": g["L0_ffn_w2"],
            "x": g["x"].reshape(B, C, PIX), "ids": g["x_txt"].reshape(1, B * TXT_T),
            "pos": g["fside_BS_continuous_positions"].reshape(1, B * TXT_T)}


def kernel(**inputs):
    from concourse import bacc
    from concourse.bass_utils import run_bass_kernel_spmd

    nc = bacc.Bacc("TRN2", target_bir_lowering=False, num_devices=1)
    arrays, ins = {}, {}
    for name, value in inputs_of({k: np.asarray(v) for k, v in inputs.items()}).items():
        arrays["in_" + name] = np.ascontiguousarray(value)
        ins[name] = nc.dram_tensor("in_" + name, value.shape, mybir.dt.from_np(value.dtype), kind="ExternalInput").ap()
    out = nc.dram_tensor("out_h", (B, TOK, C), FP32, kind="ExternalOutput").ap()
    build(nc, ins, out)
    result = run_bass_kernel_spmd(nc, [arrays], core_ids=[0])
    return result.results[0]["out_h"]
```
